# Optimizing a Trainium2 kernel written in Bass

```python
import numpy as np
import jax
import jax.numpy as jnp

def _softmax(x, axis=-1):
    return jax.nn.softmax(x, axis=axis)

def _gelu(x):
    return jax.nn.gelu(x, approximate=True)

def _silu(x):
    return jax.nn.silu(x)

def _sigmoid(x):
    return jax.nn.sigmoid(x)

def _layernorm(x, axis=-1, eps=1e-05):
    m = jnp.mean(x, axis=axis, keepdims=True)
    v = jnp.var(x, axis=axis, keepdims=True)
    return (x - m) / jnp.sqrt(v + eps)

def _scatter_add(tgt, idx, src, axis=0):
    return tgt.at[idx].add(src)

def _segment_sum(src, seg, n):
    return jax.ops.segment_sum(src, seg, n)
kernel_name = 'mk_gnn_preln_d2_gnn_r32_379704'

def setup_inputs(seed: int=0):
    np.random.seed(seed)
    _w = jnp.asarray

    def _rec_inputs():
        import jax
        import jax.numpy as jnp
        _gk = jax.random.key(seed)
        x = -0.0006008 + 1.001 * jax.random.normal(jax.random.fold_in(_gk, 1), (3125, 256), jnp.float32)
        _s = jax.random.randint(jax.random.fold_in(_gk, 2), (25000,), 0, 3125, jnp.int32)
        _d = jax.random.randint(jax.random.fold_in(_gk, 3), (25000,), 0, 3125, jnp.int32)
        _loop = jnp.arange(3125, dtype=jnp.int32)
        src = jnp.concatenate([_s, _d, _loop])
        dst = jnp.concatenate([_d, _s, _loop])
        _o = jnp.argsort(dst, stable=True)
        src = src[_o]
        dst = dst[_o]
        edge_type_2 = jax.random.randint(jax.random.fold_in(_gk, 12), (53125,), 0, 2, jnp.int32)
        edge_weight = jax.random.uniform(jax.random.fold_in(_gk, 13), (53125,), jnp.float32, 0.0, 1)
        return (x, src, dst, edge_type_2, edge_weight)
    x, src, dst, edge_type_2, edge_weight = _rec_inputs()

    def _L0_gnn_setup():
        import jax, jax.numpy as jnp
        import numpy as np
        N_NODES = 10000
        N_EDGES = 10000
        D = 256
        D_OUT = 256
        NUM_REL = 2
        key = jax.random.key(seed)
        ks = jax.random.split(key, 16)
        s = 1.0 / np.sqrt(D)
        inp = {}
        inp['feat'] = jax.random.normal(ks[0], (N_NODES, D), dtype=jnp.float32)
        inp['src'] = jax.random.randint(ks[1], (N_EDGES,), 0, N_NODES, dtype=jnp.int32)
        inp['dst'] = jax.random.randint(ks[2], (N_EDGES,), 0, N_NODES, dtype=jnp.int32)
        inp['rel'] = jax.random.randint(ks[3], (N_EDGES,), 0, NUM_REL, dtype=jnp.int32)
        inp['W_rel'] = jax.random.normal(ks[4], (NUM_REL, D, D), dtype=jnp.float32) * s
        inp['b_rel'] = jax.random.normal(ks[5], (NUM_REL, D), dtype=jnp.float32) * s
        inp['W_ih'] = jax.random.normal(ks[6], (4 * D, D), dtype=jnp.float32) * s
        inp['b_ih'] = jax.random.normal(ks[7], (4 * D,), dtype=jnp.float32) * s
        inp['b_hh'] = jax.random.normal(ks[8], (4 * D,), dtype=jnp.float32) * s
        h = D // 2
        inp['W1'] = jax.random.normal(ks[9], (h, D), dtype=jnp.float32) * s
        inp['b1'] = jax.random.normal(ks[10], (h,), dtype=jnp.float32) * s
        inp['W2'] = jax.random.normal(ks[11], (h, h), dtype=jnp.float32) * (1.0 / np.sqrt(h))
        inp['b2'] = jax.random.normal(ks[12], (h,), dtype=jnp.float32) * (1.0 / np.sqrt(h))
        inp['W3'] = jax.random.normal(ks[13], (D_OUT, h), dtype=jnp.float32) * (1.0 / np.sqrt(h))
        inp['b3'] = jax.random.normal(ks[14], (D_OUT,), dtype=jnp.float32) * (1.0 / np.sqrt(h))
        return inp
    _L0_gnn_all = _L0_gnn_setup()
    _L0_gnn_in = {k: v for k, v in _L0_gnn_all.items() if k in ('W_rel', 'b_rel', 'W_ih', 'b_ih', 'b_hh', 'W1', 'b1', 'W2', 'b2', 'W3', 'b3')}
    del _L0_gnn_all

    def _L1_gnn_setup():
        import jax, jax.numpy as jnp
        import numpy as np
        N_NODES = 3125
        N_EDGES = 100000
        DIM_IN = 256
        DIM_OUT = 256
        key = jax.random.key(seed)
        ks = jax.random.split(key, 8)
        feat_in = jax.random.normal(ks[0], (N_NODES, DIM_IN), dtype=jnp.float32)
        edge_row = jax.random.randint(ks[1], (N_EDGES,), 0, N_NODES, dtype=jnp.int32)
        edge_col = jax.random.randint(ks[2], (N_EDGES,), 0, N_NODES, dtype=jnp.int32)
        edge_val = jax.random.uniform(ks[3], (N_EDGES,), dtype=jnp.float32)
        s1 = 1.0 / np.sqrt(DIM_IN)
        s2 = 1.0 / np.sqrt(DIM_OUT)
        W1 = jax.random.normal(ks[4], (DIM_IN, DIM_OUT), dtype=jnp.float32) * s1
        b1 = jnp.zeros((DIM_OUT,), dtype=jnp.float32)
        W2 = jax.random.normal(ks[5], (DIM_OUT, DIM_OUT), dtype=jnp.float32) * s2
        b2 = jnp.zeros((DIM_OUT,), dtype=jnp.float32)
        eps = jnp.zeros((1,), dtype=jnp.float32)
        offset = jnp.zeros((DIM_OUT,), dtype=jnp.float32)
        scale = jnp.ones((DIM_OUT,), dtype=jnp.float32)
        return {'feat_in': feat_in, 'edge_row': edge_row, 'edge_col': edge_col, 'edge_val': edge_val, 'W1': W1, 'b1': b1, 'W2': W2, 'b2': b2, 'eps': eps, 'offset': offset, 'scale': scale}
    _L1_gnn_all = _L1_gnn_setup()
    _L1_gnn_in = {k: v for k, v in _L1_gnn_all.items() if k in ('W1', 'b1', 'W2', 'b2', 'eps', 'offset', 'scale')}
    del _L1_gnn_all
    return {'x': x, 'src': src, 'dst': dst, 'edge_type_2': edge_type_2, 'edge_weight': edge_weight, 'L0_gnn_W_rel': _L0_gnn_in['W_rel'], 'L0_gnn_b_rel': _L0_gnn_in['b_rel'], 'L0_gnn_W_ih': _L0_gnn_in['W_ih'], 'L0_gnn_b_ih': _L0_gnn_in['b_ih'], 'L0_gnn_b_hh': _L0_gnn_in['b_hh'], 'L0_gnn_W1': _L0_gnn_in['W1'], 'L0_gnn_b1': _L0_gnn_in['b1'], 'L0_gnn_W2': _L0_gnn_in['W2'], 'L0_gnn_b2': _L0_gnn_in['b2'], 'L0_gnn_W3': _L0_gnn_in['W3'], 'L0_gnn_b3': _L0_gnn_in['b3'], 'L1_gnn_W1': _L1_gnn_in['W1'], 'L1_gnn_b1': _L1_gnn_in['b1'], 'L1_gnn_W2': _L1_gnn_in['W2'], 'L1_gnn_b2': _L1_gnn_in['b2'], 'L1_gnn_eps': _L1_gnn_in['eps'], 'L1_gnn_offset': _L1_gnn_in['offset'], 'L1_gnn_scale': _L1_gnn_in['scale']}

def reference(x, src, dst, edge_type_2, edge_weight, L0_gnn_W_rel, L0_gnn_b_rel, L0_gnn_W_ih, L0_gnn_b_ih, L0_gnn_b_hh, L0_gnn_W1, L0_gnn_b1, L0_gnn_W2, L0_gnn_b2, L0_gnn_W3, L0_gnn_b3, L1_gnn_W1, L1_gnn_b1, L1_gnn_W2, L1_gnn_b2, L1_gnn_eps, L1_gnn_offset, L1_gnn_scale):
    import jax
    import jax.numpy as jnp

    def _L0_gnn_ref(feat, src, dst, rel, W_rel, b_rel, W_ih, b_ih, b_hh, W1, b1, W2, b2, W3, b3):
        import jax, jax.numpy as jnp
        import numpy as np
        N_NODES = 10000
        N_EDGES = 10000
        D = 256
        D_OUT = 256
        NUM_REL = 2
        n_nodes = feat.shape[0]
        S = feat[src]

        def edge_nn(x, W, b):
            h = jax.nn.relu(x @ W.T + b)
            return jax.nn.relu(h @ W.T + b)
        msgs = jnp.zeros_like(S)
        for r in range(W_rel.shape[0]):
            msgs = jnp.where((rel == r)[:, None], edge_nn(S, W_rel[r], b_rel[r]), msgs)
        agg = jax.ops.segment_sum(msgs, dst, num_segments=n_nodes)
        gates = agg @ W_ih.T + b_ih + b_hh
        i, f, g, o = jnp.split(gates, 4, axis=-1)
        c = jax.nn.sigmoid(i) * jnp.tanh(g)
        hn = jax.nn.sigmoid(o) * jnp.tanh(c)
        x = jax.nn.relu(hn @ W1.T + b1)
        x = jax.nn.relu(x @ W2.T + b2)
        return x @ W3.T + b3

    def _L1_gnn_ref(feat_in, edge_row, edge_col, edge_val, W1, b1, W2, b2, eps, offset, scale):
        import jax, jax.numpy as jnp
        import numpy as np
        N_NODES = 3125
        N_EDGES = 100000
        DIM_IN = 256
        DIM_OUT = 256
        msg = edge_val[:, None] * feat_in[edge_col]
        aggr = jax.ops.segment_sum(msg, edge_row, num_segments=feat_in.shape[0])
        aggr = aggr + (1.0 + eps) * feat_in
        h = jnp.maximum(aggr @ W1 + b1, 0.0) @ W2 + b2
        h = jnp.maximum(h, 0.0)
        mean = jnp.mean(h, axis=1, keepdims=True)
        var = jnp.var(h, axis=1, keepdims=True) + 1e-10
        return (h - mean) * scale * jax.lax.rsqrt(var) + offset
    h = jnp.maximum(_layernorm(x, axis=-1), 0.0)
    x = x + _L0_gnn_ref(h, src, dst, edge_type_2, L0_gnn_W_rel, L0_gnn_b_rel, L0_gnn_W_ih, L0_gnn_b_ih, L0_gnn_b_hh, L0_gnn_W1, L0_gnn_b1, L0_gnn_W2, L0_gnn_b2, L0_gnn_W3, L0_gnn_b3)
    h = jnp.maximum(_layernorm(x, axis=-1), 0.0)
    x = x + _L1_gnn_ref(h, src, dst, edge_weight, L1_gnn_W1, L1_gnn_b1, L1_gnn_W2, L1_gnn_b2, L1_gnn_eps, L1_gnn_offset, L1_gnn_scale)
    return x

_drawn_inputs = setup_inputs


def setup_inputs(seed=0):
    import zlib

    import numpy as np

    out = dict(_drawn_inputs(seed))
    spreads = {'L1_gnn_b1': (0.0, 0.382),
     'L1_gnn_b2': (0.0, 0.1),
     'L1_gnn_offset': (0.0, 0.1),
     'L1_gnn_scale': (1.0, 0.2)}
    factors = {'L0_gnn_b_ih': 8.0, 'L0_gnn_b_hh': 8.0}
    for name, (base, spread) in spreads.items():
        noise = np.random.default_rng([zlib.crc32(name.encode()), seed]).standard_normal(out[name].shape)
        drawn = base * np.exp(spread * noise) if base else spread * noise
        out[name] = jnp.asarray(drawn.astype(out[name].dtype))
    for name, factor in factors.items():
        out[name] = (out[name] * factor).astype(out[name].dtype)
    return out
```

```python
from contextlib import ExitStack

import concourse.bass as bass
from concourse import mybir

P = 128
F32 = mybir.dt.float32
I32 = mybir.dt.int32
ALU = mybir.AluOpType
ACT = mybir.ActivationFunctionType
AX = mybir.AxisListType

GROUP = 8
ACCS = 4
LAG = 3


def gnn_kernel(nc, x, src, dst, edge_type_2, edge_weight, W_rel, b_rel, W_ih, b_ih, b_hh, W1, b1, W2, b2,
               W3, b3, G_W1, G_b1, G_W2, G_b2, G_eps, G_offset, G_scale, out):
    NODES, D = x.shape
    EDGES = src.shape[0]
    NT = -(-NODES // P)
    LAST = NODES - (NT - 1) * P
    ET = -(-EDGES // P)
    NG = ET // GROUP
    NPAIR = NG // 2
    ROWS = NT * P + P
    KD = D // P
    assert D == 256 and NG * GROUP == ET and NG % 2 == 0 and ET <= 512 and NPAIR == NT + 1
    assert ROWS == 26 * P and b1.shape[0] == P
    EC = -(-ET // P)
    FULL = (EC - 1) * P
    RT = ET - FULL
    PART = EDGES - (ET - 1) * P
    ZROW = 2 * NODES
    FLAG = NG

    ctx = ExitStack()
    with ctx:
        def sb(name, shape, dt=F32):
            return ctx.enter_context(nc.sbuf_tensor(name, shape, dt))

        def sem(name):
            return ctx.enter_context(nc.semaphore(name))

        msg_table = nc.dram_tensor("msg_table", [2 * NODES + 1, D], F32).ap()
        h_table = nc.dram_tensor("h_table", [ROWS, D], F32).ap()
        acc = [nc.dram_tensor(f"acc{k}", [ROWS, D], F32).ap() for k in range(ACCS)]

        ident = sb("ident", [P, P])
        iota_row = sb("iota_row", [P, P])
        earlier = sb("earlier", [P, P])
        row0 = sb("row0", [P, P])
        spare = sb("spare", [P, 1])
        wbase = sb("wbase", [P, NT])
        ones = sb("ones", [P, P])
        minus_half = sb("minus_half", [P, 2])
        rel_raw = sb("rel_raw", [P, 2, KD, D])
        relT = sb("relT", [P, 2, KD, D])
        ih_raw = sb("ih_raw", [P, 6, D])
        ihT = sb("ihT", [P, 6, KD, P])
        w1_raw = sb("w1_raw", [P, D])
        w2_raw = sb("w2_raw", [P, P])
        w3_raw = sb("w3_raw", [P, KD, P])
        w1T = sb("w1T", [P, KD, P])
        w2T = sb("w2T", [P, P])
        w3T = sb("w3T", [P, D])
        gw1 = sb("gw1", [P, KD, D])
        gw2 = sb("gw2", [P, KD, D])
        NB = 24
        bias_rows = sb("bias_rows", [NB, P])
        bias = sb("bias", [P, NB])
        gate_bias = sb("gate_bias", [P, 8])
        gate_half = sb("gate_half", [P, 8])
        brel_b = sb("brel_b", [P, 2, D])
        b3_row = sb("b3_row", [1, D])
        b2_b = sb("b2_b", [P, D])
        scale_b = sb("scale_b", [P, D])
        offset_b = sb("offset_b", [P, D])
        eps_b = sb("eps_b", [P, 1])
        xr = sb("xr", [P, NT, D])
        aggT = sb("aggT", [P, KD, ROWS])
        e_int = sb("e_int", [P, 3, EC, P], I32)
        e_w = sb("e_w", [P, EC, P])
        e_f = sb("e_f", [P, 3, EC, P])
        srcT = sb("srcT", [P, ET])
        dstT = sb("dstT", [P, ET])
        typT = sb("typT", [P, ET])
        wT = sb("wT", [P, ET])
        loc = sb("loc", [P, NG, GROUP])
        base_f = sb("base_f", [P, NG])
        to_spare = sb("to_spare", [P, ET])
        isr = sb("isr", [P, 2, ET])
        gidx = sb("gidx", [P, ET], I32)
        dst_i = sb("dst_i", [P, ET], I32)
        ctrl = sb("ctrl", [1, NG + 8], I32)
        chk = sb("chk", [P, 8])
        chk_row = sb("chk_row", [1, 4, NG])
        bst = sb("bst", [P, 2, 6])
        mv = sb("mv", [P, 2, 2])
        veps = sb("veps", [P, 2])
        rstd = sb("rstd", [P, 2])
        nbias = sb("nbias", [P, 2])
        hrow = sb("hrow", [P, D])
        hT = sb("hT", [P, KD, P])
        midT = sb("midT", [P, 2, KD, P])
        ysum = sb("ysum", [P, 2, D])
        yrow = sb("yrow", [P, 2, D])
        ix = sb("ix", [P, 2, GROUP], I32)
        msgs = sb("msgs", [P, 2, GROUP, D])
        oh = sb("oh", [P, 2, GROUP, P])
        tg = sb("tg", [P, 6, P])
        cell = sb("cell", [P, 2, P])
        tcell = sb("tcell", [P, 2, P])
        hn = sb("hn", [P, 2, P])
        x1T = sb("x1T", [P, P])
        x2T = sb("x2T", [P, P])
        hsc = sb("hsc", [P, D])
        onep = sb("onep", [P, 1])
        wloc = sb("wloc", [P, GROUP])
        scol = sb("scol", [P, GROUP])
        same = oh[:, 0]
        ohw = oh[:, 1]
        prior = sb("prior", [P, GROUP, P])
        dup = sb("dup", [P, GROUP])
        sidx_f = sb("sidx_f", [P, GROUP])
        sidx = sb("sidx", [P, 2, GROUP], I32)
        m_sb = sb("m_sb", [P, GROUP, P])
        hwin = sb("hwin", [P, 2, D])
        comb = sb("comb", [P, 2, GROUP, D])
        fa = [msgs[:, q].rearrange("p (k u) d -> p k u d", k=ACCS) for q in range(2)]
        fsum = comb[:, 0].rearrange("p (a u) d -> p a u d", u=2)
        ft = comb[:, 1].rearrange("p (a u) d -> p a u d", u=2)

        bank = [ctx.enter_context(nc.psum_tensor(f"bank{i}", [P, 512], F32)) for i in range(8)]

        s_xin = [sem(f"s_xin{i}") for i in range(3)]
        s_edges = sem("s_edges"); s_wrel = sem("s_wrel"); s_bias = sem("s_bias"); s_wts = sem("s_wts")
        s_pad = sem("s_pad"); s_zero = sem("s_zero"); s_aggz = sem("s_aggz")
        s_const = sem("s_const"); s_const_step = sem("s_const_step")
        s_relps = sem("s_relps"); s_relT = sem("s_relT")
        s_ef = sem("s_ef"); s_eps_ps = sem("s_eps_ps"); s_eT = sem("s_eT")
        s_base_ps = sem("s_base_ps"); s_base = sem("s_base"); s_prep = sem("s_prep")
        s_viol = sem("s_viol"); s_ctrl = sem("s_ctrl"); s_gidx = sem("s_gidx")
        s_wps = sem("s_wps"); s_wT = sem("s_wT"); s_gb = sem("s_gb")
        s_stats = sem("s_stats"); s_aggr = sem("s_aggr"); s_veps = sem("s_veps"); s_rstd = sem("s_rstd"); s_nbias = sem("s_nbias")
        s_hrow = sem("s_hrow"); s_tr = sem("s_tr"); s_hT = sem("s_hT"); s_a = sem("s_a"); s_mid = sem("s_mid")
        s_b = sem("s_b"); s_ysum = sem("s_ysum"); s_yrow = sem("s_yrow")
        s_ystored = [sem(f"s_ystored{r}") for r in range(2)]
        s_staged = [sem(f"s_staged{b}") for b in range(2)]
        s_gathered = [sem(f"s_gathered{b}") for b in range(2)]
        s_oh = sem("s_oh"); s_summed = sem("s_summed"); s_added = sem("s_added")
        s_gates = sem("s_gates"); s_tg = sem("s_tg"); s_cell = sem("s_cell"); s_tcell = sem("s_tcell")
        s_hn = sem("s_hn"); s_w1 = sem("s_w1"); s_x1 = sem("s_x1"); s_w2 = sem("s_w2"); s_x2 = sem("s_x2")
        s_w3 = sem("s_w3"); s_xr = sem("s_xr"); s_hrow1 = sem("s_hrow1"); s_hsc = sem("s_hsc")
        s_off = sem("s_off")
        s_hstored = sem("s_hstored"); s_acc0 = sem("s_acc0")
        g_staged = sem("g_staged"); g_gathered = sem("g_gathered"); g_loc = sem("g_loc"); g_oh = sem("g_oh")
        g_summed = sem("g_summed"); g_added = sem("g_added")
        s_scol = sem("s_scol"); s_srow = sem("s_srow"); s_same = sem("s_same"); s_eq = sem("s_eq")
        s_ohw = sem("s_ohw"); s_prior = sem("s_prior"); s_dup = sem("s_dup"); s_dupm = sem("s_dupm")
        s_sidx = sem("s_sidx"); s_m = sem("s_m"); s_mcopied = sem("s_mcopied"); s_comb = sem("s_comb")
        s_combsb = sem("s_combsb")
        s_hwin = [sem(f"s_hwin{b}") for b in range(2)]
        s_passed = sem("s_passed")
        s_scattered = [sem(f"s_scattered{k}") for k in range(ACCS)]
        g_staged2 = sem("g_staged2"); g_gathered2 = sem("g_gathered2")
        f_loaded = [sem(f"f_loaded{q}") for q in range(2)]
        f_s23 = sem("f_s23"); f_s01 = sem("f_s01"); f_sum = sem("f_sum"); f_tr = sem("f_tr"); f_aT = sem("f_aT")
        f_a = sem("f_a"); f_h = sem("f_h"); f_b = sem("f_b"); f_t = sem("f_t"); f_r = sem("f_r")
        f_stats = sem("f_stats"); f_aggr = sem("f_aggr"); f_veps = sem("f_veps"); f_rstd = sem("f_rstd"); f_q = sem("f_q")
        f_out = sem("f_out"); f_stored = [sem(f"f_stored{q}") for q in range(2)]

        go_aggr = sem("go_aggr"); go_scale = sem("go_scale"); go_gather = sem("go_gather")
        go_windows = sem("go_windows")

        block = ctx.enter_context(nc.Block())

        NF = 6
        assert NT == 4 * NF + 1

        def flag_of(e):
            e.wait_ge(s_ctrl, 2)
            return e.value_load(ctrl[0:1, FLAG:FLAG + 1], min_val=0, max_val=1)

        @block.sync
        def _(sp):
            xq = [(0, 2), (2, 10), (10, NT - 1)]
            for i, (a, b) in enumerate(xq):
                sp.dma_start(xr[:, a:b, :], x[a * P:b * P, :].rearrange("(t p) d -> p t d", p=P)).then_inc(s_xin[i], 16)
                if i == 0:
                    for r in range(2):
                        sp.dma_start(rel_raw[:, r], W_rel[r].rearrange("(c p) i -> p c i", p=P)).then_inc(s_wrel, 16)
            sp.wait_ge(s_pad, 3)
            sp.dma_start(xr[0:LAST, NT - 1, :], x[(NT - 1) * P:NODES, :]).then_inc(s_xin[2], 16)
            sp.wait_ge(s_aggz, 1)
            for k in range(ACCS):
                sp.dma_start(acc[k].rearrange("(p a) d -> p (a d)", p=P),
                             aggT[:, :, :].rearrange("p k n -> p (k n)")).then_inc(s_zero, 16)
            sp.dma_start(msg_table[ZROW:ZROW + 1, :], aggT[0:1, 0, 0:D]).then_inc(s_zero, 16)
            sp.dma_start(h_table[NT * P:ROWS, :], aggT[:, 0, 0:D]).then_inc(s_zero, 16)

            def store_messages(t, rows):
                for r in range(2):
                    sp.wait_ge(s_yrow, t * 2 + (r + 1))
                    sp.dma_start(msg_table[bass.ds(t * P + r * NODES, rows), :],
                                 yrow[0:rows, r, :]).then_inc(s_ystored[r], 16)

            with sp.Fori(0, NT - 1) as t:
                store_messages(t, P)
            store_messages(NT - 1, LAST)

            def store_h(w, rows):
                sp.wait_ge(s_hrow1, w + 1)
                sp.dma_start(h_table[bass.ds(w * P, P), :], hrow[:, :]).then_inc(s_hstored, 16)
                sp.wait_ge(s_hsc, w + 1)
                sp.dma_start(acc[0][bass.ds(w * P, rows), :], hsc[0:rows, :]).then_inc(s_acc0, 16)

            sp.wait_ge(s_zero, 16 * (ACCS + 2))
            sp.wait_ge(s_gidx, 1)
            flag = flag_of(sp)
            with sp.If(flag < 1):
                def stage(i, b):
                    sp.wait_ge(s_gathered[b], i * (16 * GROUP))
                    sp.dma_start(ix[:, b, :], gidx[:, bass.ds(i * (2 * GROUP) + b * GROUP, GROUP)]).then_inc(s_staged[b], 16)

                for i in range(LAG):
                    stage(i, 0)
                    stage(i, 1)
                with sp.Fori(LAG, NPAIR) as i:
                    stage(i, 0)
                    stage(i, 1)
                    store_h(i - LAG, P)
                for w in range(NPAIR - LAG, NT - 1):
                    store_h(w, P)
                store_h(NT - 1, LAST)
                sp.wait_ge(s_hstored, 16 * NT)
                with sp.Fori(0, NPAIR) as i:
                    for b in range(2):
                        base = sp.value_load(ctrl[0:1, bass.ds(i * 2 + b, 1)], min_val=0, max_val=NODES - 1)
                        sp.wait_ge(s_comb, i * 2 + b + 1)
                        sp.dma_start(hwin[:, b, :], h_table[bass.ds(base, P), :]).then_inc(s_hwin[b], 16)
            with sp.Else():
                with sp.Fori(0, NG) as g:
                    sp.wait_ge(g_gathered, g * (16 * GROUP))
                    sp.dma_start(ix[:, 0, :], gidx[:, bass.ds(g * GROUP, GROUP)]).then_inc(g_staged, 16)
                with sp.Fori(0, NT - 1) as w:
                    store_h(w, P)
                store_h(NT - 1, LAST)
                sp.wait_ge(s_hstored, 16 * NT)
                with sp.Fori(0, NG) as g:
                    sp.wait_ge(g_gathered2, g * (16 * GROUP))
                    sp.dma_start(ix[:, 1, :], dst_i[:, bass.ds(g * GROUP, GROUP)]).then_inc(g_staged2, 16)
            for k in range(ACCS):
                sp.wait_ge(s_scattered[k], 16 * (ET // ACCS))

            def load_sums(i, q, tiles):
                sp.wait_ge(f_sum, i * 2 + q + 1)
                for k in range(ACCS):
                    sp.dma_start(fa[q][:, k, 0:tiles, :],
                                 acc[k][bass.ds(i * (4 * P) + q * 2 * P, tiles * P), :].rearrange("(u p) d -> p u d", p=P)
                                 ).then_inc(f_loaded[q], 16)

            def store_out(i, q, rows):
                sp.wait_ge(f_out, i * 2 + q + 1)
                if rows == 2 * P:
                    sp.dma_start(out[bass.ds(i * (4 * P) + q * 2 * P, rows), :].rearrange("(u p) d -> p u d", p=P),
                                 ft[:, 2 + q, :, :]).then_inc(f_stored[q], 16)
                else:
                    sp.dma_start(out[NODES - rows:NODES, :], ft[0:rows, 2 + q, 0, :]).then_inc(f_stored[q], 16)

            load_sums(0, 0, 2)
            load_sums(0, 1, 2)
            with sp.Fori(0, NF - 1) as i:
                for q in range(2):
                    load_sums(i + 1, q, 2)
                    store_out(i, q, 2 * P)
            load_sums(NF, 0, 1)
            store_out(NF - 1, 0, 2 * P)
            store_out(NF - 1, 1, 2 * P)
            store_out(NF, 0, LAST)
            sp.wait_ge(f_stored[0], 16 * (NF + 1))
            sp.wait_ge(f_stored[1], 16 * NF)

        @block.gpsimd
        def _(pool):
            pool.memset(e_int[0:RT, 2, EC - 1, :], 2).then_inc(s_pad, 1)
            pool.memset(e_w[0:RT, EC - 1, :], 0.0).then_inc(s_pad, 1)
            pool.memset(xr[:, NT - 1, :], 0.0).then_inc(s_pad, 1)
            pool.memset(ident[:, :], 0.0)
            pool.memset(row0[:, :], 0.0)
            pool.memset(earlier[:, :], 1.0)
            pool.memset(ones[:, :], 1.0)
            pool.memset(minus_half[:, :], -0.5)
            pool.iota(iota_row[:, :], [[1, P]], base=0, channel_multiplier=0, allow_small_or_imprecise_dtypes=True)
            pool.iota(wbase[:, :], [[P, NT]], base=0, channel_multiplier=0, allow_small_or_imprecise_dtypes=True)
            pool.iota(spare[:, :], [[1, 1]], base=NODES, channel_multiplier=1,
                      allow_small_or_imprecise_dtypes=True).then_inc(s_const_step, 1)
            pool.wait_ge(s_const_step, 1)
            pool.affine_select(out=ident[:, :], in_=ident[:, :], compare_op=ALU.not_equal, fill=1.0, base=0,
                               pattern=[[-1, P]], channel_multiplier=1)
            pool.affine_select(out=row0[:, :], in_=row0[:, :], compare_op=ALU.not_equal, fill=1.0, base=0,
                               pattern=[[0, P]], channel_multiplier=1)
            pool.affine_select(out=earlier[:, :], in_=earlier[:, :], compare_op=ALU.is_gt, fill=0.0, base=0,
                               pattern=[[-1, P]], channel_multiplier=1).then_inc(s_const, 1)
            pool.memset(aggT[:, :, :], 0.0).then_inc(s_aggz, 1)
            pool.sem_inc(s_passed, GROUP)

            def gather(table, index, b, signal):
                for j in range(GROUP):
                    pool.indirect_dma_start(msgs[:, b, j, :], None, table,
                                            bass.IndirectOffsetOnAxis(ap=ix[:, index, j:j + 1], axis=0)).then_inc(signal, 16)

            def scatter(i, b):
                pool.wait_ge(s_sidx, i * 2 + b + 1)
                pool.wait_ge(s_combsb, i * 2 + b + 1)
                for j in range(GROUP):
                    k = j % ACCS
                    pool.wait_ge(s_acc0, 16 * NT)
                    pool.wait_ge(s_scattered[k], i * 64 + (32 * b + 16 * (j // ACCS)))
                    pool.sem_inc(s_passed, 1)
                    pool.indirect_dma_start(acc[k], bass.IndirectOffsetOnAxis(ap=sidx[:, b, j:j + 1], axis=0),
                                            comb[:, b, j, :], None, compute_op=ALU.add).then_inc(s_scattered[k], 16)

            def scale_bias(n, which):
                pool.wait_ge(s_aggr, n + 1)
                pool.sem_inc(go_scale, 1)
                pool.tensor_scalar(veps[:, which:which + 1], mv[:, which, 1:2], 1e-5, None, ALU.add).then_inc(s_veps, 1)
                pool.wait_ge(s_veps, n + 1)
                pool.tensor_tensor(rstd[:, which:which + 1], veps[:, which:which + 1], minus_half[:, 0:1], ALU.pow).then_inc(s_rstd, 1)
                pool.wait_ge(s_rstd, n + 1)
                pool.sem_inc(go_scale, 1)
                pool.tensor_scalar(nbias[:, which:which + 1], mv[:, which, 0:1], rstd[:, which:which + 1], -1.0,
                                   ALU.mult, ALU.mult).then_inc(s_nbias, 1)

            with pool.Fori(0, NT) as t:
                scale_bias(t, 0)
            for r in range(2):
                pool.wait_ge(s_ystored[r], 16 * NT)
            pool.wait_ge(s_zero, 16 * (ACCS + 2))
            flag = flag_of(pool)
            with pool.If(flag < 1):
                def gather_pair(i):
                    for b in range(2):
                        pool.wait_ge(s_zero, 16 * (ACCS + 2))
                        pool.wait_ge(s_staged[b], i * 16 + 16)
                        pool.wait_ge(s_summed, i * 2 + b + 1)
                        pool.sem_inc(go_gather, 1)
                        gather(msg_table, b, b, s_gathered[b])

                for i in range(LAG + 1):
                    gather_pair(i)
                with pool.Fori(LAG + 1, NPAIR) as i:
                    scale_bias(i + (NT - LAG - 1), 1)
                    gather_pair(i)
                for w in range(NPAIR - LAG - 1, NT):
                    scale_bias(NT + w, 1)
                with pool.Fori(0, NPAIR) as i:
                    scatter(i, 0)
                    scatter(i, 1)
            with pool.Else():
                with pool.Fori(0, NG) as g:
                    pool.wait_ge(s_zero, 16 * (ACCS + 2))
                    pool.wait_ge(g_staged, g * 16 + 16)
                    pool.wait_ge(g_summed, g * NT)
                    pool.sem_inc(go_gather, 1)
                    gather(msg_table, 0, 0, g_gathered)
                with pool.Fori(0, NT) as w:
                    scale_bias(w + NT, 1)
                with pool.Fori(0, NPAIR) as i:
                    for b in range(2):
                        pool.wait_ge(s_hstored, 16 * NT)
                        pool.wait_ge(g_staged2, i * 32 + (16 * b + 16))
                        pool.wait_ge(s_comb, i * 2 + (b + 2))
                        pool.sem_inc(go_gather, 1)
                        gather(h_table, 1, 1, g_gathered2)
                        scatter(i, b)
            pool.nop()

            def sum23(i, q, n):
                pool.wait_ge(f_loaded[q], i * (16 * ACCS) + 16 * ACCS)
                pool.wait_ge(f_sum, i * 2 + q + 1)
                pool.tensor_tensor(fsum[:, 2 + q, 0:n, :], fa[q][:, 2, 0:n, :], fa[q][:, 3, 0:n, :], ALU.add).then_inc(f_s23, 1)

            def row_scale(i, q, n):
                pool.wait_ge(f_out, i * 2 + q)
                pool.wait_ge(f_aggr, i * 2 + q + 1)
                pool.sem_inc(go_scale, 1)
                pool.tensor_scalar(veps[:, 0:n], mv[:, 0:n, 1:2].rearrange("p u a -> p (u a)"), 1e-10, None,
                                   ALU.add).then_inc(f_veps, 1)
                pool.wait_ge(f_veps, i * 2 + q + 1)
                pool.tensor_tensor(rstd[:, 0:n], veps[:, 0:n], minus_half[:, 0:n], ALU.pow).then_inc(f_rstd, 1)

            sum23(0, 0, 2)
            with pool.Fori(0, NF - 1) as i:
                sum23(i, 1, 2)
                row_scale(i, 0, 2)
                sum23(i + 1, 0, 2)
                row_scale(i, 1, 2)
            sum23(NF - 1, 1, 2)
            row_scale(NF - 1, 0, 2)
            sum23(NF, 0, 1)
            row_scale(NF - 1, 1, 2)
            row_scale(NF, 0, 1)

        @block.scalar
        def _(act):
            act.wait_ge(s_pad, 2)
            for n, a in enumerate((src, dst, edge_type_2)):
                act.dma_start(e_int[:, n, 0:EC - 1, :], a[0:FULL * P].rearrange("(c p e) -> p c e", p=P, e=P)).then_inc(s_edges, 16)
                act.dma_start(e_int[0:RT - 1, n, EC - 1, :], a[FULL * P:(ET - 1) * P].rearrange("(p e) -> p e", e=P)).then_inc(s_edges, 16)
                act.dma_start(e_int[RT - 1:RT, n, EC - 1, 0:PART], a[(ET - 1) * P:EDGES].unsqueeze(0)).then_inc(s_edges, 16)
                if n < 2:
                    act.dma_start(e_int[RT - 1:RT, n, EC - 1, PART:P], a[EDGES - (P - PART):EDGES].unsqueeze(0)).then_inc(s_edges, 16)
            act.dma_start(e_w[:, 0:EC - 1, :], edge_weight[0:FULL * P].rearrange("(c p e) -> p c e", p=P, e=P)).then_inc(s_edges, 16)
            act.dma_start(e_w[0:RT - 1, EC - 1, :], edge_weight[FULL * P:(ET - 1) * P].rearrange("(p e) -> p e", e=P)).then_inc(s_edges, 16)
            act.dma_start(e_w[RT - 1:RT, EC - 1, 0:PART], edge_weight[(ET - 1) * P:EDGES].unsqueeze(0)).then_inc(s_edges, 16)
            act.dma_start(bias_rows[0:4, :], b_rel.rearrange("r (k p) -> (r k) p", p=P)).then_inc(s_bias, 16)
            act.dma_start(bias_rows[4:12, :], b_ih.rearrange("(k p) -> k p", p=P)).then_inc(s_bias, 16)
            act.dma_start(bias_rows[12:20, :], b_hh.rearrange("(k p) -> k p", p=P)).then_inc(s_bias, 16)
            act.dma_start(bias_rows[20:21, :], b1.unsqueeze(0)).then_inc(s_bias, 16)
            act.dma_start(bias_rows[21:22, :], b2.unsqueeze(0)).then_inc(s_bias, 16)
            act.dma_start(bias_rows[22:24, :], G_b1.rearrange("(k p) -> k p", p=P)).then_inc(s_bias, 16)
            act.dma_start(brel_b[:, :, :], b_rel.unsqueeze(0).to_broadcast([P, 2, D])).then_inc(s_bias, 16)

            def load_weights():
                loads = [(ih_raw[:, 0:2, :], W_ih[0:D, :].rearrange("(c p) i -> p c i", p=P)),
                         (ih_raw[:, 2:6, :], W_ih[2 * D:4 * D, :].rearrange("(c p) i -> p c i", p=P)),
                         (w1_raw[:, :], W1), (w2_raw[:, :], W2),
                         (w3_raw[:, :, :], W3.rearrange("(c p) i -> p c i", p=P)),
                         (gw1[:, :, :], G_W1.rearrange("(k p) o -> p k o", p=P)),
                         (gw2[:, :, :], G_W2.rearrange("(k p) o -> p k o", p=P)),
                         (b3_row[:, :], b3.unsqueeze(0)),
                         (b2_b[:, :], G_b2.unsqueeze(0).to_broadcast([P, D])),
                         (scale_b[:, :], G_scale.unsqueeze(0).to_broadcast([P, D])),
                         (offset_b[:, :], G_offset.unsqueeze(0).to_broadcast([P, D])),
                         (eps_b[:, :], G_eps.unsqueeze(0).to_broadcast([P, 1]))]
                for to, of in loads:
                    act.dma_start(to, of).then_inc(s_wts, 16)
                assert len(loads) == N_WTS

            def norm_row(t):
                act.wait_ge(s_nbias, t + 1)
                act.wait_ge(s_tr, t)
                act.activation(hrow[:, :], xr[:, bass.ds(t, 1), :].rearrange("p a d -> p (a d)"), ACT.Relu,
                               bias=nbias[:, 0:1], scale=rstd[:, 0:1]).then_inc(s_hrow, 1)

            def copy_hT(t):
                act.wait_ge(s_tr, t + 1)
                act.wait_ge(s_a, t * 2)
                act.copy(hT[:, :, :].rearrange("p k n -> p (k n)"), bank[0][:, 0:D]).then_inc(s_hT, 1)

            def mid(t, r):
                act.wait_ge(s_a, t * 2 + (r + 1))
                act.wait_ge(s_b, t * 2)
                for o in range(KD):
                    last = act.activation(midT[:, r, o, :], bank[2 + r][:, o * P:(o + 1) * P], ACT.Relu,
                                          bias=bias[:, 2 * r + o:2 * r + o + 1])
                last.then_inc(s_mid, 1)

            def messages(t, r):
                act.wait_ge(s_ysum, t * 2 + (r + 1))
                act.wait_ge(s_ystored[r], t * 16)
                act.activation(yrow[:, r, :], ysum[:, r, :], ACT.Relu).then_inc(s_yrow, 1)

            act.wait_ge(s_xin[0], 16)
            norm_row(0)
            copy_hT(0)
            act.wait_ge(s_relT, 3)
            act.wait_ge(s_xin[1], 16)
            act.wait_ge(s_xin[2], 32)
            load_weights()

            def table_tile(t, last):
                mid(t, 0)
                if not last:
                    norm_row(t + 1)
                mid(t, 1)
                if not last:
                    copy_hT(t + 1)
                messages(t, 0)
                messages(t, 1)

            with act.Fori(0, NT - 1) as t:
                table_tile(t, False)
            table_tile(NT - 1, True)

            def gates(w):
                act.wait_ge(s_gates, w + 1)
                act.wait_ge(s_hn, w)
                for c in range(6):
                    half = c // 2 != 1
                    col = (0, 1, 4, 5, 6, 7)[c]
                    last = act.activation(tg[:, c, :], bank[2 + c // 4][:, (c % 4) * P:(c % 4 + 1) * P], ACT.Tanh,
                                          bias=(gate_half if half else gate_bias)[:, col:col + 1],
                                          scale=0.5 if half else 1.0)
                last.then_inc(s_tg, 1)

            def cell_tanh(w):
                act.wait_ge(s_cell, w + 1)
                act.wait_ge(s_hn, w)
                act.activation(tcell[:, :, :].rearrange("p k n -> p (k n)"), cell[:, :, :].rearrange("p k n -> p (k n)"),
                               ACT.Tanh, scale=0.5).then_inc(s_tcell, 1)

            def mlp1(w):
                act.wait_ge(s_w1, w + 1)
                act.wait_ge(s_w2, w)
                act.activation(x1T[:, :], bank[4][:, 0:P], ACT.Relu, bias=bias[:, 20:21], scale=0.5).then_inc(s_x1, 1)

            def mlp2(w):
                act.wait_ge(s_w2, w + 1)
                act.wait_ge(s_w3, w)
                act.activation(x2T[:, :], bank[4][:, P:2 * P], ACT.Relu, bias=bias[:, 21:22]).then_inc(s_x2, 1)

            def norm_row1(w):
                act.wait_ge(s_nbias, w + (NT + 1))
                act.wait_ge(s_hstored, w * 16)
                act.activation(hrow[:, :], xr[:, bass.ds(w, 1), :].rearrange("p a d -> p (a d)"), ACT.Relu,
                               bias=nbias[:, 1:2], scale=rstd[:, 1:2]).then_inc(s_hrow1, 1)
                act.wait_ge(s_hrow1, w + 1)
                act.wait_ge(s_acc0, w * 16)
                act.activation(hsc[:, :], hrow[:, :], ACT.Copy, scale=onep[:, 0:1]).then_inc(s_hsc, 1)

            def node_tile(w):
                gates(w)
                cell_tanh(w)
                mlp1(w)
                mlp2(w)
                norm_row1(w)

            def copy_m(i, b):
                act.wait_ge(s_m, i * 2 + (b + 1))
                act.wait_ge(s_comb, i * 2 + (b + 2))
                for c in range(2):
                    last = act.copy(m_sb[:, 4 * c:4 * c + 4, :].rearrange("p j e -> p (j e)"), bank[2 + c][:, :])
                last.then_inc(s_mcopied, 1)

            def copy_comb(i, b):
                act.wait_ge(s_comb, i * 2 + (b + 3))
                act.wait_ge(s_passed, i * (2 * GROUP) + (b * GROUP + ACCS))
                for c in range(4):
                    last = act.copy(comb[:, b, 2 * c:2 * c + 2, :].rearrange("p j d -> p (j d)"), bank[4 + c][:, :])
                last.then_inc(s_combsb, 1)

            flag = flag_of(act)
            with act.If(flag < 1):
                with act.Fori(0, NT) as w:
                    node_tile(w)
                with act.Fori(0, NPAIR) as i:
                    for b in range(2):
                        copy_m(i, b)
                        copy_comb(i, b)
            with act.Else():
                with act.Fori(0, NT) as w:
                    node_tile(w)
                with act.Fori(0, NPAIR) as i:
                    copy_comb(i, 0)
                    copy_comb(i, 1)
            act.nop()

            def copy_aT(i, q, n):
                act.wait_ge(f_tr, i * 2 + (q + 1))
                act.wait_ge(f_a, i * 2 + q)
                act.copy(fsum[:, 0, :, :].rearrange("p u d -> p (u d)")[:, 0:KD * n * P], bank[0][:, 0:KD * n * P]).then_inc(f_aT, 1)

            def relu_hT(i, q, n):
                act.wait_ge(f_a, i * 2 + (q + 1))
                act.wait_ge(f_b, i * 2 + q)
                for o in range(KD):
                    last = act.activation(fsum[:, 1, :, :].rearrange("p u d -> p (u d)")[:, o * n * P:(o + 1) * n * P],
                                          bank[2][:, o * n * P:(o + 1) * n * P],
                                          ACT.Relu, bias=bias[:, 22 + o:23 + o])
                last.then_inc(f_h, 1)

            def relu_rows(i, q, n):
                act.wait_ge(f_t, i * 2 + (q + 1))
                act.wait_ge(f_q, i * 2 + q)
                act.activation(ft[:, 1, 0:n, :].rearrange("p u d -> p (u d)"), ft[:, 0, 0:n, :].rearrange("p u d -> p (u d)"),
                               ACT.Relu).then_inc(f_r, 1)

            with act.Fori(0, NF) as i:
                for q in range(2):
                    copy_aT(i, q, 2)
                    relu_hT(i, q, 2)
                    relu_rows(i, q, 2)
            copy_aT(NF, 0, 1)
            relu_hT(NF, 0, 1)
            relu_rows(NF, 0, 1)

        @block.vector
        def _(dve):
            def stats(v, n, which, applied, count, summed=None):
                dve.wait_ge(s_xin[0], 16)
                dve.wait_ge(applied, count)
                if summed is not None:
                    dve.wait_ge(s_xr, summed)
                dve.bn_stats(bst[:, which, :], v).then_inc(s_stats, 1)
                dve.wait_ge(s_stats, n + 1)
                dve.sem_inc(go_aggr, 1)
                dve.bn_aggr(mv[:, which, :], bst[:, which, :]).then_inc(s_aggr, 1)

            def x_tile(t):
                return xr[:, bass.ds(t, 1), :].rearrange("p a d -> p (a d)")

            dve.wait_ge(s_xin[0], 16)
            stats(xr[:, 0, :], 0, 0, s_hrow, 0)
            dve.wait_ge(s_relps, 1)
            dve.tensor_copy(relT[:, 0].rearrange("p k o -> p (k o)"), bank[4][:, :]).then_inc(s_relT, 1)
            dve.wait_ge(s_relps, 2)
            dve.tensor_copy(relT[:, 1].rearrange("p k o -> p (k o)"), bank[5][:, :]).then_inc(s_relT, 1)
            dve.wait_ge(s_relps, 3)
            dve.tensor_copy(bias[:, :], bank[6][:, 0:NB]).then_inc(s_relT, 1)
            dve.wait_ge(s_relT, 3)
            dve.tensor_tensor(gate_bias[:, :], bias[:, 4:12], bias[:, 12:20], ALU.add).then_inc(s_gb, 1)
            dve.wait_ge(s_gb, 1)
            dve.tensor_scalar(gate_half[:, :], gate_bias[:, :], 0.5, None, ALU.mult).then_inc(s_gb, 1)
            dve.wait_ge(s_xin[1], 16)
            dve.wait_ge(s_xin[2], 32)

            def edges_to_float():
                dve.wait_ge(s_edges, 16 * 14)
                dve.tensor_copy(e_f[:, :, 0:EC - 1, :], e_int[:, :, 0:EC - 1, :])
                dve.tensor_copy(e_f[0:RT, :, EC - 1, :], e_int[0:RT, :, EC - 1, :]).then_inc(s_ef, 1)

            def edge_columns():
                for n, to in enumerate((srcT, dstT, typT, wT)):
                    dve.wait_ge(s_eps_ps, n + 1)
                    dve.tensor_copy(to[:, :], bank[(6, 7, 1, 6)[n]][:, 0:ET]).then_inc(s_eT, 1)

                prep = [0]

                def step(ins):
                    prep[0] += 1
                    ins.then_inc(s_prep, 1)
                    dve.wait_ge(s_prep, prep[0])

                dve.wait_ge(s_eT, 4)
                dve.wait_ge(s_base_ps, 1)
                dve.tensor_copy(base_f[:, :], bank[7][:, 0:NG]).then_inc(s_base, 1)
                dve.wait_ge(s_base, 1)
                for r in range(2):
                    step(dve.tensor_scalar(isr[:, r, :], typT[:, :], float(r), None, ALU.is_equal))
                    step(dve.scalar_tensor_tensor(out=isr[:, r, :], in0=srcT[:, :], scalar=float(r * NODES - ZROW),
                                                  in1=isr[:, r, :], op0=ALU.add, op1=ALU.mult))
                step(dve.scalar_tensor_tensor(out=gidx[:, :], in0=isr[:, 0, :], scalar=float(ZROW), in1=isr[:, 1, :],
                                              op0=ALU.add, op1=ALU.add))
                step(dve.tensor_copy(dst_i[:, :], dstT[:, :]))
                step(dve.tensor_scalar(to_spare[:, :], srcT[:, :], -1.0, spare[:, 0:1], ALU.mult, ALU.add))
                dve.tensor_scalar(onep[:, :], eps_b[:, :], 1.0, None, ALU.add).then_inc(s_gidx, 1)
                step(dve.tensor_tensor(loc[:, :, :], dstT[:, :].rearrange("p (g j) -> p g j", j=GROUP),
                                       base_f[:, :].unsqueeze(2).to_broadcast([P, NG, GROUP]), ALU.subtract))
                step(dve.tensor_reduce(chk[:, 0:1], loc[:, :, :].rearrange("p g j -> p (g j)"), AX.X, ALU.max))
                step(dve.tensor_reduce(chk[:, 1:2], loc[:, :, :].rearrange("p g j -> p (g j)"), AX.X, ALU.min))
                step(dve.tensor_scalar(chk[:, 2:3], chk[:, 0:1], float(P - 1), None, ALU.is_gt))
                step(dve.scalar_tensor_tensor(out=chk[:, 3:4], in0=chk[:, 1:2], scalar=0.0, in1=chk[:, 2:3],
                                              op0=ALU.is_lt, op1=ALU.add))
                step(dve.tensor_tensor(chk_row[:, 0, 0:NG - 1], base_f[0:1, 1:NG], base_f[0:1, 0:NG - 1], ALU.is_lt))
                step(dve.tensor_reduce(chk_row[:, 1, 0:1], chk_row[:, 0, 0:NG - 1], AX.X, ALU.max))
                nw = NPAIR - LAG
                step(dve.scalar_tensor_tensor(out=chk_row[:, 2, 0:nw], in0=wbase[0:1, 0:nw], scalar=float(P),
                                              in1=base_f[0:1, 2 * LAG:NG:2], op0=ALU.add, op1=ALU.is_gt))
                step(dve.tensor_reduce(chk_row[:, 1, 1:2], chk_row[:, 2, 0:nw], AX.X, ALU.max))
                dve.tensor_copy(ctrl[0:1, 0:NG], base_f[0:1, :])
                step(dve.tensor_tensor(chk_row[:, 1, 2:3], chk_row[:, 1, 0:1], chk_row[:, 1, 1:2], ALU.add))
                step(dve.tensor_tensor(chk[0:1, 3:4], chk[0:1, 3:4], chk_row[:, 1, 2:3], ALU.add))
                dve.sem_inc(s_viol, 1)
                dve.wait_ge(s_viol, 2)
                step(dve.tensor_scalar(ctrl[0:1, FLAG:FLAG + 1], bank[7][0:1, P:P + 1], 0.0, None, ALU.is_gt))
                dve.sem_inc(s_ctrl, 2)

            def add_bias(t, r):
                dve.wait_ge(s_b, t * 2 + (r + 1))
                dve.wait_ge(s_yrow, t * 2)
                dve.tensor_tensor(ysum[:, r, :], bank[4 + r][:, 0:D], brel_b[:, r, :], ALU.add).then_inc(s_ysum, 1)

            def table_tile(t, last):
                if not last:
                    stats(x_tile(t + 1), t + 1, 0, s_hrow, t + 1)
                add_bias(t, 0)
                add_bias(t, 1)

            dve.wait_ge(s_bias, 16 * 7)
            edges_to_float()
            dve.wait_ge(s_wts, 16 * N_WTS)
            edge_columns()
            evacuate = [(w3T[:, :], bank[6][:, 0:D]), (w1T[:, :, :].rearrange("p k o -> p (k o)"), bank[1][:, 0:D]),
                        (w2T[:, :], bank[1][:, D:D + P])] + \
                       [(ihT[:, 2 * c:2 * c + 2].rearrange("p c k o -> p (c k o)"), bank[(6, 7, 6)[c]][:, :]) for c in range(3)]
            for n, (to, of) in enumerate(evacuate):
                dve.wait_ge(s_wps, n + 1)
                dve.tensor_copy(to, of).then_inc(s_wT, 1)

            with dve.Fori(0, NT - 1) as t:
                table_tile(t, False)
            table_tile(NT - 1, True)
            dve.sem_inc(s_added, 2)
            dve.wait_ge(s_zero, 16 * (ACCS + 2))

            def one_hot(i, b):
                dve.wait_ge(s_summed, i * 2 + (b + 1))
                dve.tensor_tensor(oh[:, b, :, :], iota_row[:, :].unsqueeze(1).to_broadcast([P, GROUP, P]),
                                  loc[:, bass.ds(i * 2 + b, 1), :].rearrange("p a j -> p (a j)").unsqueeze(2).to_broadcast([P, GROUP, P]),
                                  ALU.is_equal).then_inc(s_oh, 1)

            def add_window(i, b):
                base = dve.value_load(ctrl[0:1, bass.ds(i * 2 + b, 1)], min_val=0, max_val=NODES - 1)
                dve.wait_ge(s_summed, i * 2 + (b + 3))
                dve.wait_ge(s_added, i * 2 + (b + 2))
                v = aggT[:, :, bass.ds(base, P)]
                dve.tensor_tensor(v, v, bank[b][:, 0:D].rearrange("p (k n) -> p k n", k=KD), ALU.add).then_inc(s_added, 1)

            def cell_c(w):
                dve.wait_ge(s_tg, w + 1)
                dve.wait_ge(s_tcell, w)
                dve.scalar_tensor_tensor(out=cell[:, :, :], in0=tg[:, 0:2, :], scalar=1.0, in1=tg[:, 2:4, :],
                                         op0=ALU.add, op1=ALU.mult).then_inc(s_cell, 1)

            def cell_h(w):
                dve.wait_ge(s_tcell, w + 1)
                dve.wait_ge(s_w1, w)
                dve.scalar_tensor_tensor(out=hn[:, :, :], in0=tg[:, 4:6, :], scalar=1.0, in1=tcell[:, :, :],
                                         op0=ALU.add, op1=ALU.mult).then_inc(s_hn, 1)

            def residual(w):
                dve.wait_ge(s_w3, w + 1)
                dve.tensor_tensor(x_tile(w), x_tile(w), bank[5][:, 0:D], ALU.add).then_inc(s_xr, 1)
                stats(x_tile(w), w + NT, 1, s_hrow1, w, w + 1)
                dve.wait_ge(s_hrow1, w + 1)
                dve.tensor_tensor(x_tile(w), x_tile(w), offset_b[:, :], ALU.add).then_inc(s_off, 1)

            def sources(i, b, pre):
                dve.wait_ge(s_srow, i * 2 + b)
                dve.wait_ge(s_sidx, i * 2 + b)
                dve.tensor_copy(scol[:, :], srcT[:, bass.ds(i * (2 * GROUP) + b * GROUP, GROUP)]).then_inc(s_scol, 1)

            def same_source(i, b, used):
                dve.wait_ge(s_srow, i * 2 + (b + 1))
                dve.wait_ge(*used(i, b))
                dve.wait_ge(s_prior, i * 2 + b)
                for c in range(2):
                    last = dve.tensor_tensor(same[:, 4 * c:4 * c + 4, :], bank[c][:, :].rearrange("p (j e) -> p j e", e=P),
                                             scol[:, 4 * c:4 * c + 4].unsqueeze(2).to_broadcast([P, 4, P]), ALU.is_equal)
                last.then_inc(s_same, 1)

            def scatter_rows(i, b):
                dve.wait_ge(s_same, i * 2 + (b + 1))
                dve.wait_ge(s_dup, i * 2 + b)
                dve.tensor_tensor(prior[:, :, :], same, earlier[:, :].unsqueeze(1).to_broadcast([P, GROUP, P]),
                                  ALU.mult).then_inc(s_prior, 1)
                dve.wait_ge(s_prior, i * 2 + (b + 1))
                dve.wait_ge(s_dupm, i * 2 + b)
                dve.tensor_reduce(dup[:, :], prior[:, :, :], AX.X, ALU.max).then_inc(s_dup, 1)
                dve.wait_ge(s_dup, i * 2 + (b + 1))
                dve.wait_ge(s_sidx, i * 2 + b)
                dve.tensor_tensor(sidx_f[:, :], dup[:, :], to_spare[:, bass.ds(i * (2 * GROUP) + b * GROUP, GROUP)],
                                  ALU.mult).then_inc(s_dupm, 1)
                dve.wait_ge(s_dupm, i * 2 + (b + 1))
                dve.wait_ge(s_passed, i * (2 * GROUP) + (b * GROUP + ACCS))
                dve.tensor_tensor(sidx[:, b, :], sidx_f[:, :], scol[:, :], ALU.add).then_inc(s_sidx, 1)

            def weigh(i, b, what, sem_in, used):
                dve.wait_ge(sem_in, i * 2 + (b + 1))
                dve.wait_ge(*used(i, b))
                wcol = wT[:, bass.ds(i * (2 * GROUP) + b * GROUP, GROUP)].unsqueeze(2).to_broadcast([P, GROUP, P])
                dve.tensor_tensor(ohw, what, wcol, ALU.mult).then_inc(s_ohw, 1)

            dve.wait_ge(s_wT, 6)
            flag = flag_of(dve)
            with dve.If(flag < 1):
                one_hot(0, 0)
                one_hot(0, 1)
                for i in range(LAG):
                    add_window(i, 0)
                    one_hot(i + 1, 0)
                    add_window(i, 1)
                    one_hot(i + 1, 1)
                with dve.Fori(LAG, NPAIR - 1) as i:
                    w = i - LAG
                    cell_c(w)
                    cell_h(w)
                    add_window(i, 0)
                    one_hot(i + 1, 0)
                    add_window(i, 1)
                    one_hot(i + 1, 1)
                    residual(w)
                w = NPAIR - 1 - LAG
                cell_c(w)
                cell_h(w)
                add_window(NPAIR - 1, 0)
                add_window(NPAIR - 1, 1)
                residual(w)
                for w in range(NPAIR - LAG, NT):
                    cell_c(w)
                    cell_h(w)
                    residual(w)

                used = lambda i, b: (s_m, i * 2 + b)
                with dve.Fori(0, NPAIR) as i:
                    for b in range(2):
                        sources(i, b, 0)
                        dve.wait_ge(s_m, i * 2 + b)
                        dve.tensor_tensor(ohw, iota_row[:, :].unsqueeze(1).to_broadcast([P, GROUP, P]),
                                          loc[:, bass.ds(i * 2 + b, 1), :].rearrange("p a j -> p (a j)").unsqueeze(2).to_broadcast([P, GROUP, P]),
                                          ALU.is_equal).then_inc(s_eq, 1)
                        same_source(i, b, used)
                        weigh(i, b, ohw, s_eq, used)
                        scatter_rows(i, b)
            with dve.Else():
                with dve.Fori(0, NG) as g:
                    with dve.Fori(0, NT) as w:
                        k = g * NT + w
                        dve.wait_ge(g_oh, k)
                        dve.tensor_tensor(wloc[:, :], dstT[:, bass.ds(g * GROUP, GROUP)],
                                          wbase[:, bass.ds(w, 1)].to_broadcast([P, GROUP]), ALU.subtract).then_inc(g_loc, 1)
                        dve.wait_ge(g_loc, k + 1)
                        dve.wait_ge(g_summed, k)
                        dve.tensor_tensor(oh[:, 0, :, :], iota_row[:, :].unsqueeze(1).to_broadcast([P, GROUP, P]),
                                          wloc[:, :].unsqueeze(2).to_broadcast([P, GROUP, P]), ALU.is_equal).then_inc(g_oh, 1)
                        dve.wait_ge(g_summed, k + 1)
                        dve.wait_ge(g_added, k)
                        v = aggT[:, :, bass.ds(w * P, P)]
                        dve.tensor_tensor(v, v, bank[0][:, 0:D].rearrange("p (k n) -> p k n", k=KD), ALU.add).then_inc(g_added, 1)
                with dve.Fori(0, NT) as w:
                    cell_c(w)
                    cell_h(w)
                    residual(w)
                used = lambda i, b: (s_comb, i * 2 + (b + 2))
                with dve.Fori(0, NPAIR) as i:
                    for b in range(2):
                        sources(i, b, 0)
                        same_source(i, b, used)
                        weigh(i, b, same, s_same, used)
                        scatter_rows(i, b)
            dve.nop()

            dve.sem_inc(f_sum, 2)

            def total(i, q, n):
                dve.wait_ge(f_loaded[q], i * (16 * ACCS) + 16 * ACCS)
                dve.wait_ge(f_tr, i * 2 + q)
                dve.tensor_tensor(prior_sum[:, 0:n, :], fa[q][:, 0, 0:n, :], fa[q][:, 1, 0:n, :], ALU.add).then_inc(f_s01, 1)
                dve.wait_ge(f_s01, i * 2 + (q + 1))
                dve.wait_ge(f_s23, i * 2 + (q + 1))
                dve.tensor_tensor(total_sb[:, 0:n, :], prior_sum[:, 0:n, :], fsum[:, 2 + q, 0:n, :], ALU.add).then_inc(f_sum, 1)

            def finish(i, q, n):
                dve.wait_ge(f_b, i * 2 + (q + 1))
                dve.wait_ge(f_r, i * 2 + q)
                dve.tensor_tensor(ft[:, 0, 0:n, :], bank[4][:, 0:n * D].rearrange("p (u d) -> p u d", u=n),
                                  b2_b[:, :].unsqueeze(1).to_broadcast([P, n, D]), ALU.add).then_inc(f_t, 1)
                dve.wait_ge(f_r, 1)
                dve.wait_ge(f_r, i * 2 + (q + 1))
                for u in range(n):
                    last = dve.bn_stats(bst[:, u, :], ft[:, 1, u, :])
                last.then_inc(f_stats, 1)
                dve.wait_ge(f_stats, i * 2 + (q + 1))
                dve.wait_ge(f_rstd, i * 2 + q)
                dve.sem_inc(go_aggr, 1)
                for u in range(n):
                    last = dve.bn_aggr(mv[:, u, :], bst[:, u, :])
                last.then_inc(f_aggr, 1)
                dve.wait_ge(f_aggr, i * 2 + (q + 1))
                for u in range(n):
                    last = dve.scalar_tensor_tensor(out=nrm[:, u, :], in0=ft[:, 1, u, :], scalar=mv[:, u, 0:1],
                                                    in1=scale_b[:, :], op0=ALU.subtract, op1=ALU.mult)
                last.then_inc(f_q, 1)
                dve.wait_ge(f_rstd, i * 2 + (q + 1))
                dve.wait_ge(f_q, i * 2 + (q + 1))
                dve.wait_ge(f_stored[q], i * 16)
                for u in range(n):
                    last = dve.scalar_tensor_tensor(out=ft[:, 2 + q, u, :], in0=nrm[:, u, :], scalar=rstd[:, u:u + 1],
                                                    in1=x_tile(i * 4 + (2 * q + u)), op0=ALU.mult, op1=ALU.add)
                last.then_inc(f_out, 1)

            dve.wait_ge(s_off, NT)
            dve.wait_ge(s_sidx, NG)
            prior_sum = m_sb[:, 0:4, :].rearrange("p a e -> p (a e)").rearrange("p (u d) -> p u d", u=2)
            total_sb = m_sb[:, 4:8, :].rearrange("p a e -> p (a e)").rearrange("p (u d) -> p u d", u=2)
            nrm = prior[:, 0:4, :].rearrange("p a e -> p (a e)").rearrange("p (u d) -> p u d", u=2)
            total(0, 0, 2)
            with dve.Fori(0, NF - 1) as i:
                total(i, 1, 2)
                finish(i, 0, 2)
                total(i + 1, 0, 2)
                finish(i, 1, 2)
            total(NF - 1, 1, 2)
            finish(NF - 1, 0, 2)
            total(NF, 0, 1)
            finish(NF - 1, 1, 2)
            finish(NF, 0, 1)

        @block.tensor
        def _(pe):
            pe.wait_ge(s_const, 1)
            pe.wait_ge(s_wrel, 32)
            for r in range(2):
                for k in range(KD):
                    for c in range(KD):
                        last = pe.transpose(bank[4 + r][:, k * D + c * P:k * D + (c + 1) * P],
                                            rel_raw[:, r, c, k * P:(k + 1) * P], ident[:, :])
                last.then_inc(s_relps, 1)
            pe.wait_ge(s_bias, 16 * 7)
            pe.transpose(bank[6][:, 0:NB], bias_rows[:, :], ident[0:NB, 0:NB]).then_inc(s_relps, 1)

            def turn(t):
                pe.wait_ge(s_hrow, t + 1)
                pe.wait_ge(s_hT, t)
                for k in range(KD):
                    last = pe.transpose(bank[0][:, k * P:(k + 1) * P], hrow[:, k * P:(k + 1) * P], ident[:, :])
                last.then_inc(s_tr, 1)

            def product1(t, r):
                pe.wait_ge(s_hT, t + 1)
                pe.wait_ge(s_mid, t * 2)
                for o in range(KD):
                    for k in range(KD):
                        last = pe.matmul(bank[2 + r][:, o * P:(o + 1) * P], relT[:, r, k, o * P:(o + 1) * P],
                                         hT[:, k, :], start=(k == 0), stop=(k == KD - 1))
                last.then_inc(s_a, 1)

            def product2(t, r):
                pe.wait_ge(s_mid, t * 2 + (r + 1))
                pe.wait_ge(s_ysum, t * 2)
                for k in range(KD):
                    last = pe.matmul(bank[4 + r][:, 0:D], midT[:, r, k, :], relT[:, r, k, :], start=(k == 0), stop=(k == KD - 1))
                last.then_inc(s_b, 1)

            turn(0)

            pe.wait_ge(s_relT, 3)
            pe.wait_ge(s_ef, 1)
            for n in range(4):
                if n == 3:
                    pe.wait_ge(s_eT, 1)
                a = e_f[:, n] if n < 3 else e_w
                for c in range(EC):
                    rows = P if c < EC - 1 else RT
                    last = pe.transpose(bank[(6, 7, 1, 6)[n]][:, c * P:c * P + rows], a[0:rows, c, :], ident[0:rows, 0:rows])
                last.then_inc(s_eps_ps, 1)
            pe.wait_ge(s_eT, 4)
            pe.matmul(bank[7][:, 0:NG], row0[:, :], dstT[:, 0:ET:GROUP], start=True, stop=True).then_inc(s_base_ps, 1)
            pe.wait_ge(s_viol, 1)
            pe.matmul(bank[7][0:1, P:P + 1], chk[:, 3:4], ones[:, 0:1], start=True, stop=True).then_inc(s_viol, 1)
            pe.wait_ge(s_wts, 16 * N_WTS)
            for c in range(KD):
                last = pe.transpose(bank[6][:, c * P:(c + 1) * P], w3_raw[:, c, :], ident[:, :])
            last.then_inc(s_wps, 1)
            for k in range(KD):
                last = pe.transpose(bank[1][:, k * P:(k + 1) * P], w1_raw[:, k * P:(k + 1) * P], ident[:, :])
            last.then_inc(s_wps, 1)
            pe.wait_ge(s_wT, 2)
            pe.transpose(bank[1][:, D:D + P], w2_raw[:, :], ident[:, :]).then_inc(s_wps, 1)
            pe.wait_ge(s_ctrl, 2)
            for n in range(3):
                if n == 2:
                    pe.wait_ge(s_wT, 4)
                for c in range(2):
                    for k in range(KD):
                        last = pe.transpose(bank[(6, 7, 6)[n]][:, (2 * c + k) * P:(2 * c + k + 1) * P],
                                            ih_raw[:, 2 * n + c, k * P:(k + 1) * P], ident[:, :])
                last.then_inc(s_wps, 1)

            def table_tile(t, last):
                product1(t, 0)
                product1(t, 1)
                if not last:
                    turn(t + 1)
                product2(t, 0)
                product2(t, 1)

            with pe.Fori(0, NT - 1) as t:
                table_tile(t, False)
            table_tile(NT - 1, True)
            pe.wait_ge(s_ysum, 2 * NT)
            pe.wait_ge(s_wT, 6)
            pe.sem_inc(s_summed, 2)

            def sum_window(b, parts, signal):
                for k, j0, j1 in parts:
                    for j in range(j0, j1):
                        last = pe.matmul(bank[b][:, k * P:(k + 1) * P], msgs[:, b, j, k * P:(k + 1) * P], oh[:, b, j, :],
                                         start=(j == 0), stop=(j == GROUP - 1))
                if signal is not None:
                    last.then_inc(signal, 1)

            def ready(i, b):
                pe.wait_ge(s_oh, i * 2 + (b + 1))
                pe.wait_ge(s_gathered[b], i * (16 * GROUP) + 16 * GROUP)
                pe.wait_ge(s_added, i * 2 + (b + 1))

            def gates(w):
                pe.wait_ge(s_tg, w)
                for c in range(6):
                    for k in range(KD):
                        last = pe.matmul(bank[2 + c // 4][:, (c % 4) * P:(c % 4 + 1) * P], ihT[:, c, k, :],
                                         aggT[:, k, bass.ds(w * P, P)], start=(k == 0), stop=(k == KD - 1))
                last.then_inc(s_gates, 1)

            def mlp1(w):
                pe.wait_ge(s_hn, w + 1)
                pe.wait_ge(s_x1, w)
                for k in range(KD):
                    last = pe.matmul(bank[4][:, 0:P], w1T[:, k, :], hn[:, k, :], start=(k == 0), stop=(k == KD - 1))
                last.then_inc(s_w1, 1)

            def mlp2(w):
                pe.wait_ge(s_x1, w + 1)
                pe.wait_ge(s_x2, w)
                pe.matmul(bank[4][:, P:2 * P], w2T[:, :], x1T[:, :], start=True, stop=True).then_inc(s_w2, 1)

            def mlp3(w):
                pe.wait_ge(s_x2, w + 1)
                pe.wait_ge(s_xr, w)
                pe.matmul(bank[5][:, 0:D], ones[0:1, :], b3_row[:, :], start=True, stop=False)
                pe.matmul(bank[5][:, 0:D], x2T[:, :], w3T[:, :], start=False, stop=True).then_inc(s_w3, 1)

            def node_tile(w):
                gates(w)
                mlp1(w)
                mlp2(w)
                mlp3(w)

            def source_rows(i, b):
                pe.wait_ge(s_scol, i * 2 + (b + 1))
                pe.wait_ge(s_same, i * 2 + b)
                for j in range(GROUP):
                    last = pe.transpose(bank[j // 4][:, (j % 4) * P:(j % 4 + 1) * P],
                                        scol[:, j:j + 1].to_broadcast([P, P]), ident[:, :])
                last.then_inc(s_srow, 1)

            def rows_out(i, b, lhs, rhs):
                pe.wait_ge(s_combsb, i * 2 + b)
                for j in range(GROUP):
                    last = pe.matmul(bank[4 + j // 2][:, (j % 2) * D:(j % 2 + 1) * D], lhs(j), rhs(j), start=True, stop=True)
                last.then_inc(s_comb, 1)

            flag = flag_of(pe)
            with pe.If(flag < 1):
                half0, half1 = (0, 0, GROUP), (1, 0, GROUP)

                def both(i):
                    for b in range(2):
                        ready(i, b)
                        sum_window(b, (half0, half1), s_summed)

                for i in range(LAG):
                    both(i)
                with pe.Fori(LAG, NPAIR) as i:
                    w = i - LAG
                    pe.wait_ge(s_added, i * 2 + 2)
                    gates(w)
                    ready(i, 0)
                    sum_window(0, (half0, half1), s_summed)
                    mlp1(w)
                    ready(i, 1)
                    sum_window(1, (half0,), None)
                    mlp2(w)
                    sum_window(1, (half1,), s_summed)
                    mlp3(w)
                pe.wait_ge(s_added, NG + 2)
                for w in range(NPAIR - LAG, NT):
                    node_tile(w)
                pe.sem_inc(s_comb, 2)
                pe.wait_ge(s_xr, NT)
                with pe.Fori(0, NPAIR) as i:
                    for b in range(2):
                        source_rows(i, b)
                        pe.wait_ge(s_same, i * 2 + (b + 1))
                        pe.wait_ge(s_ohw, i * 2 + (b + 1))
                        pe.wait_ge(s_mcopied, i * 2 + b)
                        for j in range(GROUP):
                            last = pe.matmul(bank[2 + j // 4][:, (j % 4) * P:(j % 4 + 1) * P], ohw[:, j, :], same[:, j, :],
                                             start=True, stop=True)
                        last.then_inc(s_m, 1)
                        pe.wait_ge(s_mcopied, i * 2 + (b + 1))
                        pe.wait_ge(s_hwin[b], i * 16 + 16)
                        rows_out(i, b, lambda j: m_sb[:, j, :], lambda j: hwin[:, b, :])
            with pe.Else():
                with pe.Fori(0, NG) as g:
                    pe.wait_ge(g_gathered, g * (16 * GROUP) + 16 * GROUP)
                    pe.sem_inc(go_windows, 1)
                    with pe.Fori(0, NT) as w:
                        pe.wait_ge(g_oh, g * NT + w + 1)
                        pe.wait_ge(g_added, g * NT + w)
                        sum_window(0, ((0, 0, GROUP), (1, 0, GROUP)), g_summed)
                pe.wait_ge(g_added, NG * NT)
                with pe.Fori(0, NT) as w:
                    node_tile(w)
                pe.sem_inc(s_comb, 2)
                pe.wait_ge(s_xr, NT)
                with pe.Fori(0, NPAIR) as i:
                    for b in range(2):
                        source_rows(i, b)
                        pe.wait_ge(s_ohw, i * 2 + (b + 1))
                        pe.wait_ge(g_gathered2, i * (32 * GROUP) + 16 * GROUP * (b + 1))
                        rows_out(i, b, lambda j: ohw[:, j, :], lambda j: msgs[:, 1, j, :])
            pe.nop()

            total_v = m_sb[:, 4:8, :].rearrange("p a e -> p (a e)").rearrange("p (u d) -> p u d", u=2)
            aT = fsum[:, 0, :, :].rearrange("p u d -> p (u d)")
            gT = fsum[:, 1, :, :].rearrange("p u d -> p (u d)")

            def turn_sums(i, q, n):
                pe.wait_ge(f_sum, i * 2 + (q + 3))
                pe.wait_ge(f_aT, i * 2 + q)
                for k in range(KD):
                    for u in range(n):
                        last = pe.transpose(bank[0][:, (k * n + u) * P:(k * n + u + 1) * P], total_v[:, u, k * P:(k + 1) * P], ident[:, :])
                last.then_inc(f_tr, 1)

            def mlp_in(i, q, n):
                pe.wait_ge(f_aT, i * 2 + (q + 1))
                pe.wait_ge(f_h, i * 2 + q)
                for o in range(KD):
                    for k in range(KD):
                        last = pe.matmul(bank[2][:, o * n * P:(o + 1) * n * P], gw1[:, k, o * P:(o + 1) * P],
                                         aT[:, k * n * P:(k + 1) * n * P], start=(k == 0), stop=(k == KD - 1))
                last.then_inc(f_a, 1)

            def mlp_out(i, q, n):
                pe.wait_ge(f_h, i * 2 + (q + 1))
                pe.wait_ge(f_t, i * 2 + q)
                for u in range(n):
                    for k in range(KD):
                        last = pe.matmul(bank[4][:, u * D:(u + 1) * D], gT[:, (k * n + u) * P:(k * n + u + 1) * P],
                                         gw2[:, k, :], start=(k == 0), stop=(k == KD - 1))
                last.then_inc(f_b, 1)

            pe.wait_ge(s_combsb, NG)
            turn_sums(0, 0, 2)
            with pe.Fori(0, NF - 1) as i:
                mlp_in(i, 0, 2)
                turn_sums(i, 1, 2)
                mlp_out(i, 0, 2)
                mlp_in(i, 1, 2)
                turn_sums(i + 1, 0, 2)
                mlp_out(i, 1, 2)
            mlp_in(NF - 1, 0, 2)
            turn_sums(NF - 1, 1, 2)
            mlp_out(NF - 1, 0, 2)
            mlp_in(NF - 1, 1, 2)
            turn_sums(NF, 0, 1)
            mlp_out(NF - 1, 1, 2)
            mlp_in(NF, 0, 1)
            mlp_out(NF, 0, 1)


N_WTS = 12

_INS = ['x', 'src', 'dst', 'edge_type_2', 'edge_weight', 'L0_gnn_W_rel', 'L0_gnn_b_rel', 'L0_gnn_W_ih', 'L0_gnn_b_ih',
        'L0_gnn_b_hh', 'L0_gnn_W1', 'L0_gnn_b1', 'L0_gnn_W2', 'L0_gnn_b2', 'L0_gnn_W3', 'L0_gnn_b3', 'L1_gnn_W1',
        'L1_gnn_b1', 'L1_gnn_W2', 'L1_gnn_b2', 'L1_gnn_eps', 'L1_gnn_offset', 'L1_gnn_scale']


def kernel(**inputs):
    import numpy as _np
    import concourse.bacc as _bacc
    from concourse import mybir as _mybir
    from concourse.bass_utils import run_bass_kernel_spmd as _run

    nc = _bacc.Bacc("TRN2", target_bir_lowering=False, num_devices=1)
    arrays, args = {}, []
    for name in _INS:
        a = _np.ascontiguousarray(inputs[name])
        arrays[f"in_{name}_dram"] = a
        args.append(nc.dram_tensor(f"in_{name}_dram", a.shape, _mybir.dt.from_np(a.dtype), kind="ExternalInput").ap())
    shape = inputs['x'].shape
    args.append(nc.dram_tensor("out_0_dram", shape, _mybir.dt.float32, kind="ExternalOutput").ap())
    gnn_kernel(nc, *args)
    r = _run(nc, [arrays], core_ids=[0])
    return r.results[0]["out_0_dram"]
```

```python
from contextlib import ExitStack

import concourse.bass as bass
from concourse import mybir

P = 128
F32 = mybir.dt.float32
I32 = mybir.dt.int32
ALU = mybir.AluOpType
ACT = mybir.ActivationFunctionType
AX = mybir.AxisListType

GROUP = 8
ACCS = 4
LAG = 3


def gnn_kernel(nc, x, src, dst, edge_type_2, edge_weight, W_rel, b_rel, W_ih, b_ih, b_hh, W1, b1, W2, b2,
               W3, b3, G_W1, G_b1, G_W2, G_b2, G_eps, G_offset, G_scale, out):
    NODES, D = x.shape
    EDGES = src.shape[0]
    NT = -(-NODES // P)
    LAST = NODES - (NT - 1) * P
    ET = -(-EDGES // P)
    NG = ET // GROUP
    NPAIR = NG // 2
    ROWS = NT * P + P
    KD = D // P
    assert D == 256 and NG * GROUP == ET and NG % 2 == 0 and ET <= 512 and NPAIR == NT + 1
    assert ROWS == 26 * P and b1.shape[0] == P
    EC = -(-ET // P)
    FULL = (EC - 1) * P
    RT = ET - FULL
    PART = EDGES - (ET - 1) * P
    ZROW = 2 * NODES
    FLAG = NG

    ctx = ExitStack()
    with ctx:
        def sb(name, shape, dt=F32):
            return ctx.enter_context(nc.sbuf_tensor(name, shape, dt))

        def sem(name):
            return ctx.enter_context(nc.semaphore(name))

        msg_table = nc.dram_tensor("msg_table", [2 * NODES + 1, D], F32).ap()
        g_table = nc.dram_tensor("g_table", [ROWS, D], F32).ap()
        acc = [nc.dram_tensor(f"acc{k}", [ROWS, D], F32).ap() for k in range(ACCS)]

        ident = sb("ident", [P, P])
        iota_row = sb("iota_row", [P, P])
        earlier = sb("earlier", [P, P])
        row0 = sb("row0", [P, P])
        spare = sb("spare", [P, 1])
        wbase = sb("wbase", [P, NT])
        ones = sb("ones", [P, P])
        minus_half = sb("minus_half", [P, 2])
        minus_one = sb("minus_one", [P, 1])
        ln_eps = sb("ln_eps", [P, 1])
        zeros = sb("zeros", [P, D])
        rel_raw = sb("rel_raw", [P, 2, KD, D])
        relT = sb("relT", [P, 2, KD, D])
        ih_raw = sb("ih_raw", [P, 6, D])
        ihT = sb("ihT", [P, 6, KD, P])
        w1_raw = sb("w1_raw", [P, D])
        w2_raw = sb("w2_raw", [P, P])
        w3_raw = sb("w3_raw", [P, KD, P])
        w1T = sb("w1T", [P, KD, P])
        w2T = sb("w2T", [P, P])
        w3T = sb("w3T", [P, D])
        gw1 = sb("gw1", [P, KD, D])
        gw2 = sb("gw2", [P, KD, D])
        NB = 22
        bias_rows = sb("bias_rows", [NB, P])
        bias = sb("bias", [P, NB])
        gate_bias = sb("gate_bias", [P, 8])
        gate_half = sb("gate_half", [P, 8])
        brel_b = sb("brel_b", [P, 2, D])
        b3_row = sb("b3_row", [1, D])
        b2_row = sb("b2_row", [1, D])
        gb1_b = sb("gb1_b", [P, D])
        scale_b = sb("scale_b", [P, D])
        offset_b = sb("offset_b", [P, D])
        eps_b = sb("eps_b", [P, 1])
        xr = sb("xr", [P, NT, D])
        aggT = sb("aggT", [P, KD, ROWS])
        e_int = sb("e_int", [P, 3, EC, P], I32)
        e_w = sb("e_w", [P, EC, P])
        e_f = sb("e_f", [P, 3, EC, P])
        srcT = sb("srcT", [P, ET])
        dstT = sb("dstT", [P, ET])
        typT = sb("typT", [P, ET])
        wT = sb("wT", [P, ET])
        loc = sb("loc", [P, NG, GROUP])
        base_f = sb("base_f", [P, NG])
        to_spare = sb("to_spare", [P, ET])
        isr = sb("isr", [P, 2, ET])
        gidx = sb("gidx", [P, ET], I32)
        dst_i = sb("dst_i", [P, ET], I32)
        ctrl = sb("ctrl", [1, NG + 8], I32)
        chk = sb("chk", [P, 8])
        chk_row = sb("chk_row", [1, 4, NG])
        bst0 = sb("bst0", [P, 6])
        mv_of = sb("mv_of", [P, 2])
        mv0 = sb("mv0", [P, NT, 2])
        veps0 = sb("veps0", [P, NT])
        mrs0 = sb("mrs0", [P, NT])
        rstd0 = sb("rstd0", [P, NT])
        nbias0 = sb("nbias0", [P, NT])
        bst = sb("bst", [P, 2, 6])
        mv = sb("mv", [P, 2, 2])
        veps = sb("veps", [P, 2])
        rstd = sb("rstd", [P, 2])
        nbias = sb("nbias", [P, 2])
        mrs = sb("mrs", [P, 2])
        hrow = sb("hrow", [P, D])
        hT = sb("hT", [P, KD, P])
        midT = sb("midT", [P, 2, KD, P])
        ysum = sb("ysum", [P, 2, D])
        yrow = sb("yrow", [P, 2, D])
        ix = sb("ix", [P, 2, GROUP], I32)
        msgs = sb("msgs", [P, 2, GROUP, D])
        oh = sb("oh", [P, 2, GROUP, P])
        tg = sb("tg", [P, 6, P])
        cell = sb("cell", [P, 2, P])
        tcell = sb("tcell", [P, 2, P])
        hn = sb("hn", [P, 2, P])
        x1T = sb("x1T", [P, P])
        x2T = sb("x2T", [P, P])
        grow = sb("grow", [P, D])
        gsc = sb("gsc", [P, D])
        onep = sb("onep", [P, 1])
        wloc = sb("wloc", [P, GROUP])
        scol = sb("scol", [P, 2, GROUP])
        same = sb("same", [P, 2, GROUP, P])
        ohw = oh
        prior = sb("prior", [P, GROUP, P])
        dup = sb("dup", [P, GROUP])
        sidx_f = sb("sidx_f", [P, GROUP])
        sidx = sb("sidx", [P, ET], I32)
        sx = sb("sx", [P, 2, GROUP], I32)
        m_sb = sb("m_sb", [P, 2, GROUP, P])
        hwin = sb("hwin", [P, 2, D])
        comb = sb("comb", [P, 2, GROUP, D])
        fa = [msgs[:, q].rearrange("p (k u) d -> p k u d", k=ACCS) for q in range(2)]
        def pair_of(buffer, slot):
            return buffer.rearrange("p a b -> p (a b)")[:, slot * 2 * D:(slot + 1) * 2 * D].rearrange("p (u d) -> p u d", u=2)

        f_s01 = pair_of(comb[:, 0], 0)
        f_s23 = [pair_of(comb[:, 0], 1 + q) for q in range(2)]
        f_tot = [pair_of(comb[:, 1], q) for q in range(2)]
        f_rT = [pair_of(comb[:, 1], 2 + q) for q in range(2)]
        f_r = [pair_of(oh[:, 0], q) for q in range(2)]
        f_n = pair_of(oh[:, 1], 0)
        f_q = [pair_of(same[:, 0], q) for q in range(2)]
        f_o = [pair_of(same[:, 1], q) for q in range(2)]

        bank = [ctx.enter_context(nc.psum_tensor(f"bank{i}", [P, 512], F32)) for i in range(8)]

        s_xin = [sem(f"s_xin{i}") for i in range(3)]
        s_edges = sem("s_edges"); s_wrel = sem("s_wrel"); s_bias = sem("s_bias"); s_wts = sem("s_wts")
        s_pad = sem("s_pad"); s_zero = sem("s_zero"); s_zrow = sem("s_zrow"); s_aggz = sem("s_aggz")
        s_const = sem("s_const"); s_const_step = sem("s_const_step")
        s_relps = sem("s_relps"); s_relT = sem("s_relT")
        s_ef = sem("s_ef"); s_eps_ps = sem("s_eps_ps"); s_eT = sem("s_eT")
        s_base_ps = sem("s_base_ps"); s_base = sem("s_base"); s_prep = sem("s_prep")
        s_viol = sem("s_viol"); s_ctrl = sem("s_ctrl"); s_gidx = sem("s_gidx")
        s_wps = sem("s_wps"); s_wT = sem("s_wT"); s_gb = sem("s_gb")
        s_stats0 = sem("s_stats0"); s_aggr0 = sem("s_aggr0"); s_veps0 = sem("s_veps0"); s_rstd0 = sem("s_rstd0")
        s_mv_of = sem("s_mv_of"); s_mrs0 = sem("s_mrs0"); s_nbias0 = sem("s_nbias0")
        s_stats = sem("s_stats"); s_aggr = sem("s_aggr"); s_veps = sem("s_veps"); s_rstd = sem("s_rstd"); s_nbias = sem("s_nbias")
        s_hrow = sem("s_hrow"); s_tr = sem("s_tr"); s_hT = sem("s_hT"); s_a = sem("s_a"); s_mid = sem("s_mid")
        s_b = sem("s_b"); s_ysum = sem("s_ysum"); s_yrow = sem("s_yrow")
        s_ystored = [sem(f"s_ystored{r}") for r in range(2)]
        s_staged = [sem(f"s_staged{b}") for b in range(2)]
        s_gathered = [sem(f"s_gathered{b}") for b in range(2)]
        s_oh = sem("s_oh"); s_summed = sem("s_summed"); s_added = sem("s_added")
        s_gates = sem("s_gates"); s_tg = sem("s_tg"); s_cell = sem("s_cell"); s_tcell = sem("s_tcell")
        s_hn = sem("s_hn"); s_w1 = sem("s_w1"); s_x1 = sem("s_x1"); s_w2 = sem("s_w2"); s_x2 = sem("s_x2")
        s_w3 = sem("s_w3"); s_xr = sem("s_xr"); s_hrow1 = sem("s_hrow1")
        s_tr1 = sem("s_tr1"); s_hT1 = sem("s_hT1"); s_g = sem("s_g"); s_grow = sem("s_grow"); s_gsc = sem("s_gsc")
        s_off = sem("s_off")
        s_gstored = sem("s_gstored"); s_acc0 = sem("s_acc0")
        g_staged = sem("g_staged"); g_gathered = sem("g_gathered"); g_loc = sem("g_loc"); g_oh = sem("g_oh")
        g_summed = sem("g_summed"); g_added = sem("g_added")
        s_scol = sem("s_scol"); s_srow = sem("s_srow"); s_same = sem("s_same"); s_eq = sem("s_eq")
        s_ohw = sem("s_ohw"); s_prior = sem("s_prior"); s_dup = sem("s_dup"); s_dupm = sem("s_dupm")
        s_sidx = sem("s_sidx"); s_m = sem("s_m"); s_mcopied = sem("s_mcopied"); s_comb = sem("s_comb")
        s_combsb = sem("s_combsb")
        s_hwin = [sem(f"s_hwin{b}") for b in range(2)]
        s_passed = sem("s_passed")
        s_scattered = [sem(f"s_scattered{k}") for k in range(ACCS)]
        s_sstaged = [sem(f"s_sstaged{b}") for b in range(2)]
        g_staged2 = sem("g_staged2"); g_gathered2 = sem("g_gathered2")
        f_loaded = [sem(f"f_loaded{q}") for q in range(2)]
        l_s23 = sem("l_s23"); l_s01 = sem("l_s01"); l_tot = sem("l_tot"); l_turned = sem("l_turned")
        l_rT = sem("l_rT"); l_prod = sem("l_prod"); l_r = sem("l_r"); l_stats = sem("l_stats")
        l_aggr = sem("l_aggr"); l_veps = sem("l_veps"); l_rstd = sem("l_rstd"); l_mrs = sem("l_mrs")
        l_nbias = sem("l_nbias"); l_n = sem("l_n"); l_q = sem("l_q"); l_out = sem("l_out")
        l_stored = [sem(f"l_stored{q}") for q in range(2)]
        go_aggr = sem("go_aggr"); go_scale = sem("go_scale"); go_gather = sem("go_gather")
        go_windows = sem("go_windows"); go_stage = sem("go_stage")

        block = ctx.enter_context(nc.Block())

        NPT = (NT + 1) // 2
        assert NT == 2 * NPT - 1 and NPT % 2 == 1
        X_LOADS = [(0, 3), (3, 10), (10, NT - 1)]
        LEAD = X_LOADS[0][1]
        MID = 8
        N_CLEARED = 16 * (NT * (ACCS - 1) + ACCS + 2)
        NSLOT = 7

        def flag_of(e):
            e.wait_ge(s_ctrl, 2)
            return e.value_load(ctrl[0:1, FLAG:FLAG + 1], min_val=0, max_val=1)

        @block.sync
        def _(sp):
            def load_x(n):
                a, b = X_LOADS[n]
                sp.dma_start(xr[:, a:b, :], x[a * P:b * P, :].rearrange("(t p) d -> p t d", p=P)).then_inc(s_xin[n], 16)

            load_x(0)
            for r in range(2):
                sp.dma_start(rel_raw[:, r], W_rel[r].rearrange("(c p) i -> p c i", p=P)).then_inc(s_wrel, 16)
            sp.wait_ge(s_bias, 16 * 6)
            load_x(1)
            load_x(2)
            sp.wait_ge(s_pad, 3)
            sp.dma_start(xr[0:LAST, NT - 1, :], x[(NT - 1) * P:NODES, :]).then_inc(s_xin[2], 16)
            for n, a in enumerate((src, dst, edge_type_2, edge_weight)):
                e, c = (e_int[:, n], None) if n < 3 else (e_w, None)
                sp.dma_start(e[:, 0:EC - 1, :], a[0:FULL * P].rearrange("(c p e) -> p c e", p=P, e=P)).then_inc(s_edges, 16)
                sp.dma_start(e[0:RT - 1, EC - 1, :], a[FULL * P:(ET - 1) * P].rearrange("(p e) -> p e", e=P)).then_inc(s_edges, 16)
                sp.dma_start(e[RT - 1:RT, EC - 1, 0:PART], a[(ET - 1) * P:EDGES].unsqueeze(0)).then_inc(s_edges, 16)
                if n < 2:
                    sp.dma_start(e[RT - 1:RT, EC - 1, PART:P], a[EDGES - (P - PART):EDGES].unsqueeze(0)).then_inc(s_edges, 16)
            loads = [(ih_raw[:, 0:2, :], W_ih[0:D, :].rearrange("(c p) i -> p c i", p=P)),
                     (ih_raw[:, 2:6, :], W_ih[2 * D:4 * D, :].rearrange("(c p) i -> p c i", p=P)),
                     (w1_raw[:, :], W1), (w2_raw[:, :], W2),
                     (w3_raw[:, :, :], W3.rearrange("(c p) i -> p c i", p=P)),
                     (gw1[:, :, :], G_W1.rearrange("(k p) o -> p k o", p=P)),
                     (gw2[:, :, :], G_W2.rearrange("(k p) o -> p k o", p=P)),
                     (b3_row[:, :], b3.unsqueeze(0)),
                     (b2_row[:, :], G_b2.unsqueeze(0)),
                     (gb1_b[:, :], G_b1.unsqueeze(0).to_broadcast([P, D])),
                     (scale_b[:, :], G_scale.unsqueeze(0).to_broadcast([P, D])),
                     (offset_b[:, :], G_offset.unsqueeze(0).to_broadcast([P, D])),
                     (eps_b[:, :], G_eps.unsqueeze(0).to_broadcast([P, 1]))]
            assert len(loads) == N_WTS
            sp.dma_start(msg_table[ZROW:ZROW + 1, :], zeros[0:1, :]).then_inc(s_zrow, 16)

            def store_messages(t, rows):
                for r in range(2):
                    sp.wait_ge(s_yrow, t * 2 + (r + 1))
                    sp.dma_start(msg_table[bass.ds(t * P + r * NODES, rows), :],
                                 yrow[0:rows, r, :]).then_inc(s_ystored[r], 16)

            for t in range(4):
                store_messages(t, P)
                for to, of in loads[t::4]:
                    sp.dma_start(to, of).then_inc(s_wts, 16)
            with sp.Fori(4, NT - 1) as t:
                store_messages(t, P)
            sp.wait_ge(s_gidx, 1)
            for b in range(2):
                sp.dma_start(ix[:, b, :], gidx[:, b * GROUP:(b + 1) * GROUP]).then_inc(s_staged[b], 16)
            store_messages(NT - 1, LAST)

            def store_g(w, rows):
                sp.wait_ge(s_grow, w + 1)
                sp.dma_start(g_table[bass.ds(w * P, P), :], grow[:, :]).then_inc(s_gstored, 16)
                sp.wait_ge(s_gsc, w + 1)
                sp.dma_start(acc[0][bass.ds(w * P, rows), :], gsc[0:rows, :]).then_inc(s_acc0, 16)

            def clear_rows(w):
                for k in range(1, ACCS):
                    sp.dma_start(acc[k][bass.ds(w * P, P), :], zeros[:, :]).then_inc(s_zero, 16)

            def clear_spare_rows():
                for to in [acc[k][NT * P:ROWS, :] for k in range(ACCS)] + [g_table[NT * P:ROWS, :]]:
                    sp.dma_start(to, zeros[:, :]).then_inc(s_zero, 16)
                sp.dma_start(acc[0][NODES:NT * P, :], zeros[0:NT * P - NODES, :]).then_inc(s_zero, 16)

            def stage_rows(i, b):
                sp.wait_ge(s_sidx, i * 2 + b + 1)
                sp.sem_inc(go_stage, 1)
                sp.wait_ge(s_passed, i * (2 * GROUP) + (b * GROUP + ACCS))
                sp.sem_inc(go_stage, 1)
                sp.dma_start(sx[:, b, :], sidx[:, bass.ds(i * (2 * GROUP) + b * GROUP, GROUP)]).then_inc(s_sstaged[b], 16)

            flag = flag_of(sp)
            with sp.If(flag < 1):
                def stage(i):
                    for b in range(2):
                        sp.wait_ge(s_gathered[b], i * (16 * GROUP))
                        sp.dma_start(ix[:, b, :], gidx[:, bass.ds(i * (2 * GROUP) + b * GROUP, GROUP)]).then_inc(s_staged[b], 16)

                with sp.Fori(0, LAG + 1) as i:
                    stage(i + 1)
                    clear_rows(i)
                with sp.Fori(LAG + 1, NPAIR - 1) as i:
                    stage(i + 1)
                    clear_rows(i)
                    store_g(i - (LAG + 1), P)
                clear_spare_rows()
                for w in range(NPAIR - LAG - 2, NT - 1):
                    store_g(w, P)
                store_g(NT - 1, LAST)
                sp.wait_ge(s_gstored, 16 * NT)
                sp.wait_ge(s_zero, N_CLEARED)
                def load_window(i, b):
                    base = sp.value_load(ctrl[0:1, bass.ds(i * 2 + b, 1)], min_val=0, max_val=NODES - 1)
                    sp.wait_ge(s_comb, i * 4 + (2 * b + 2))
                    sp.dma_start(hwin[:, b, :], g_table[bass.ds(base, P), :]).then_inc(s_hwin[b], 16)

                load_window(0, 0)
                with sp.Fori(0, NPAIR - 1) as i:
                    load_window(i, 1)
                    stage_rows(i, 0)
                    load_window(i + 1, 0)
                    stage_rows(i, 1)
                load_window(NPAIR - 1, 1)
                stage_rows(NPAIR - 1, 0)
                stage_rows(NPAIR - 1, 1)
            with sp.Else():
                with sp.Fori(0, NT) as w:
                    clear_rows(w)
                clear_spare_rows()
                sp.wait_ge(s_staged[0], 16)
                with sp.Fori(0, NG) as g:
                    sp.wait_ge(g_gathered, g * (16 * GROUP))
                    sp.dma_start(ix[:, 0, :], gidx[:, bass.ds(g * GROUP, GROUP)]).then_inc(g_staged, 16)
                sp.wait_ge(s_zero, N_CLEARED)
                with sp.Fori(0, NT - 1) as w:
                    store_g(w, P)
                store_g(NT - 1, LAST)
                sp.wait_ge(s_gstored, 16 * NT)
                with sp.Fori(0, NPAIR) as i:
                    for b in range(2):
                        sp.wait_ge(g_gathered2, i * (32 * GROUP) + b * (16 * GROUP))
                        sp.dma_start(ix[:, 1, :], dst_i[:, bass.ds(i * (2 * GROUP) + b * GROUP, GROUP)]).then_inc(g_staged2, 16)
                        stage_rows(i, b)
            for k in range(ACCS):
                sp.wait_ge(s_scattered[k], 16 * (ET // ACCS))

            def load_sums(p, q, n):
                sp.wait_ge(l_tot, p + 1)
                for k in range(ACCS):
                    sp.dma_start(fa[q][:, k, 0:n, :],
                                 acc[k][bass.ds(p * (2 * P), n * P), :].rearrange("(u p) d -> p u d", p=P)).then_inc(f_loaded[q], 16)

            def store_out(p, q):
                sp.wait_ge(l_out, p + 2)
                sp.dma_start(out[bass.ds(p * (2 * P), 2 * P), :].rearrange("(u p) d -> p u d", p=P), f_o[q]).then_inc(l_stored[q], 16)

            load_sums(0, 0, 2)
            load_sums(1, 1, 2)
            load_sums(2, 0, 2)
            load_sums(3, 1, 2)
            load_sums(4, 0, 2)
            load_sums(5, 1, 2)
            with sp.Fori(0, NPT // 2 - 3) as i:
                for q in range(2):
                    store_out(i * 2 + q, q)
                    load_sums(i * 2 + (q + 6), q, 2)
            store_out(NPT - 7, 0)
            load_sums(NPT - 1, 0, 1)
            for p in range(NPT - 6, NPT - 1):
                store_out(p, p % 2)
            sp.wait_ge(l_out, NPT + 1)
            sp.dma_start(out[(NT - 1) * P:NODES, :], f_o[0][0:LAST, 0, :]).then_inc(l_stored[0], 16)
            sp.wait_ge(l_stored[0], 16 * (NPT // 2 + 1))
            sp.wait_ge(l_stored[1], 16 * (NPT // 2))

        @block.gpsimd
        def _(pool):
            pool.memset(zeros[:, :], 0.0)
            pool.memset(e_int[0:RT, 2, EC - 1, :], 2).then_inc(s_pad, 1)
            pool.memset(e_w[0:RT, EC - 1, :], 0.0).then_inc(s_pad, 1)
            pool.memset(xr[:, NT - 1, :], 0.0).then_inc(s_pad, 1)
            pool.memset(ident[:, :], 0.0)
            pool.memset(row0[:, :], 0.0)
            pool.memset(earlier[:, :], 1.0)
            pool.memset(ones[:, :], 1.0)
            pool.memset(minus_half[:, :], -0.5)
            pool.memset(minus_one[:, :], -1.0)
            pool.memset(ln_eps[:, :], 1e-5)
            pool.iota(iota_row[:, :], [[1, P]], base=0, channel_multiplier=0, allow_small_or_imprecise_dtypes=True)
            pool.iota(wbase[:, :], [[P, NT]], base=0, channel_multiplier=0, allow_small_or_imprecise_dtypes=True)
            pool.iota(spare[:, :], [[1, 1]], base=NODES, channel_multiplier=1,
                      allow_small_or_imprecise_dtypes=True).then_inc(s_const_step, 1)
            pool.wait_ge(s_const_step, 1)
            pool.affine_select(out=ident[:, :], in_=ident[:, :], compare_op=ALU.not_equal, fill=1.0, base=0,
                               pattern=[[-1, P]], channel_multiplier=1)
            pool.affine_select(out=row0[:, :], in_=row0[:, :], compare_op=ALU.not_equal, fill=1.0, base=0,
                               pattern=[[0, P]], channel_multiplier=1)
            pool.affine_select(out=earlier[:, :], in_=earlier[:, :], compare_op=ALU.is_gt, fill=0.0, base=0,
                               pattern=[[-1, P]], channel_multiplier=1).then_inc(s_const, 1)

            def scale_bias0(t):
                col = bass.ds(t, 1)
                pool.wait_ge(s_aggr0, t + 1)
                pool.tensor_tensor(veps0[:, col], mv0[:, col, 1:2].rearrange("p t a -> p (t a)"), ln_eps[:, :], ALU.add).then_inc(s_veps0, 1)
                pool.wait_ge(s_veps0, t + 1)
                pool.tensor_tensor(rstd0[:, col], veps0[:, col], minus_half[:, 0:1], ALU.pow).then_inc(s_rstd0, 1)
                pool.wait_ge(s_rstd0, t + 1)
                pool.tensor_tensor(mrs0[:, col], mv0[:, col, 0:1].rearrange("p t a -> p (t a)"), rstd0[:, col], ALU.mult).then_inc(s_mrs0, 1)
                pool.wait_ge(s_mrs0, t + 1)
                pool.tensor_tensor(nbias0[:, col], mrs0[:, col], minus_one[:, :], ALU.mult).then_inc(s_nbias0, 1)

            with pool.Fori(0, LEAD + 2) as t:
                scale_bias0(t)
            pool.wait_ge(s_edges, 16 * 14)
            for n in range(3):
                pool.tensor_copy(e_f[:, n, 0:EC - 1, :], e_int[:, n, 0:EC - 1, :])
                pool.tensor_copy(e_f[0:RT, n, EC - 1, :], e_int[0:RT, n, EC - 1, :]).then_inc(s_ef, 1)
                scale_bias0(LEAD + 2 + n)
            assert MID == LEAD + 5
            for k in range(KD):
                pool.memset(aggT[:, k, :], 0.0).then_inc(s_aggz, 1)
                scale_bias0(MID + k)
            with pool.Fori(MID + KD, NT) as t:
                scale_bias0(t)
            pool.sem_inc(s_passed, GROUP)

            def gather(table, index, b, signal, j0=0, j1=GROUP):
                for j in range(j0, j1):
                    pool.indirect_dma_start(msgs[:, b, j, :], None, table,
                                            bass.IndirectOffsetOnAxis(ap=ix[:, index, j:j + 1], axis=0)).then_inc(signal, 16)

            def scatter(i, b):
                pool.wait_ge(s_sstaged[b], i * 16 + 16)
                for j in range(GROUP):
                    k = j % ACCS
                    if j % (GROUP // 2) == 0:
                        pool.wait_ge(s_combsb, i * 4 + (2 * b + j // (GROUP // 2) + 3))
                    if k == 0:
                        pool.wait_ge(s_acc0, 16 * NT)
                    pool.wait_ge(s_scattered[k], i * 64 + (32 * b + 16 * (j // ACCS)))
                    pool.sem_inc(s_passed, 1)
                    pool.indirect_dma_start(acc[k], bass.IndirectOffsetOnAxis(ap=sx[:, b, j:j + 1], axis=0),
                                            comb[:, b, j, :], None, compute_op=ALU.add).then_inc(s_scattered[k], 16)

            def scale_bias(n, which):
                pool.wait_ge(s_aggr, n + 1)
                pool.sem_inc(go_scale, 1)
                pool.tensor_scalar(veps[:, which:which + 1], mv[:, which, 1:2], 1e-5, None, ALU.add).then_inc(s_veps, 1)
                pool.wait_ge(s_veps, n + 1)
                pool.tensor_tensor(rstd[:, which:which + 1], veps[:, which:which + 1], minus_half[:, 0:1], ALU.pow).then_inc(s_rstd, 1)
                pool.wait_ge(s_rstd, n + 1)
                pool.sem_inc(go_scale, 1)
                pool.tensor_scalar(nbias[:, which:which + 1], mv[:, which, 0:1], rstd[:, which:which + 1], -1.0,
                                   ALU.mult, ALU.mult).then_inc(s_nbias, 1)

            for r in range(2):
                pool.wait_ge(s_ystored[r], 16 * NT)
            pool.wait_ge(s_zrow, 16)
            flag = flag_of(pool)
            with pool.If(flag < 1):
                def gather_pair(i, v):
                    for b in range(2):
                        pool.wait_ge(s_staged[b], i * 16 + 16)
                        pool.wait_ge(s_summed, i * 2 + b + 1)
                        pool.sem_inc(go_gather, 1)
                        gather(msg_table, b, b, s_gathered[b], 0, GROUP // 2)
                        if b == 1 and v is not None:
                            scale_bias(v, 1)
                        gather(msg_table, b, b, s_gathered[b], GROUP // 2, GROUP)

                for i in range(LAG + 1):
                    gather_pair(i, None)
                with pool.Fori(LAG + 1, NPAIR) as i:
                    gather_pair(i, i - (LAG + 1))
                for w in range(NPAIR - LAG - 1, NT):
                    scale_bias(w, 1)
                with pool.Fori(0, NPAIR) as i:
                    scatter(i, 0)
                    scatter(i, 1)
            with pool.Else():
                with pool.Fori(0, NG) as g:
                    pool.wait_ge(g_staged, g * 16 + 16)
                    pool.wait_ge(g_summed, g * NT)
                    pool.sem_inc(go_gather, 1)
                    gather(msg_table, 0, 0, g_gathered)
                with pool.Fori(0, NT) as w:
                    scale_bias(w, 1)
                with pool.Fori(0, NPAIR) as i:
                    for b in range(2):
                        pool.wait_ge(s_gstored, 16 * NT)
                        pool.wait_ge(g_staged2, i * 32 + (16 * b + 16))
                        pool.wait_ge(s_comb, i * 4 + (2 * b + 4))
                        pool.sem_inc(go_gather, 1)
                        gather(g_table, 1, 1, g_gathered2)
                        scatter(i, b)
            pool.nop()

            def sum23(p, q, n):
                pool.wait_ge(f_loaded[q], (p - q) * (8 * ACCS) + 16 * ACCS)
                pool.wait_ge(l_tot, p + 1)
                pool.tensor_tensor(f_s23[q][:, 0:n, :], fa[q][:, 2, 0:n, :], fa[q][:, 3, 0:n, :], ALU.add).then_inc(l_s23, 1)

            def row_scale(p, q, n):
                pool.wait_ge(l_n, p)
                pool.wait_ge(l_aggr, p + 1)
                pool.sem_inc(go_scale, 1)
                mean, var = (mv[:, 0:n, c:c + 1].rearrange("p t a -> p (t a)") for c in range(2))
                pool.tensor_scalar(veps[:, 0:n], var, 1e-10, None, ALU.add).then_inc(l_veps, 1)
                pool.wait_ge(l_veps, p + 1)
                pool.tensor_tensor(rstd[:, 0:n], veps[:, 0:n], minus_half[:, 0:n], ALU.pow).then_inc(l_rstd, 1)
                pool.wait_ge(l_rstd, p + 1)
                pool.tensor_tensor(mrs[:, 0:n], mean, rstd[:, 0:n], ALU.mult).then_inc(l_mrs, 1)
                pool.wait_ge(l_mrs, p + 1)
                pool.sem_inc(go_scale, 1)
                pool.tensor_scalar(nbias[:, 0:n], mrs[:, 0:n], -1.0, None, ALU.mult).then_inc(l_nbias, 1)

            def times_scale(p, q, n):
                pool.wait_ge(l_n, p + 1)
                pool.wait_ge(l_out, p)
                pool.tensor_tensor(f_q[q][:, 0:n, :], f_n[:, 0:n, :], scale_b[:, :].unsqueeze(1).to_broadcast([P, n, D]),
                                   ALU.mult).then_inc(l_q, 1)

            sum23(0, 0, 2)
            sum23(1, 1, 2)
            with pool.Fori(0, NPT // 2 - 1) as i:
                for q in range(2):
                    sum23(i * 2 + (q + 2), q, 2)
                    row_scale(i * 2 + q, q, 2)
                    times_scale(i * 2 + q, q, 2)
            sum23(NPT - 1, 0, 1)
            row_scale(NPT - 3, 0, 2)
            times_scale(NPT - 3, 0, 2)
            row_scale(NPT - 2, 1, 2)
            times_scale(NPT - 2, 1, 2)
            row_scale(NPT - 1, 0, 1)
            times_scale(NPT - 1, 0, 1)

        @block.scalar
        def _(act):
            act.dma_start(bias_rows[0:4, :], b_rel.rearrange("r (k p) -> (r k) p", p=P)).then_inc(s_bias, 16)
            act.dma_start(brel_b[:, :, :], b_rel.unsqueeze(0).to_broadcast([P, 2, D])).then_inc(s_bias, 16)
            act.dma_start(bias_rows[4:12, :], b_ih.rearrange("(k p) -> k p", p=P)).then_inc(s_bias, 16)
            act.dma_start(bias_rows[12:20, :], b_hh.rearrange("(k p) -> k p", p=P)).then_inc(s_bias, 16)
            act.dma_start(bias_rows[20:21, :], b1.unsqueeze(0)).then_inc(s_bias, 16)
            act.dma_start(bias_rows[21:22, :], b2.unsqueeze(0)).then_inc(s_bias, 16)

            def norm_row(t):
                act.wait_ge(s_tr, t)
                act.wait_ge(s_nbias0, t + 1)
                act.activation(hrow[:, :], xr[:, bass.ds(t, 1), :].rearrange("p a d -> p (a d)"), ACT.Relu,
                               bias=nbias0[:, bass.ds(t, 1)], scale=rstd0[:, bass.ds(t, 1)]).then_inc(s_hrow, 1)

            def copy_hT(t):
                act.wait_ge(s_tr, t + 1)
                act.wait_ge(s_a, t * 2)
                act.copy(hT[:, :, :].rearrange("p k n -> p (k n)"), bank[0][:, 0:D]).then_inc(s_hT, 1)

            def mid(t, r):
                act.wait_ge(s_a, t * 2 + (r + 1))
                act.wait_ge(s_b, t * 2)
                for o in range(KD):
                    last = act.activation(midT[:, r, o, :], bank[2 + r][:, o * P:(o + 1) * P], ACT.Relu,
                                          bias=bias[:, 2 * r + o:2 * r + o + 1])
                last.then_inc(s_mid, 1)

            def messages(t, r):
                act.wait_ge(s_ysum, t * 2 + (r + 1))
                act.wait_ge(s_ystored[r], t * 16)
                act.activation(yrow[:, r, :], ysum[:, r, :], ACT.Relu).then_inc(s_yrow, 1)

            norm_row(0)
            copy_hT(0)
            act.wait_ge(s_relT, 3)

            def table_tile(t, before, more):
                if more:
                    norm_row(t + 1)
                if before is not None:
                    messages(before, 1)
                mid(t, 0)
                mid(t, 1)
                if more:
                    copy_hT(t + 1)
                messages(t, 0)

            table_tile(0, None, True)
            with act.Fori(1, NT - 1) as t:
                table_tile(t, t - 1, True)
            table_tile(NT - 1, NT - 2, False)
            messages(NT - 1, 1)

            def gates(w):
                act.wait_ge(s_gates, w + 1)
                act.wait_ge(s_hn, w)
                for c in range(6):
                    half = c // 2 != 1
                    col = (0, 1, 4, 5, 6, 7)[c]
                    last = act.activation(tg[:, c, :], bank[2 + c // 4][:, (c % 4) * P:(c % 4 + 1) * P], ACT.Tanh,
                                          bias=(gate_half if half else gate_bias)[:, col:col + 1],
                                          scale=0.5 if half else 1.0)
                last.then_inc(s_tg, 1)

            def cell_tanh(w):
                act.wait_ge(s_cell, w + 1)
                act.wait_ge(s_hn, w)
                act.activation(tcell[:, :, :].rearrange("p k n -> p (k n)"), cell[:, :, :].rearrange("p k n -> p (k n)"),
                               ACT.Tanh, scale=0.5).then_inc(s_tcell, 1)

            def mlp1(w):
                act.wait_ge(s_w1, w + 1)
                act.wait_ge(s_w2, w)
                act.activation(x1T[:, :], bank[4][:, 0:P], ACT.Relu, bias=bias[:, 20:21], scale=0.5).then_inc(s_x1, 1)

            def mlp2(w):
                act.wait_ge(s_w2, w + 1)
                act.wait_ge(s_w3, w)
                act.activation(x2T[:, :], bank[4][:, P:2 * P], ACT.Relu, bias=bias[:, 21:22]).then_inc(s_x2, 1)

            def norm_row1(w):
                act.wait_ge(s_tr1, w)
                act.wait_ge(s_nbias, w + 1)
                act.activation(hrow[:, :], xr[:, bass.ds(w, 1), :].rearrange("p a d -> p (a d)"), ACT.Relu,
                               bias=nbias[:, 1:2], scale=rstd[:, 1:2]).then_inc(s_hrow1, 1)

            def copy_hT1(w):
                act.wait_ge(s_tr1, w + 1)
                act.wait_ge(s_g, w)
                act.copy(hT[:, :, :].rearrange("p k n -> p (k n)"), bank[6][:, 0:D]).then_inc(s_hT1, 1)

            def g_rows(w):
                act.wait_ge(s_gsc, w + 1)
                act.wait_ge(s_gstored, w * 16)
                act.copy(grow[:, :], bank[7][:, 0:D]).then_inc(s_grow, 1)

            def node_tile(w, v):
                if w is not None:
                    gates(w)
                    cell_tanh(w)
                if v is not None:
                    norm_row1(v)
                if w is not None:
                    mlp1(w)
                if v is not None:
                    copy_hT1(v)
                    g_rows(v)
                if w is not None:
                    mlp2(w)

            def copy_m(i, b):
                act.wait_ge(s_m, i * 2 + (b + 2))
                act.wait_ge(s_comb, i * 4 + (2 * b + 2))
                for c in range(2):
                    last = act.copy(m_sb[:, b, 4 * c:4 * c + 4, :].rearrange("p j e -> p (j e)"), bank[2 + c][:, :])
                last.then_inc(s_mcopied, 1)

            def copy_comb(i, b):
                for h in range(2):
                    act.wait_ge(s_comb, i * 4 + (2 * b + h + 5))
                    act.wait_ge(s_passed, i * (2 * GROUP) + (b * GROUP + h * ACCS))
                    for c in range(2 * h, 2 * h + 2):
                        last = act.copy(comb[:, b, 2 * c:2 * c + 2, :].rearrange("p j d -> p (j d)"), bank[4 + c][:, :])
                    last.then_inc(s_combsb, 1)

            act.sem_inc(s_combsb, 2)
            flag = flag_of(act)
            with act.If(flag < 1):
                node_tile(0, None)
                with act.Fori(1, NT) as w:
                    node_tile(w, w - 1)
                node_tile(None, NT - 1)
                copy_m(0, 0)
                with act.Fori(0, NPAIR - 1) as i:
                    copy_m(i, 1)
                    copy_comb(i, 0)
                    copy_m(i + 1, 0)
                    copy_comb(i, 1)
                copy_m(NPAIR - 1, 1)
                copy_comb(NPAIR - 1, 0)
                copy_comb(NPAIR - 1, 1)
            with act.Else():
                with act.Fori(0, NT) as w:
                    node_tile(w, None)
                    node_tile(None, w)
                with act.Fori(0, NPAIR) as i:
                    copy_comb(i, 0)
                    copy_comb(i, 1)
            act.nop()

            def relu_turned(p, q, n):
                act.wait_ge(l_turned, p + 1)
                act.wait_ge(l_prod, p + 1)
                act.activation(f_rT[q].rearrange("p u d -> p (u d)")[:, 0:KD * n * P], bank[q][:, 0:KD * n * P],
                               ACT.Relu).then_inc(l_rT, 1)

            def relu_rows(p, q, n):
                act.wait_ge(l_prod, p + 3)
                act.wait_ge(l_aggr, p)
                act.activation(f_r[q][:, 0:n, :].rearrange("p u d -> p (u d)"), bank[2 + q][:, 0:n * D], ACT.Relu).then_inc(l_r, 1)

            def normalise(p, q, n):
                act.wait_ge(l_nbias, p + 1)
                act.wait_ge(l_q, p)
                for u in range(n):
                    last = act.activation(f_n[:, u, :], f_r[q][:, u, :], ACT.Identity, bias=nbias[:, u:u + 1], scale=rstd[:, u:u + 1])
                last.then_inc(l_n, 1)

            relu_turned(0, 0, 2)
            with act.Fori(0, NPT // 2 - 1) as i:
                for q in range(2):
                    relu_rows(i * 2 + q, q, 2)
                    relu_turned(i * 2 + (q + 1), 1 - q, 2)
                    normalise(i * 2 + q, q, 2)
            relu_rows(NPT - 3, 0, 2)
            relu_turned(NPT - 2, 1, 2)
            normalise(NPT - 3, 0, 2)
            relu_rows(NPT - 2, 1, 2)
            relu_turned(NPT - 1, 0, 1)
            normalise(NPT - 2, 1, 2)
            relu_rows(NPT - 1, 0, 1)
            normalise(NPT - 1, 0, 1)

        @block.vector
        def _(dve):
            def stats(v, n, which, applied, count, summed=None):
                dve.wait_ge(s_xin[0], 16)
                dve.wait_ge(applied, count)
                if summed is not None:
                    dve.wait_ge(s_xr, summed)
                dve.bn_stats(bst[:, which, :], v).then_inc(s_stats, 1)
                dve.wait_ge(s_stats, n + 1)
                dve.sem_inc(go_aggr, 1)
                dve.bn_aggr(mv[:, which, :], bst[:, which, :]).then_inc(s_aggr, 1)

            def x_tile(t):
                return xr[:, bass.ds(t, 1), :].rearrange("p a d -> p (a d)")

            def stats0(t):
                dve.wait_ge(s_aggr0, t)
                dve.sem_inc(go_aggr, 1)
                dve.bn_stats(bst0[:, :], x_tile(t)).then_inc(s_stats0, 1)
                dve.wait_ge(s_stats0, t + 1)
                dve.sem_inc(go_aggr, 1)
                dve.bn_aggr(mv_of[:, :], bst0[:, :]).then_inc(s_mv_of, 1)
                dve.wait_ge(s_mv_of, t + 1)
                dve.tensor_copy(mv0[:, bass.ds(t, 1), :].rearrange("p a s -> p (a s)"), mv_of[:, :]).then_inc(s_aggr0, 1)

            dve.wait_ge(s_xin[0], 16)
            dve.sem_inc(go_aggr, 1)
            for t in range(LEAD):
                stats0(t)
            dve.wait_ge(s_relps, 1)
            dve.tensor_copy(relT[:, 0].rearrange("p k o -> p (k o)"), bank[4][:, :]).then_inc(s_relT, 1)
            dve.wait_ge(s_relps, 2)
            dve.tensor_copy(relT[:, 1].rearrange("p k o -> p (k o)"), bank[5][:, :]).then_inc(s_relT, 1)
            dve.wait_ge(s_relps, 3)
            dve.tensor_copy(bias[:, :], bank[6][:, 0:NB]).then_inc(s_relT, 1)
            dve.wait_ge(s_relT, 3)
            dve.tensor_tensor(gate_bias[:, :], bias[:, 4:12], bias[:, 12:20], ALU.add).then_inc(s_gb, 1)
            dve.wait_ge(s_gb, 1)
            dve.tensor_scalar(gate_half[:, :], gate_bias[:, :], 0.5, None, ALU.mult).then_inc(s_gb, 1)

            def edge_columns():
                for n, to in enumerate((srcT, dstT, typT)):
                    dve.wait_ge(s_eps_ps, n + 1)
                    dve.tensor_copy(to[:, :], bank[(6, 7, 1)[n]][:, 0:ET]).then_inc(s_eT, 1)
                yield
                dve.wait_ge(s_eps_ps, 4)
                dve.tensor_copy(wT[:, :], bank[6][:, 0:ET]).then_inc(s_eT, 1)

                prep = [0]

                def step(ins):
                    prep[0] += 1
                    ins.then_inc(s_prep, 1)
                    dve.wait_ge(s_prep, prep[0])

                dve.wait_ge(s_eT, 4)
                for r in range(2):
                    step(dve.tensor_scalar(isr[:, r, :], typT[:, :], float(r), None, ALU.is_equal))
                    step(dve.scalar_tensor_tensor(out=isr[:, r, :], in0=srcT[:, :], scalar=float(r * NODES - ZROW),
                                                  in1=isr[:, r, :], op0=ALU.add, op1=ALU.mult))
                yield
                step(dve.scalar_tensor_tensor(out=gidx[:, :], in0=isr[:, 0, :], scalar=float(ZROW), in1=isr[:, 1, :],
                                              op0=ALU.add, op1=ALU.add))
                step(dve.tensor_copy(dst_i[:, :], dstT[:, :]))
                step(dve.tensor_scalar(to_spare[:, :], srcT[:, :], -1.0, spare[:, 0:1], ALU.mult, ALU.add))
                dve.tensor_scalar(onep[:, :], eps_b[:, :], 1.0, None, ALU.add).then_inc(s_gidx, 1)
                yield
                dve.wait_ge(s_base_ps, 1)
                dve.tensor_copy(base_f[:, :], bank[7][:, 0:NG]).then_inc(s_base, 1)
                evacuate(0, 2)
                yield
                dve.wait_ge(s_base, 1)
                step(dve.tensor_tensor(loc[:, :, :], dstT[:, :].rearrange("p (g j) -> p g j", j=GROUP),
                                       base_f[:, :].unsqueeze(2).to_broadcast([P, NG, GROUP]), ALU.subtract))
                step(dve.tensor_reduce(chk[:, 0:1], loc[:, :, :].rearrange("p g j -> p (g j)"), AX.X, ALU.max))
                step(dve.tensor_reduce(chk[:, 1:2], loc[:, :, :].rearrange("p g j -> p (g j)"), AX.X, ALU.min))
                step(dve.tensor_scalar(chk[:, 2:3], chk[:, 0:1], float(P - 1), None, ALU.is_gt))
                step(dve.scalar_tensor_tensor(out=chk[:, 3:4], in0=chk[:, 1:2], scalar=0.0, in1=chk[:, 2:3],
                                              op0=ALU.is_lt, op1=ALU.add))
                evacuate(2, 5)
                yield
                step(dve.tensor_tensor(chk_row[:, 0, 0:NG - 1], base_f[0:1, 1:NG], base_f[0:1, 0:NG - 1], ALU.is_lt))
                step(dve.tensor_reduce(chk_row[:, 1, 0:1], chk_row[:, 0, 0:NG - 1], AX.X, ALU.max))
                nw = NPAIR - LAG
                step(dve.scalar_tensor_tensor(out=chk_row[:, 2, 0:nw], in0=wbase[0:1, 0:nw], scalar=float(P),
                                              in1=base_f[0:1, 2 * LAG:NG:2], op0=ALU.add, op1=ALU.is_gt))
                step(dve.tensor_reduce(chk_row[:, 1, 1:2], chk_row[:, 2, 0:nw], AX.X, ALU.max))
                dve.tensor_copy(ctrl[0:1, 0:NG], base_f[0:1, :])
                step(dve.tensor_tensor(chk_row[:, 1, 2:3], chk_row[:, 1, 0:1], chk_row[:, 1, 1:2], ALU.add))
                step(dve.tensor_tensor(chk[0:1, 3:4], chk[0:1, 3:4], chk_row[:, 1, 2:3], ALU.add))
                dve.sem_inc(s_viol, 1)
                evacuate(5, 6)
                yield
                dve.wait_ge(s_viol, 2)
                step(dve.tensor_scalar(ctrl[0:1, FLAG:FLAG + 1], bank[6][0:1, 0:1], 0.0, None, ALU.is_gt))
                dve.sem_inc(s_ctrl, 2)
                yield

            def evacuate(a, b):
                of = [(w3T[:, :], bank[6][:, 0:D]), (w1T[:, :, :].rearrange("p k o -> p (k o)"), bank[1][:, 0:D]),
                      (w2T[:, :], bank[1][:, D:D + P])] + \
                     [(ihT[:, 2 * c:2 * c + 2].rearrange("p c k o -> p (c k o)"), bank[(6, 7, 6)[c]][:, :]) for c in range(3)]
                for n in range(a, b):
                    dve.wait_ge(s_wps, n + 1)
                    dve.tensor_copy(*of[n]).then_inc(s_wT, 1)

            def add_bias(t, r):
                dve.wait_ge(s_b, t * 2 + (r + 1))
                dve.wait_ge(s_yrow, t * 2)
                dve.tensor_tensor(ysum[:, r, :], bank[4 + r][:, 0:D], brel_b[:, r, :], ALU.add).then_inc(s_ysum, 1)

            def table_tile(t, ahead=True):
                if ahead:
                    stats0(t + LEAD)
                add_bias(t, 0)
                add_bias(t, 1)

            dve.wait_ge(s_bias, 16 * 6)
            dve.wait_ge(s_xin[1], 16)
            dve.sem_inc(go_aggr, 1)
            with dve.Fori(0, X_LOADS[1][1] - LEAD) as t:
                table_tile(t)
            dve.wait_ge(s_xin[2], 32)
            dve.sem_inc(go_aggr, 1)
            with dve.Fori(X_LOADS[1][1] - LEAD, MID) as t:
                table_tile(t)
            slots = edge_columns()
            for n in range(NSLOT):
                next(slots)
                table_tile(MID + n)
            with dve.Fori(MID + NSLOT, NT - LEAD) as t:
                table_tile(t)
            with dve.Fori(NT - LEAD, NT) as t:
                table_tile(t, False)
            dve.sem_inc(s_added, 2)
            dve.wait_ge(s_aggz, KD)

            def one_hot(i, b):
                dve.wait_ge(s_summed, i * 2 + (b + 1))
                dve.tensor_tensor(oh[:, b, :, :], iota_row[:, :].unsqueeze(1).to_broadcast([P, GROUP, P]),
                                  loc[:, bass.ds(i * 2 + b, 1), :].rearrange("p a j -> p (a j)").unsqueeze(2).to_broadcast([P, GROUP, P]),
                                  ALU.is_equal).then_inc(s_oh, 1)

            def add_window(i, b):
                base = dve.value_load(ctrl[0:1, bass.ds(i * 2 + b, 1)], min_val=0, max_val=NODES - 1)
                dve.wait_ge(s_summed, i * 2 + (b + 3))
                dve.wait_ge(s_added, i * 2 + (b + 2))
                v = aggT[:, :, bass.ds(base, P)]
                dve.tensor_tensor(v, v, bank[b][:, 0:D].rearrange("p (k n) -> p k n", k=KD), ALU.add).then_inc(s_added, 1)

            def cell_c(w):
                dve.wait_ge(s_tg, w + 1)
                dve.wait_ge(s_tcell, w)
                dve.scalar_tensor_tensor(out=cell[:, :, :], in0=tg[:, 0:2, :], scalar=1.0, in1=tg[:, 2:4, :],
                                         op0=ALU.add, op1=ALU.mult).then_inc(s_cell, 1)

            def cell_h(w):
                dve.wait_ge(s_tcell, w + 1)
                dve.wait_ge(s_w1, w)
                dve.scalar_tensor_tensor(out=hn[:, :, :], in0=tg[:, 4:6, :], scalar=1.0, in1=tcell[:, :, :],
                                         op0=ALU.add, op1=ALU.mult).then_inc(s_hn, 1)

            def residual(w):
                dve.wait_ge(s_w3, w + 1)
                dve.tensor_tensor(x_tile(w), x_tile(w), bank[5][:, 0:D], ALU.add).then_inc(s_xr, 1)
                stats(x_tile(w), w, 1, s_hrow1, w, w + 1)

            def open_acc(v):
                dve.wait_ge(s_hrow1, v + 1)
                dve.tensor_tensor(x_tile(v), x_tile(v), offset_b[:, :], ALU.add).then_inc(s_off, 1)
                dve.wait_ge(s_g, v + 1)
                dve.wait_ge(s_acc0, v * 16)
                dve.scalar_tensor_tensor(out=gsc[:, :], in0=bank[7][:, 0:D], scalar=onep[:, 0:1], in1=gb1_b[:, :],
                                         op0=ALU.mult, op1=ALU.add).then_inc(s_gsc, 1)

            def sources(i, b, done):
                dve.wait_ge(s_sidx, done)
                dve.tensor_copy(scol[:, b, :], srcT[:, bass.ds(i * (2 * GROUP) + b * GROUP, GROUP)]).then_inc(s_scol, 1)

            def same_source(i, b, used):
                dve.wait_ge(s_srow, i * 2 + (b + 1))
                dve.wait_ge(*used(i, b))
                dve.wait_ge(s_prior, i * 2 + b)
                for c in range(2):
                    last = dve.tensor_tensor(same[:, b, 4 * c:4 * c + 4, :], bank[c][:, :].rearrange("p (j e) -> p j e", e=P),
                                             scol[:, b, 4 * c:4 * c + 4].unsqueeze(2).to_broadcast([P, 4, P]), ALU.is_equal)
                last.then_inc(s_same, 1)

            def scatter_rows(i, b):
                dve.wait_ge(s_same, i * 2 + (b + 1))
                dve.wait_ge(s_dup, i * 2 + b)
                dve.tensor_tensor(prior[:, :, :], same[:, b], earlier[:, :].unsqueeze(1).to_broadcast([P, GROUP, P]),
                                  ALU.mult).then_inc(s_prior, 1)
                dve.wait_ge(s_prior, i * 2 + (b + 1))
                dve.wait_ge(s_dupm, i * 2 + b)
                dve.tensor_reduce(dup[:, :], prior[:, :, :], AX.X, ALU.max).then_inc(s_dup, 1)
                dve.wait_ge(s_dup, i * 2 + (b + 1))
                dve.wait_ge(s_sidx, i * 2 + b)
                dve.tensor_tensor(sidx_f[:, :], dup[:, :], to_spare[:, bass.ds(i * (2 * GROUP) + b * GROUP, GROUP)],
                                  ALU.mult).then_inc(s_dupm, 1)
                dve.wait_ge(s_dupm, i * 2 + (b + 1))
                dve.tensor_tensor(sidx[:, bass.ds(i * (2 * GROUP) + b * GROUP, GROUP)], sidx_f[:, :], scol[:, b, :], ALU.add).then_inc(s_sidx, 1)

            def weigh(i, b, what, sem_in, used):
                dve.wait_ge(sem_in, i * 2 + (b + 1))
                dve.wait_ge(*used(i, b))
                wcol = wT[:, bass.ds(i * (2 * GROUP) + b * GROUP, GROUP)].unsqueeze(2).to_broadcast([P, GROUP, P])
                dve.tensor_tensor(ohw[:, b], what, wcol, ALU.mult).then_inc(s_ohw, 1)

            dve.wait_ge(s_wT, 6)
            flag = flag_of(dve)
            with dve.If(flag < 1):
                one_hot(0, 0)
                one_hot(0, 1)
                for i in range(LAG):
                    add_window(i, 0)
                    one_hot(i + 1, 0)
                    add_window(i, 1)
                    one_hot(i + 1, 1)
                def node_round(i, w, v, more):
                    cell_c(w)
                    cell_h(w)
                    add_window(i, 0)
                    if more:
                        one_hot(i + 1, 0)
                    if v is not None:
                        open_acc(v)
                    add_window(i, 1)
                    if more:
                        one_hot(i + 1, 1)
                    residual(w)

                node_round(LAG, 0, None, True)
                with dve.Fori(LAG + 1, NPAIR - 1) as i:
                    node_round(i, i - LAG, i - (LAG + 1), True)
                node_round(NPAIR - 1, NPAIR - 1 - LAG, NPAIR - 2 - LAG, False)
                for w in range(NPAIR - LAG, NT):
                    cell_c(w)
                    cell_h(w)
                    open_acc(w - 1)
                    residual(w)
                open_acc(NT - 1)

                used = lambda i, b: (s_m, i * 2 + b)
                dve.sem_inc(s_m, 1)
                sources(0, 0, 0)

                def group_round(i, b, more):
                    if more:
                        sources(*((i, 1) if b == 0 else (i + 1, 0)), i * 2 + b)
                    dve.wait_ge(*used(i, b))
                    dve.tensor_tensor(ohw[:, b], iota_row[:, :].unsqueeze(1).to_broadcast([P, GROUP, P]),
                                      loc[:, bass.ds(i * 2 + b, 1), :].rearrange("p a j -> p (a j)").unsqueeze(2).to_broadcast([P, GROUP, P]),
                                      ALU.is_equal).then_inc(s_eq, 1)
                    same_source(i, b, used)
                    weigh(i, b, ohw[:, b], s_eq, used)
                    scatter_rows(i, b)

                with dve.Fori(0, NPAIR - 1) as i:
                    group_round(i, 0, True)
                    group_round(i, 1, True)
                group_round(NPAIR - 1, 0, True)
                group_round(NPAIR - 1, 1, False)
            with dve.Else():
                with dve.Fori(0, NG) as g:
                    with dve.Fori(0, NT) as w:
                        k = g * NT + w
                        dve.wait_ge(g_oh, k)
                        dve.tensor_tensor(wloc[:, :], dstT[:, bass.ds(g * GROUP, GROUP)],
                                          wbase[:, bass.ds(w, 1)].to_broadcast([P, GROUP]), ALU.subtract).then_inc(g_loc, 1)
                        dve.wait_ge(g_loc, k + 1)
                        dve.wait_ge(g_summed, k)
                        dve.tensor_tensor(oh[:, 0, :, :], iota_row[:, :].unsqueeze(1).to_broadcast([P, GROUP, P]),
                                          wloc[:, :].unsqueeze(2).to_broadcast([P, GROUP, P]), ALU.is_equal).then_inc(g_oh, 1)
                        dve.wait_ge(g_summed, k + 1)
                        dve.wait_ge(g_added, k)
                        v = aggT[:, :, bass.ds(w * P, P)]
                        dve.tensor_tensor(v, v, bank[0][:, 0:D].rearrange("p (k n) -> p k n", k=KD), ALU.add).then_inc(g_added, 1)
                with dve.Fori(0, NT) as w:
                    cell_c(w)
                    cell_h(w)
                    residual(w)
                    open_acc(w)
                used = lambda i, b: (s_comb, i * 4 + (2 * b + 2))
                with dve.Fori(0, NPAIR) as i:
                    for b in range(2):
                        sources(i, b, i * 2 + b)
                        same_source(i, b, used)
                        weigh(i, b, same[:, b], s_same, used)
                        scatter_rows(i, b)
            dve.nop()

            dve.sem_inc(l_tot, 2)

            def total(p, q, n):
                dve.wait_ge(f_loaded[q], (p - q) * (8 * ACCS) + 16 * ACCS)
                dve.wait_ge(l_tot, p + 2)
                dve.tensor_tensor(f_s01[:, 0:n, :], fa[q][:, 0, 0:n, :], fa[q][:, 1, 0:n, :], ALU.add).then_inc(l_s01, 1)
                dve.wait_ge(l_s01, p + 1)
                dve.wait_ge(l_s23, p + 1)
                dve.wait_ge(l_turned, p)
                dve.tensor_tensor(f_tot[q][:, 0:n, :], f_s01[:, 0:n, :], f_s23[q][:, 0:n, :], ALU.add).then_inc(l_tot, 1)

            def row_stats(p, q, n):
                dve.wait_ge(l_r, p + 1)
                dve.wait_ge(l_aggr, p)
                for u in range(n):
                    last = dve.bn_stats(bst[:, u, :], f_r[q][:, u, :])
                last.then_inc(l_stats, 1)
                dve.wait_ge(l_stats, p + 1)
                dve.wait_ge(l_nbias, p)
                dve.sem_inc(go_aggr, 1)
                for u in range(n):
                    last = dve.bn_aggr(mv[:, u, :], bst[:, u, :])
                last.then_inc(l_aggr, 1)

            def add_rows(p, q, n):
                dve.wait_ge(l_q, p + 1)
                dve.wait_ge(l_stored[q], (p - q) * 8)
                dve.tensor_tensor(f_o[q][:, 0:n, :], f_q[q][:, 0:n, :], xr[:, bass.ds(p * 2, n), :], ALU.add).then_inc(l_out, 1)

            def pair_round(p, q, n, before, after):
                if after:
                    total(p + 1, 1 - q, after)
                if before:
                    add_rows(p - 2, q, 2)
                row_stats(p, q, n)

            dve.wait_ge(s_off, NT)
            dve.sem_inc(l_out, 1)
            total(0, 0, 2)
            pair_round(0, 0, 2, False, 2)
            pair_round(1, 1, 2, False, 2)
            with dve.Fori(1, NPT // 2 - 1) as i:
                pair_round(i * 2, 0, 2, True, 2)
                pair_round(i * 2 + 1, 1, 2, True, 2)
            pair_round(NPT - 3, 0, 2, True, 2)
            pair_round(NPT - 2, 1, 2, True, 1)
            pair_round(NPT - 1, 0, 1, True, 0)
            add_rows(NPT - 2, 1, 2)
            add_rows(NPT - 1, 0, 1)

        @block.tensor
        def _(pe):
            pe.wait_ge(s_const, 1)
            pe.wait_ge(s_wrel, 32)
            for r in range(2):
                for k in range(KD):
                    for c in range(KD):
                        last = pe.transpose(bank[4 + r][:, k * D + c * P:k * D + (c + 1) * P],
                                            rel_raw[:, r, c, k * P:(k + 1) * P], ident[:, :])
                last.then_inc(s_relps, 1)
            pe.wait_ge(s_bias, 16 * 6)
            pe.transpose(bank[6][:, 0:NB], bias_rows[:, :], ident[0:NB, 0:NB]).then_inc(s_relps, 1)

            def turn(t):
                pe.wait_ge(s_hrow, t + 1)
                pe.wait_ge(s_hT, t)
                for k in range(KD):
                    last = pe.transpose(bank[0][:, k * P:(k + 1) * P], hrow[:, k * P:(k + 1) * P], ident[:, :])
                last.then_inc(s_tr, 1)

            def product1(t, r):
                pe.wait_ge(s_hT, t + 1)
                pe.wait_ge(s_mid, t * 2)
                for o in range(KD):
                    for k in range(KD):
                        last = pe.matmul(bank[2 + r][:, o * P:(o + 1) * P], relT[:, r, k, o * P:(o + 1) * P],
                                         hT[:, k, :], start=(k == 0), stop=(k == KD - 1))
                last.then_inc(s_a, 1)

            def product2(t, r):
                pe.wait_ge(s_mid, t * 2 + (r + 1))
                pe.wait_ge(s_ysum, t * 2)
                for k in range(KD):
                    last = pe.matmul(bank[4 + r][:, 0:D], midT[:, r, k, :], relT[:, r, k, :], start=(k == 0), stop=(k == KD - 1))
                last.then_inc(s_b, 1)

            def edge_columns(n):
                a = e_f[:, n] if n < 3 else e_w
                for c in range(EC):
                    rows = P if c < EC - 1 else RT
                    last = pe.transpose(bank[(6, 7, 1, 6)[n]][:, c * P:c * P + rows], a[0:rows, c, :], ident[0:rows, 0:rows])
                last.then_inc(s_eps_ps, 1)

            def gate_weights(n):
                for c in range(2):
                    for k in range(KD):
                        last = pe.transpose(bank[(6, 7, 6)[n]][:, (2 * c + k) * P:(2 * c + k + 1) * P],
                                            ih_raw[:, 2 * n + c, k * P:(k + 1) * P], ident[:, :])
                last.then_inc(s_wps, 1)

            def layout():
                pe.wait_ge(s_ef, 3)
                for n in range(3):
                    edge_columns(n)
                yield
                pe.wait_ge(s_eT, 1)
                edge_columns(3)
                yield
                pe.wait_ge(s_eT, 2)
                pe.matmul(bank[7][:, 0:NG], row0[:, :], dstT[:, 0:ET:GROUP], start=True, stop=True).then_inc(s_base_ps, 1)
                yield
                pe.wait_ge(s_wts, 16 * N_WTS)
                pe.wait_ge(s_eT, 4)
                for c in range(KD):
                    last = pe.transpose(bank[6][:, c * P:(c + 1) * P], w3_raw[:, c, :], ident[:, :])
                last.then_inc(s_wps, 1)
                for k in range(KD):
                    last = pe.transpose(bank[1][:, k * P:(k + 1) * P], w1_raw[:, k * P:(k + 1) * P], ident[:, :])
                last.then_inc(s_wps, 1)
                yield
                pe.wait_ge(s_wT, 2)
                pe.transpose(bank[1][:, D:D + P], w2_raw[:, :], ident[:, :]).then_inc(s_wps, 1)
                gate_weights(0)
                pe.wait_ge(s_base, 1)
                gate_weights(1)
                yield
                pe.wait_ge(s_wT, 4)
                gate_weights(2)
                yield
                pe.wait_ge(s_viol, 1)
                pe.wait_ge(s_wT, 6)
                pe.matmul(bank[6][0:1, 0:1], chk[:, 3:4], ones[:, 0:1], start=True, stop=True).then_inc(s_viol, 1)
                yield

            turn(0)
            pe.wait_ge(s_relT, 3)

            def table_tile(t, last):
                product1(t, 0)
                product1(t, 1)
                if not last:
                    turn(t + 1)
                product2(t, 0)
                product2(t, 1)

            with pe.Fori(0, MID) as t:
                table_tile(t, False)
            slots = layout()
            for n in range(NSLOT):
                next(slots)
                table_tile(MID + n, False)
            with pe.Fori(MID + NSLOT, NT - 1) as t:
                table_tile(t, False)
            table_tile(NT - 1, True)
            pe.wait_ge(s_ysum, 2 * NT)
            pe.wait_ge(s_wT, 6)
            pe.sem_inc(s_summed, 2)

            def sum_window(b, parts, signal):
                for k, j0, j1 in parts:
                    for j in range(j0, j1):
                        last = pe.matmul(bank[b][:, k * P:(k + 1) * P], msgs[:, b, j, k * P:(k + 1) * P], oh[:, b, j, :],
                                         start=(j == 0), stop=(j == GROUP - 1))
                if signal is not None:
                    last.then_inc(signal, 1)

            def ready(i, b):
                pe.wait_ge(s_oh, i * 2 + (b + 1))
                pe.wait_ge(s_gathered[b], i * (16 * GROUP) + 16 * GROUP)
                pe.wait_ge(s_added, i * 2 + (b + 1))

            def gates(w):
                pe.wait_ge(s_tg, w)
                for c in range(6):
                    for k in range(KD):
                        last = pe.matmul(bank[2 + c // 4][:, (c % 4) * P:(c % 4 + 1) * P], ihT[:, c, k, :],
                                         aggT[:, k, bass.ds(w * P, P)], start=(k == 0), stop=(k == KD - 1))
                last.then_inc(s_gates, 1)

            def mlp1(w):
                pe.wait_ge(s_hn, w + 1)
                pe.wait_ge(s_x1, w)
                for k in range(KD):
                    last = pe.matmul(bank[4][:, 0:P], w1T[:, k, :], hn[:, k, :], start=(k == 0), stop=(k == KD - 1))
                last.then_inc(s_w1, 1)

            def mlp2(w):
                pe.wait_ge(s_x1, w + 1)
                pe.wait_ge(s_x2, w)
                pe.matmul(bank[4][:, P:2 * P], w2T[:, :], x1T[:, :], start=True, stop=True).then_inc(s_w2, 1)

            def mlp3(w):
                pe.wait_ge(s_x2, w + 1)
                pe.wait_ge(s_xr, w)
                pe.matmul(bank[5][:, 0:D], ones[0:1, :], b3_row[:, :], start=True, stop=False)
                pe.matmul(bank[5][:, 0:D], x2T[:, :], w3T[:, :], start=False, stop=True).then_inc(s_w3, 1)

            def turn1(v):
                pe.wait_ge(s_hrow1, v + 1)
                pe.wait_ge(s_hT1, v)
                for k in range(KD):
                    last = pe.transpose(bank[6][:, k * P:(k + 1) * P], hrow[:, k * P:(k + 1) * P], ident[:, :])
                last.then_inc(s_tr1, 1)

            def g_product(v):
                pe.wait_ge(s_hT1, v + 1)
                pe.wait_ge(s_grow, v)
                for k in range(KD):
                    last = pe.matmul(bank[7][:, 0:D], hT[:, k, :], gw1[:, k, :], start=(k == 0), stop=(k == KD - 1))
                last.then_inc(s_g, 1)

            def node_tile(w, v):
                if w is not None:
                    gates(w)
                    mlp1(w)
                if v is not None:
                    turn1(v)
                    g_product(v)
                if w is not None:
                    mlp2(w)
                    mlp3(w)

            def source_rows(i, b):
                pe.wait_ge(s_scol, i * 2 + (b + 1))
                pe.wait_ge(s_same, i * 2 + b)
                for j in range(GROUP):
                    last = pe.transpose(bank[j // 4][:, (j % 4) * P:(j % 4 + 1) * P],
                                        scol[:, b, j:j + 1].to_broadcast([P, P]), ident[:, :])
                last.then_inc(s_srow, 1)

            def rows_out(i, b, lhs, rhs):
                for h in range(2):
                    pe.wait_ge(s_combsb, i * 4 + (2 * b + h + 1))
                    for j in range(h * GROUP // 2, (h + 1) * GROUP // 2):
                        last = pe.matmul(bank[4 + j // 2][:, (j % 2) * D:(j % 2 + 1) * D], lhs(j), rhs(j), start=True, stop=True)
                    last.then_inc(s_comb, 1)

            flag = flag_of(pe)
            with pe.If(flag < 1):
                half0, half1 = (0, 0, GROUP), (1, 0, GROUP)

                def both(i):
                    for b in range(2):
                        ready(i, b)
                        sum_window(b, (half0, half1), s_summed)

                for i in range(LAG):
                    both(i)

                def node_round(i, w, v):
                    pe.wait_ge(s_added, i * 2 + 2)
                    gates(w)
                    ready(i, 0)
                    sum_window(0, (half0, half1), s_summed)
                    mlp1(w)
                    if v is not None:
                        turn1(v)
                    ready(i, 1)
                    sum_window(1, (half0,), None)
                    if v is not None:
                        g_product(v)
                    mlp2(w)
                    sum_window(1, (half1,), s_summed)
                    mlp3(w)

                node_round(LAG, 0, None)
                with pe.Fori(LAG + 1, NPAIR) as i:
                    node_round(i, i - LAG, i - (LAG + 1))
                pe.wait_ge(s_added, NG + 2)
                for w in range(NPAIR - LAG, NT):
                    node_tile(w, w - 1)
                node_tile(None, NT - 1)
                pe.sem_inc(s_comb, 4)
                pe.wait_ge(s_grow, NT)

                def weights_of(i, b):
                    pe.wait_ge(s_same, i * 2 + (b + 1))
                    pe.wait_ge(s_ohw, i * 2 + (b + 1))
                    pe.wait_ge(s_mcopied, i * 2 + b)
                    for j in range(GROUP):
                        last = pe.matmul(bank[2 + j // 4][:, (j % 4) * P:(j % 4 + 1) * P], ohw[:, b, j, :], same[:, b, j, :],
                                         start=True, stop=True)
                    last.then_inc(s_m, 1)

                def window_rows(i, b):
                    pe.wait_ge(s_mcopied, i * 2 + (b + 1))
                    pe.wait_ge(s_hwin[b], i * 16 + 16)
                    rows_out(i, b, lambda j: m_sb[:, b, j, :], lambda j: hwin[:, b, :])

                source_rows(0, 0)
                weights_of(0, 0)
                source_rows(0, 1)
                with pe.Fori(0, NPAIR - 1) as i:
                    weights_of(i, 1)
                    source_rows(i + 1, 0)
                    window_rows(i, 0)
                    weights_of(i + 1, 0)
                    source_rows(i + 1, 1)
                    window_rows(i, 1)
                weights_of(NPAIR - 1, 1)
                window_rows(NPAIR - 1, 0)
                window_rows(NPAIR - 1, 1)
            with pe.Else():
                with pe.Fori(0, NG) as g:
                    pe.wait_ge(g_gathered, g * (16 * GROUP) + 16 * GROUP)
                    pe.sem_inc(go_windows, 1)
                    with pe.Fori(0, NT) as w:
                        pe.wait_ge(g_oh, g * NT + w + 1)
                        pe.wait_ge(g_added, g * NT + w)
                        sum_window(0, ((0, 0, GROUP), (1, 0, GROUP)), g_summed)
                pe.wait_ge(g_added, NG * NT)
                with pe.Fori(0, NT) as w:
                    node_tile(w, None)
                    node_tile(None, w)
                pe.sem_inc(s_comb, 4)
                pe.wait_ge(s_grow, NT)
                with pe.Fori(0, NPAIR) as i:
                    for b in range(2):
                        source_rows(i, b)
                        pe.wait_ge(s_ohw, i * 2 + (b + 1))
                        pe.wait_ge(g_gathered2, i * (32 * GROUP) + 16 * GROUP * (b + 1))
                        rows_out(i, b, lambda j: ohw[:, b, j, :], lambda j: msgs[:, 1, j, :])
            pe.nop()

            def turn_sums(p, q, n):
                pe.wait_ge(l_tot, p + 3)
                pe.wait_ge(l_rT, p)
                for k in range(KD):
                    for u in range(n):
                        last = pe.transpose(bank[q][:, (k * n + u) * P:(k * n + u + 1) * P], f_tot[q][:, u, k * P:(k + 1) * P], ident[:, :])
                last.then_inc(l_turned, 1)

            def last_product(p, q, n):
                pe.wait_ge(l_rT, p + 1)
                pe.wait_ge(l_r, p)
                rT = f_rT[q].rearrange("p u d -> p (u d)")
                for u in range(n):
                    pe.matmul(bank[2 + q][:, u * D:(u + 1) * D], ones[0:1, :], b2_row[:, :], start=True, stop=False)
                    for k in range(KD):
                        last = pe.matmul(bank[2 + q][:, u * D:(u + 1) * D], rT[:, (k * n + u) * P:(k * n + u + 1) * P],
                                         gw2[:, k, :], start=False, stop=(k == KD - 1))
                last.then_inc(l_prod, 1)

            pe.wait_ge(s_combsb, 2 * NG + 2)
            pe.sem_inc(l_prod, 2)
            turn_sums(0, 0, 2)
            with pe.Fori(0, NPT // 2 - 1) as i:
                for q in range(2):
                    last_product(i * 2 + q, q, 2)
                    turn_sums(i * 2 + (q + 1), 1 - q, 2)
            last_product(NPT - 3, 0, 2)
            turn_sums(NPT - 2, 1, 2)
            last_product(NPT - 2, 1, 2)
            turn_sums(NPT - 1, 0, 1)
            last_product(NPT - 1, 0, 1)


N_WTS = 13

_INS = ['x', 'src', 'dst', 'edge_type_2', 'edge_weight', 'L0_gnn_W_rel', 'L0_gnn_b_rel', 'L0_gnn_W_ih', 'L0_gnn_b_ih',
        'L0_gnn_b_hh', 'L0_gnn_W1', 'L0_gnn_b1', 'L0_gnn_W2', 'L0_gnn_b2', 'L0_gnn_W3', 'L0_gnn_b3', 'L1_gnn_W1',
        'L1_gnn_b1', 'L1_gnn_W2', 'L1_gnn_b2', 'L1_gnn_eps', 'L1_gnn_offset', 'L1_gnn_scale']


def kernel(**inputs):
    import numpy as _np
    import concourse.bacc as _bacc
    from concourse import mybir as _mybir
    from concourse.bass_utils import run_bass_kernel_spmd as _run

    nc = _bacc.Bacc("TRN2", target_bir_lowering=False, num_devices=1)
    arrays, args = {}, []
    for name in _INS:
        a = _np.ascontiguousarray(inputs[name])
        arrays[f"in_{name}_dram"] = a
        args.append(nc.dram_tensor(f"in_{name}_dram", a.shape, _mybir.dt.from_np(a.dtype), kind="ExternalInput").ap())
    shape = inputs['x'].shape
    args.append(nc.dram_tensor("out_0_dram", shape, _mybir.dt.float32, kind="ExternalOutput").ap())
    gnn_kernel(nc, *args)
    r = _run(nc, [arrays], core_ids=[0])
    return r.results[0]["out_0_dram"]
```

```python
from contextlib import ExitStack

import concourse.bass as bass
from concourse import mybir

P = 128
F32 = mybir.dt.float32
I32 = mybir.dt.int32
BF16 = mybir.dt.bfloat16
ALU = mybir.AluOpType
ACT = mybir.ActivationFunctionType
AX = mybir.AxisListType

GROUP = 8
ACCS = 4
LAG = 3


def gnn_kernel(nc, x, src, dst, edge_type_2, edge_weight, W_rel, b_rel, W_ih, b_ih, b_hh, W1, b1, W2, b2,
               W3, b3, G_W1, G_b1, G_W2, G_b2, G_eps, G_offset, G_scale, out):
    NODES, D = x.shape
    EDGES = src.shape[0]
    NT = -(-NODES // P)
    LAST = NODES - (NT - 1) * P
    ET = -(-EDGES // P)
    NG = ET // GROUP
    NPAIR = NG // 2
    ROWS = NT * P + P
    KD = D // P
    assert D == 256 and NG * GROUP == ET and NG % 2 == 0 and ET <= 512 and NPAIR == NT + 1
    assert ROWS == 26 * P and b1.shape[0] == P
    EC = -(-ET // P)
    FULL = (EC - 1) * P
    RT = ET - FULL
    PART = EDGES - (ET - 1) * P
    ZROW = 2 * NODES
    FLAG = NG

    ctx = ExitStack()
    with ctx:
        def sb(name, shape, dt=F32):
            return ctx.enter_context(nc.sbuf_tensor(name, shape, dt))

        def sem(name):
            return ctx.enter_context(nc.semaphore(name))

        msg_table = nc.dram_tensor("msg_table", [2 * NODES + 1, D], F32).ap()
        g_table = nc.dram_tensor("g_table", [ROWS, D], F32).ap()
        acc = [nc.dram_tensor(f"acc{k}", [ROWS, D], F32).ap() for k in range(ACCS)]

        ident = sb("ident", [P, P])
        iota_row = sb("iota_row", [P, P])
        earlier = sb("earlier", [P, P])
        row0 = sb("row0", [P, P])
        spare = sb("spare", [P, 1])
        wbase = sb("wbase", [P, NT])
        ones = sb("ones", [P, P])
        minus_half = sb("minus_half", [P, 2])
        minus_one = sb("minus_one", [P, 1])
        ln_eps = sb("ln_eps", [P, 1])
        zeros = sb("zeros", [P, D])
        rel_raw = sb("rel_raw", [P, 2, KD, D])
        relT = sb("relT", [P, 2, KD, D])
        ih_raw = sb("ih_raw", [P, 6, D])
        ihT = sb("ihT", [P, 6, KD, P])
        w1_raw = sb("w1_raw", [P, D])
        w2_raw = sb("w2_raw", [P, P])
        w3_raw = sb("w3_raw", [P, KD, P])
        w1T = sb("w1T", [P, KD, P])
        w2T = sb("w2T", [P, P])
        w3T = sb("w3T", [P, D])
        gw1 = sb("gw1", [P, KD, D])
        gw2 = sb("gw2", [P, KD, D])
        NB = 22
        bias_rows = sb("bias_rows", [NB, P])
        bias = sb("bias", [P, NB])
        gate_bias = sb("gate_bias", [P, 8])
        gate_half = sb("gate_half", [P, 8])
        brel_b = sb("brel_b", [P, 2, D])
        b_part = sb("b_part", [3, 3, 2, D], BF16)
        b_rows = sb("b_rows", [3, 2, D], BF16)
        ones_bf = sb("ones_bf", [3, P], BF16)
        gb1_b = sb("gb1_b", [P, D])
        scale_b = sb("scale_b", [P, D])
        offset_b = sb("offset_b", [P, D])
        eps_b = sb("eps_b", [P, 1])
        xr = sb("xr", [P, NT, D])
        aggT = sb("aggT", [P, KD, ROWS])
        e_int = sb("e_int", [P, 3, EC, P], I32)
        e_w = sb("e_w", [P, EC, P])
        e_f = sb("e_f", [P, 3, EC, P])
        srcT = sb("srcT", [P, ET])
        dstT = sb("dstT", [P, ET])
        typT = sb("typT", [P, ET])
        wT = sb("wT", [P, ET])
        loc = sb("loc", [P, NG, GROUP])
        base_f = sb("base_f", [P, NG])
        to_spare = sb("to_spare", [P, ET])
        isr = sb("isr", [P, 2, ET])
        gidx = sb("gidx", [P, ET], I32)
        dst_i = sb("dst_i", [P, ET], I32)
        ctrl = sb("ctrl", [1, NG + 8], I32)
        chk = sb("chk", [P, 8])
        chk_row = sb("chk_row", [1, 4, NG])
        bst0 = sb("bst0", [P, 6])
        mv_of = sb("mv_of", [P, 2])
        mv0 = sb("mv0", [P, NT, 2])
        veps0 = sb("veps0", [P, NT])
        mrs0 = sb("mrs0", [P, NT])
        rstd0 = sb("rstd0", [P, NT])
        nbias0 = sb("nbias0", [P, NT])
        bst = sb("bst", [P, 2, 6])
        mv = sb("mv", [P, 2, 2])
        veps = sb("veps", [P, 2])
        rstd = sb("rstd", [P, 2])
        nbias = sb("nbias", [P, 2])
        hrow = sb("hrow", [P, D])
        hT = sb("hT", [P, KD, P])
        midT = sb("midT", [P, 2, KD, P])
        ysum = sb("ysum", [P, 2, D])
        yrow = sb("yrow", [P, 2, D])
        ix = sb("ix", [P, 2, GROUP], I32)
        msgs = sb("msgs", [P, 2, GROUP, D])
        oh = sb("oh", [P, 2, GROUP, P])
        tg = sb("tg", [P, 6, P])
        cell = sb("cell", [P, 2, P])
        tcell = sb("tcell", [P, 2, P])
        hn = sb("hn", [P, 2, P])
        x1T = sb("x1T", [P, P])
        x2T = sb("x2T", [P, P])
        grow = sb("grow", [P, D])
        onep = sb("onep", [P, 1])
        wloc = sb("wloc", [P, GROUP])
        scol = sb("scol", [P, 2, GROUP])
        same = sb("same", [P, 2, GROUP, P])
        ohw = oh
        ohw_first = [ih_raw[:, 0:4, :].rearrange("p c i -> p (c i)").rearrange("p (j n) -> p j n", n=P),
                     rel_raw.rearrange("p r c i -> p (r c i)").rearrange("p (j n) -> p j n", n=P)]
        prior = sb("prior", [P, GROUP, P])
        dup = sb("dup", [P, GROUP])
        sidx_f = sb("sidx_f", [P, GROUP])
        sidx = sb("sidx", [P, ET], I32)
        sx = sb("sx", [P, 2, GROUP], I32)
        m_sb = sb("m_sb", [P, 2, GROUP, P])
        hwin = sb("hwin", [P, 2, D])
        comb = sb("comb", [P, 2, GROUP, D])
        b_raw, b_rest = (comb[0:3, 0, a:b, :].rearrange("p (n r) d -> p n r d", r=2) for a, b in ((0, 2), (2, 6)))
        b_acc = comb[0:3, 1, 0:6, :].rearrange("p (n r) d -> p n r d", r=2)
        def accumulator_rows(*buffers):
            flat = [b.rearrange("p a b -> p (a b)") for b in buffers]
            n = ACCS // len(flat)
            return [b[:, k * 2 * D:(k + 1) * 2 * D].rearrange("p (u d) -> p u d", u=2) for b in flat for k in range(n)]

        fa = [accumulator_rows(msgs[:, 0]), accumulator_rows(msgs[:, 1]),
              accumulator_rows(m_sb.rearrange("p b j e -> p b (j e)")),
              accumulator_rows(prior, rel_raw.rearrange("p r c i -> p (r c) i"))]
        AHEAD = len(fa)

        def pair_of(buffer, slot):
            return buffer.rearrange("p a b -> p (a b)")[:, slot * 2 * D:(slot + 1) * 2 * D].rearrange("p (u d) -> p u d", u=2)

        f_s01 = pair_of(comb[:, 0], 0)
        f_s23 = [pair_of(comb[:, 0], 1 + q) for q in range(2)]
        f_tot = [pair_of(comb[:, 1], q) for q in range(2)]
        f_rT = [pair_of(comb[:, 1], 2 + q) for q in range(2)]
        f_r = [pair_of(oh[:, 0], q) for q in range(2)]
        f_t23 = pair_of(oh[:, 1], 1)
        f_q = [pair_of(same[:, 0], q) for q in range(2)]
        f_o = [pair_of(same[:, 1], q) for q in range(2)]

        bank = [ctx.enter_context(nc.psum_tensor(f"bank{i}", [P, 512], F32)) for i in range(8)]

        s_xin = [sem(f"s_xin{i}") for i in range(3)]
        s_edges = sem("s_edges"); s_wrel = sem("s_wrel"); s_bias = sem("s_bias"); s_wts = sem("s_wts")
        s_pad = sem("s_pad"); s_zero = sem("s_zero"); s_zrow = sem("s_zrow"); s_aggz = sem("s_aggz")
        s_const = sem("s_const"); s_const_step = sem("s_const_step")
        s_relps = sem("s_relps"); s_relT = sem("s_relT")
        s_ef = sem("s_ef"); s_eps_ps = sem("s_eps_ps"); s_eT = sem("s_eT")
        s_base_ps = sem("s_base_ps"); s_base = sem("s_base"); s_prep = sem("s_prep")
        s_viol = sem("s_viol"); s_ctrl = sem("s_ctrl"); s_gidx = sem("s_gidx")
        s_wps = sem("s_wps"); s_wT = sem("s_wT"); s_gb = sem("s_gb"); s_brows = sem("s_brows")
        s_stats0 = sem("s_stats0"); s_aggr0 = sem("s_aggr0"); s_veps0 = sem("s_veps0"); s_rstd0 = sem("s_rstd0")
        s_mv_of = sem("s_mv_of"); s_mrs0 = sem("s_mrs0"); s_nbias0 = sem("s_nbias0")
        s_stats = sem("s_stats"); s_aggr = sem("s_aggr"); s_veps = sem("s_veps"); s_rstd = sem("s_rstd"); s_nbias = sem("s_nbias")
        s_hrow = sem("s_hrow"); s_tr = sem("s_tr"); s_hT = sem("s_hT"); s_a = sem("s_a"); s_mid = sem("s_mid")
        s_b = sem("s_b"); s_ysum = sem("s_ysum"); s_yrow = sem("s_yrow")
        s_ystored = [sem(f"s_ystored{r}") for r in range(2)]
        s_staged = [sem(f"s_staged{b}") for b in range(2)]
        s_gathered = [[sem(f"s_gathered{b}{h}") for h in range(2)] for b in range(2)]
        s_oh = sem("s_oh"); s_summed = sem("s_summed"); s_added = sem("s_added")
        s_gates = sem("s_gates"); s_tg = sem("s_tg"); s_cell = sem("s_cell"); s_tcell = sem("s_tcell")
        s_hn = sem("s_hn"); s_w1 = sem("s_w1"); s_x1 = sem("s_x1"); s_w2 = sem("s_w2"); s_x2 = sem("s_x2")
        s_w3 = sem("s_w3"); s_xr = sem("s_xr"); s_hrow1 = sem("s_hrow1")
        s_tr1 = sem("s_tr1"); s_hT1 = sem("s_hT1"); s_g = sem("s_g"); s_grow = sem("s_grow"); s_gsc = sem("s_gsc")
        s_off = sem("s_off")
        s_gstored = [sem(f"s_gstored{n}") for n in range(2)]
        g_staged = sem("g_staged"); g_gathered = sem("g_gathered"); g_loc = sem("g_loc"); g_oh = sem("g_oh")
        g_summed = sem("g_summed"); g_added = sem("g_added")
        s_scol = sem("s_scol"); s_srow = sem("s_srow"); s_same = sem("s_same"); s_eq = sem("s_eq")
        s_ohw = sem("s_ohw"); s_prior = sem("s_prior"); s_dup = sem("s_dup"); s_dupm = sem("s_dupm")
        s_sidx = sem("s_sidx"); s_m = sem("s_m"); s_mcopied = sem("s_mcopied"); s_comb = sem("s_comb")
        s_combsb = sem("s_combsb")
        s_hwin = [sem(f"s_hwin{b}") for b in range(2)]
        s_passed = sem("s_passed")
        s_scattered = [sem(f"s_scattered{k}") for k in range(ACCS)]
        s_sstaged = [sem(f"s_sstaged{b}") for b in range(2)]
        g_staged2 = sem("g_staged2"); g_gathered2 = sem("g_gathered2")
        f_loaded = [sem(f"f_loaded{q}") for q in range(len(fa))]
        l_s23 = sem("l_s23"); l_s01 = sem("l_s01"); l_t23 = sem("l_t23"); l_tot = sem("l_tot"); l_turned = sem("l_turned")
        l_rT = sem("l_rT"); l_prod = sem("l_prod"); l_r = sem("l_r"); l_stats = sem("l_stats")
        l_aggr = sem("l_aggr"); l_veps = sem("l_veps"); l_rstd = sem("l_rstd")
        l_q = sem("l_q"); l_out = sem("l_out")
        l_stored = [sem(f"l_stored{q}") for q in range(2)]
        go_aggr = sem("go_aggr"); go_scale = sem("go_scale"); go_gather = sem("go_gather")
        go_windows = sem("go_windows"); go_stage = sem("go_stage")

        block = ctx.enter_context(nc.Block())

        NPT = (NT + 1) // 2
        assert NT == 2 * NPT - 1 and NPT % AHEAD == 1
        X_LOADS = [(0, 3), (3, 10), (10, NT - 1)]
        LEAD = X_LOADS[0][1]
        MID = 8
        N_CLEARED = 16 * (NT * ACCS + ACCS + 1)
        EARLY = NT - LAG
        G_EARLY = EARLY - 1
        assert LAG == 3
        NSLOT = 9

        def flag_of(e):
            e.wait_ge(s_ctrl, 2)
            return e.value_load(ctrl[0:1, FLAG:FLAG + 1], min_val=0, max_val=1)

        def weighted(i, b):
            return ohw_first[b] if isinstance(i, int) and i == 0 else ohw[:, b]

        @block.sync
        def _(sp):
            def load_x(n):
                a, b = X_LOADS[n]
                sp.dma_start(xr[:, a:b, :], x[a * P:b * P, :].rearrange("(t p) d -> p t d", p=P)).then_inc(s_xin[n], 16)

            load_x(0)
            for r in range(2):
                sp.dma_start(rel_raw[:, r], W_rel[r].rearrange("(c p) i -> p c i", p=P)).then_inc(s_wrel, 16)
            sp.wait_ge(s_bias, 16 * 6)
            load_x(1)
            load_x(2)
            sp.wait_ge(s_pad, 3)
            sp.dma_start(xr[0:LAST, NT - 1, :], x[(NT - 1) * P:NODES, :]).then_inc(s_xin[2], 16)
            for n, a in enumerate((src, dst, edge_type_2, edge_weight)):
                e, c = (e_int[:, n], None) if n < 3 else (e_w, None)
                sp.dma_start(e[:, 0:EC - 1, :], a[0:FULL * P].rearrange("(c p e) -> p c e", p=P, e=P)).then_inc(s_edges, 16)
                sp.dma_start(e[0:RT - 1, EC - 1, :], a[FULL * P:(ET - 1) * P].rearrange("(p e) -> p e", e=P)).then_inc(s_edges, 16)
                sp.dma_start(e[RT - 1:RT, EC - 1, 0:PART], a[(ET - 1) * P:EDGES].unsqueeze(0)).then_inc(s_edges, 16)
                if n < 2:
                    sp.dma_start(e[RT - 1:RT, EC - 1, PART:P], a[EDGES - (P - PART):EDGES].unsqueeze(0)).then_inc(s_edges, 16)
            loads = [(ih_raw[:, 0:2, :], W_ih[0:D, :].rearrange("(c p) i -> p c i", p=P)),
                     (ih_raw[:, 2:6, :], W_ih[2 * D:4 * D, :].rearrange("(c p) i -> p c i", p=P)),
                     (w1_raw[:, :], W1), (w2_raw[:, :], W2),
                     (w3_raw[:, :, :], W3.rearrange("(c p) i -> p c i", p=P)),
                     (gw1[:, :, :], G_W1.rearrange("(k p) o -> p k o", p=P)),
                     (gw2[:, :, :], G_W2.rearrange("(k p) o -> p k o", p=P)),
                     (b_raw[:, 0, 0, :], b3.unsqueeze(0).to_broadcast([3, D])),
                     (b_raw[:, 0, 1, :], G_b2.unsqueeze(0).to_broadcast([3, D])),
                     (gb1_b[:, :], G_b1.unsqueeze(0).to_broadcast([P, D])),
                     (scale_b[:, :], G_scale.unsqueeze(0).to_broadcast([P, D])),
                     (offset_b[:, :], G_offset.unsqueeze(0).to_broadcast([P, D])),
                     (eps_b[:, :], G_eps.unsqueeze(0).to_broadcast([P, 1]))]
            assert len(loads) == N_WTS
            sp.dma_start(msg_table[ZROW:ZROW + 1, :], zeros[0:1, :]).then_inc(s_zrow, 16)

            def store_messages(t, rows):
                for r in range(2):
                    sp.wait_ge(s_yrow, t * 2 + (r + 1))
                    sp.dma_start(msg_table[bass.ds(t * P + r * NODES, rows), :],
                                 yrow[0:rows, r, :]).then_inc(s_ystored[r], 16)

            for t in range(4):
                store_messages(t, P)
                for to, of in loads[t::4]:
                    sp.dma_start(to, of).then_inc(s_wts, 16)
            with sp.Fori(4, NT - 1) as t:
                store_messages(t, P)
            sp.wait_ge(s_gidx, 1)
            for b in range(2):
                sp.dma_start(ix[:, b, :], gidx[:, b * GROUP:(b + 1) * GROUP]).then_inc(s_staged[b], 16)
            store_messages(NT - 1, LAST)

            def store_g(w):
                sp.wait_ge(s_grow, w + 1)
                sp.dma_start(g_table[bass.ds(w * P, P), :], grow[:, :]).then_inc(s_gstored[w >= G_EARLY if isinstance(w, int) else 0], 16)

            def clear_rows(w):
                for k in range(ACCS):
                    sp.dma_start(acc[k][bass.ds(w * P, P), :], zeros[:, :]).then_inc(s_zero, 16)

            def clear_spare_rows():
                for to in [acc[k][NT * P:ROWS, :] for k in range(ACCS)] + [g_table[NT * P:ROWS, :]]:
                    sp.dma_start(to, zeros[:, :]).then_inc(s_zero, 16)

            def stage_rows(i, b, fresh=False):
                sp.wait_ge(s_sidx, i * 2 + b + 1)
                sp.sem_inc(go_stage, 1)
                if not fresh:
                    sp.wait_ge(s_passed, i * (2 * GROUP) + (b * GROUP + ACCS))
                    sp.sem_inc(go_stage, 1)
                sp.dma_start(sx[:, b, :], sidx[:, bass.ds(i * (2 * GROUP) + b * GROUP, GROUP)]).then_inc(s_sstaged[b], 16)

            flag = flag_of(sp)
            with sp.If(flag < 1):
                def stage(i):
                    for b in range(2):
                        for h in range(2):
                            sp.wait_ge(s_gathered[b][h], i * (8 * GROUP))
                        sp.dma_start(ix[:, b, :], gidx[:, bass.ds(i * (2 * GROUP) + b * GROUP, GROUP)]).then_inc(s_staged[b], 16)

                with sp.Fori(0, LAG + 1) as i:
                    stage(i + 1)
                    clear_rows(i)
                with sp.Fori(LAG + 1, NPAIR - 1) as i:
                    stage(i + 1)
                    clear_rows(i)
                    store_g(i - (LAG + 1))
                clear_spare_rows()
                def load_window(i, b):
                    base = sp.value_load(ctrl[0:1, bass.ds(i * 2 + b, 1)], min_val=0, max_val=NODES - 1)
                    sp.wait_ge(s_comb, i * 4 + (2 * b + 2))
                    sp.dma_start(hwin[:, b, :], g_table[bass.ds(base, P), :]).then_inc(s_hwin[b], 16)

                sp.wait_ge(s_gstored[0], 16 * G_EARLY)
                load_window(0, 0)
                load_window(0, 1)
                sp.wait_ge(s_zero, N_CLEARED)
                stage_rows(0, 0, fresh=True)
                store_g(G_EARLY)
                load_window(1, 0)
                stage_rows(0, 1, fresh=True)
                store_g(EARLY)
                load_window(1, 1)
                stage_rows(1, 0)
                store_g(NT - 2)
                stage_rows(1, 1)
                load_window(2, 0)
                store_g(NT - 1)
                sp.wait_ge(s_gstored[1], 16 * (NT - G_EARLY))
                with sp.Fori(2, NPAIR - 1) as i:
                    load_window(i, 1)
                    stage_rows(i, 0)
                    load_window(i + 1, 0)
                    stage_rows(i, 1)
                load_window(NPAIR - 1, 1)
                stage_rows(NPAIR - 1, 0)
                stage_rows(NPAIR - 1, 1)
            with sp.Else():
                with sp.Fori(0, NT) as w:
                    clear_rows(w)
                clear_spare_rows()
                sp.wait_ge(s_staged[0], 16)
                with sp.Fori(0, NG) as g:
                    sp.wait_ge(g_gathered, g * (16 * GROUP))
                    sp.dma_start(ix[:, 0, :], gidx[:, bass.ds(g * GROUP, GROUP)]).then_inc(g_staged, 16)
                sp.wait_ge(s_zero, N_CLEARED)
                with sp.Fori(0, G_EARLY) as w:
                    store_g(w)
                for w in range(G_EARLY, NT):
                    store_g(w)
                with sp.Fori(0, NPAIR) as i:
                    for b in range(2):
                        sp.wait_ge(g_gathered2, i * (32 * GROUP) + b * (16 * GROUP))
                        sp.dma_start(ix[:, 1, :], dst_i[:, bass.ds(i * (2 * GROUP) + b * GROUP, GROUP)]).then_inc(g_staged2, 16)
                        stage_rows(i, b)

            def load_sums(p):
                q4, n = p % AHEAD, (1 if p == NPT - 1 else 2)
                if p >= AHEAD:
                    sp.wait_ge(l_tot, p - AHEAD + 3)
                for k in range(ACCS):
                    if p == 0:
                        sp.wait_ge(s_scattered[k], 16 * (ET // ACCS))
                    sp.dma_start(fa[q4][k][:, 0:n, :],
                                 acc[k][p * 2 * P:(p * 2 + n) * P, :].rearrange("(u p) d -> p u d", p=P)).then_inc(f_loaded[q4], 16)

            def store_out(p, q):
                sp.wait_ge(l_out, p + 2)
                sp.dma_start(out[bass.ds(p * (2 * P), 2 * P), :].rearrange("(u p) d -> p u d", p=P), f_o[q]).then_inc(l_stored[q], 16)

            for p in range(AHEAD + 3):
                load_sums(p)
            for p in range(NPT - 1):
                store_out(p, p % 2)
                if p + AHEAD + 3 < NPT:
                    load_sums(p + AHEAD + 3)
            sp.wait_ge(l_out, NPT + 1)
            sp.dma_start(out[(NT - 1) * P:NODES, :], f_o[0][0:LAST, 0, :]).then_inc(l_stored[0], 16)
            sp.wait_ge(l_stored[0], 16 * (NPT // 2 + 1))
            sp.wait_ge(l_stored[1], 16 * (NPT // 2))

        @block.gpsimd
        def _(pool):
            pool.memset(zeros[:, :], 0.0)
            pool.memset(e_int[0:RT, 2, EC - 1, :], 2).then_inc(s_pad, 1)
            pool.memset(e_w[0:RT, EC - 1, :], 0.0).then_inc(s_pad, 1)
            pool.memset(xr[:, NT - 1, :], 0.0).then_inc(s_pad, 1)
            pool.memset(ident[:, :], 0.0)
            pool.memset(row0[:, :], 0.0)
            pool.memset(earlier[:, :], 1.0)
            pool.memset(ones[:, :], 1.0)
            pool.memset(ones_bf[:, :], 1.0)
            pool.memset(minus_half[:, :], -0.5)
            pool.memset(minus_one[:, :], -1.0)
            pool.memset(ln_eps[:, :], 1e-5)
            pool.iota(iota_row[:, :], [[1, P]], base=0, channel_multiplier=0, allow_small_or_imprecise_dtypes=True)
            pool.iota(wbase[:, :], [[P, NT]], base=0, channel_multiplier=0, allow_small_or_imprecise_dtypes=True)
            pool.iota(spare[:, :], [[1, 1]], base=NODES, channel_multiplier=1,
                      allow_small_or_imprecise_dtypes=True).then_inc(s_const_step, 1)
            pool.wait_ge(s_const_step, 1)
            pool.affine_select(out=ident[:, :], in_=ident[:, :], compare_op=ALU.not_equal, fill=1.0, base=0,
                               pattern=[[-1, P]], channel_multiplier=1)
            pool.affine_select(out=row0[:, :], in_=row0[:, :], compare_op=ALU.not_equal, fill=1.0, base=0,
                               pattern=[[0, P]], channel_multiplier=1)
            pool.affine_select(out=earlier[:, :], in_=earlier[:, :], compare_op=ALU.is_gt, fill=0.0, base=0,
                               pattern=[[-1, P]], channel_multiplier=1).then_inc(s_const, 1)

            def scale_bias0(t):
                col = bass.ds(t, 1)
                pool.wait_ge(s_aggr0, t + 1)
                pool.tensor_tensor(veps0[:, col], mv0[:, col, 1:2].rearrange("p t a -> p (t a)"), ln_eps[:, :], ALU.add).then_inc(s_veps0, 1)
                pool.wait_ge(s_veps0, t + 1)
                pool.tensor_tensor(rstd0[:, col], veps0[:, col], minus_half[:, 0:1], ALU.pow).then_inc(s_rstd0, 1)
                pool.wait_ge(s_rstd0, t + 1)
                pool.tensor_tensor(mrs0[:, col], mv0[:, col, 0:1].rearrange("p t a -> p (t a)"), rstd0[:, col], ALU.mult).then_inc(s_mrs0, 1)
                pool.wait_ge(s_mrs0, t + 1)
                pool.tensor_tensor(nbias0[:, col], mrs0[:, col], minus_one[:, :], ALU.mult).then_inc(s_nbias0, 1)

            with pool.Fori(0, LEAD + 2) as t:
                scale_bias0(t)
            pool.wait_ge(s_edges, 16 * 14)
            for n in range(3):
                pool.tensor_copy(e_f[:, n, 0:EC - 1, :], e_int[:, n, 0:EC - 1, :])
                pool.tensor_copy(e_f[0:RT, n, EC - 1, :], e_int[0:RT, n, EC - 1, :]).then_inc(s_ef, 1)
                scale_bias0(LEAD + 2 + n)
            assert MID == LEAD + 5
            for k in range(KD):
                pool.memset(aggT[:, k, :], 0.0).then_inc(s_aggz, 1)
                scale_bias0(MID + k)
            with pool.Fori(MID + KD, NT) as t:
                scale_bias0(t)
            pool.sem_inc(s_passed, GROUP)

            def gather(table, index, b, signal, j0=0, j1=GROUP):
                for j in range(j0, j1):
                    pool.indirect_dma_start(msgs[:, b, j, :], None, table,
                                            bass.IndirectOffsetOnAxis(ap=ix[:, index, j:j + 1], axis=0)).then_inc(signal, 16)

            def scatter_half(i, b, h):
                if h == 0:
                    pool.wait_ge(s_sstaged[b], i * 16 + 16)
                pool.wait_ge(s_combsb, i * 4 + (2 * b + h + 3))
                for j in range(h * ACCS, (h + 1) * ACCS):
                    k = j % ACCS
                    pool.wait_ge(s_scattered[k], i * 64 + (32 * b + 16 * h))
                    pool.sem_inc(s_passed, 1)
                    pool.indirect_dma_start(acc[k], bass.IndirectOffsetOnAxis(ap=sx[:, b, j:j + 1], axis=0),
                                            comb[:, b, j, :], None, compute_op=ALU.add).then_inc(s_scattered[k], 16)

            def scatter(i, b):
                scatter_half(i, b, 0)
                scatter_half(i, b, 1)

            def root(n):
                pool.wait_ge(s_veps, n + 1)
                pool.tensor_tensor(rstd[:, 1:2], veps[:, 1:2], minus_half[:, 0:1], ALU.pow).then_inc(s_rstd, 1)

            for r in range(2):
                pool.wait_ge(s_ystored[r], 16 * NT)
            pool.wait_ge(s_zrow, 16)
            flag = flag_of(pool)
            with pool.If(flag < 1):
                def gather_pair(i, v):
                    for b in range(2):
                        pool.wait_ge(s_staged[b], i * 16 + 16)
                        pool.wait_ge(s_summed, i * 2 + b + 1)
                        pool.sem_inc(go_gather, 1)
                        gather(msg_table, b, b, s_gathered[b][0], 0, GROUP // 2)
                        if b == 1 and v is not None:
                            root(v)
                        gather(msg_table, b, b, s_gathered[b][1], GROUP // 2, GROUP)

                for i in range(LAG + 1):
                    gather_pair(i, None)
                with pool.Fori(LAG + 1, NPAIR) as i:
                    gather_pair(i, i - (LAG + 1))
                scatter_half(0, 0, 0)
                root(EARLY)
                scatter_half(0, 0, 1)
                scatter_half(0, 1, 0)
                scatter_half(0, 1, 1)
                root(NT - 2)
                scatter_half(1, 0, 0)
                root(NT - 1)
                scatter_half(1, 0, 1)
                scatter(1, 1)
                with pool.Fori(2, NPAIR) as i:
                    scatter(i, 0)
                    scatter(i, 1)
            with pool.Else():
                with pool.Fori(0, NG) as g:
                    pool.wait_ge(g_staged, g * 16 + 16)
                    pool.wait_ge(g_summed, g * NT)
                    pool.sem_inc(go_gather, 1)
                    gather(msg_table, 0, 0, g_gathered)
                with pool.Fori(0, NT) as w:
                    root(w)
                with pool.Fori(0, NPAIR) as i:
                    for b in range(2):
                        pool.wait_ge(s_gstored[0], 16 * G_EARLY)
                        pool.wait_ge(s_gstored[1], 16 * (NT - G_EARLY))
                        pool.wait_ge(g_staged2, i * 32 + (16 * b + 16))
                        pool.wait_ge(s_comb, i * 4 + (2 * b + 4))
                        pool.sem_inc(go_gather, 1)
                        gather(g_table, 1, 1, g_gathered2)
                        scatter(i, b)
            pool.nop()

            def sum23(p, q4, n):
                pool.wait_ge(f_loaded[q4], (p - q4) * 16 + 16 * ACCS)
                pool.wait_ge(l_s23, p)
                pool.tensor_tensor(f_t23[:, 0:n, :], fa[q4][2][:, 0:n, :], fa[q4][3][:, 0:n, :], ALU.add).then_inc(l_t23, 1)
                pool.wait_ge(l_t23, p + 1)
                pool.wait_ge(l_tot, p + 1)
                own = aggT[:, :, bass.ds(p * (2 * P), n * P)].rearrange("p k (u n) -> p u k n", u=n)
                pool.tensor_tensor(f_s23[q4 % 2][:, 0:n, :].rearrange("p u (k n) -> p u k n", k=KD),
                                   f_t23[:, 0:n, :].rearrange("p u (k n) -> p u k n", k=KD), own, ALU.add).then_inc(l_s23, 1)

            def row_root(p, n):
                pool.wait_ge(l_veps, p + 1)
                pool.sem_inc(go_scale, 1)
                pool.wait_ge(l_out, p + 1)
                pool.tensor_tensor(rstd[:, 0:n], veps[:, 0:n], minus_half[:, 0:n], ALU.pow).then_inc(l_rstd, 1)

            sum23(0, 0, 2)
            sum23(1, 1, 2)
            with pool.Fori(0, NPT // AHEAD - 1) as i:
                for q4 in range(AHEAD):
                    sum23(i * AHEAD + (q4 + 2), (q4 + 2) % AHEAD, 2)
                    row_root(i * AHEAD + q4, 2)
            for p in range(NPT - 1 - AHEAD, NPT - 2):
                sum23(p + 2, (p + 2) % AHEAD, 1 if p + 2 == NPT - 1 else 2)
                if p < NPT - 3:
                    row_root(p, 2)
            row_root(NPT - 3, 2)
            row_root(NPT - 2, 2)
            row_root(NPT - 1, 1)

        @block.scalar
        def _(act):
            act.dma_start(bias_rows[0:4, :], b_rel.rearrange("r (k p) -> (r k) p", p=P)).then_inc(s_bias, 16)
            act.dma_start(brel_b[:, :, :], b_rel.unsqueeze(0).to_broadcast([P, 2, D])).then_inc(s_bias, 16)
            act.dma_start(bias_rows[4:12, :], b_ih.rearrange("(k p) -> k p", p=P)).then_inc(s_bias, 16)
            act.dma_start(bias_rows[12:20, :], b_hh.rearrange("(k p) -> k p", p=P)).then_inc(s_bias, 16)
            act.dma_start(bias_rows[20:21, :], b1.unsqueeze(0)).then_inc(s_bias, 16)
            act.dma_start(bias_rows[21:22, :], b2.unsqueeze(0)).then_inc(s_bias, 16)

            def norm_row(t):
                act.wait_ge(s_tr, t)
                act.wait_ge(s_nbias0, t + 1)
                act.activation(hrow[:, :], xr[:, bass.ds(t, 1), :].rearrange("p a d -> p (a d)"), ACT.Relu,
                               bias=nbias0[:, bass.ds(t, 1)], scale=rstd0[:, bass.ds(t, 1)]).then_inc(s_hrow, 1)

            def copy_hT(t):
                act.wait_ge(s_tr, t + 1)
                act.wait_ge(s_a, t * 2)
                act.copy(hT[:, :, :].rearrange("p k n -> p (k n)"), bank[0][:, 0:D]).then_inc(s_hT, 1)

            def mid(t, r):
                act.wait_ge(s_a, t * 2 + (r + 1))
                act.wait_ge(s_b, t * 2)
                for o in range(KD):
                    last = act.activation(midT[:, r, o, :], bank[2 + r][:, o * P:(o + 1) * P], ACT.Relu,
                                          bias=bias[:, 2 * r + o:2 * r + o + 1])
                last.then_inc(s_mid, 1)

            def messages(t, r):
                act.wait_ge(s_ysum, t * 2 + (r + 1))
                act.wait_ge(s_ystored[r], t * 16)
                act.activation(yrow[:, r, :], ysum[:, r, :], ACT.Relu).then_inc(s_yrow, 1)

            norm_row(0)
            copy_hT(0)
            act.wait_ge(s_relT, 3)

            def table_tile(t, before, more):
                if more:
                    norm_row(t + 1)
                if before is not None:
                    messages(before, 1)
                mid(t, 0)
                mid(t, 1)
                if more:
                    copy_hT(t + 1)
                messages(t, 0)

            table_tile(0, None, True)
            with act.Fori(1, NT - 1) as t:
                table_tile(t, t - 1, True)
            table_tile(NT - 1, NT - 2, False)
            messages(NT - 1, 1)

            def gates(w):
                act.wait_ge(s_gates, w + 1)
                act.wait_ge(s_hn, w)
                for c in range(6):
                    half = c // 2 != 1
                    col = (0, 1, 4, 5, 6, 7)[c]
                    last = act.activation(tg[:, c, :], bank[2 + c // 4][:, (c % 4) * P:(c % 4 + 1) * P], ACT.Tanh,
                                          bias=(gate_half if half else gate_bias)[:, col:col + 1],
                                          scale=0.5 if half else 1.0)
                last.then_inc(s_tg, 1)

            def cell_tanh(w):
                act.wait_ge(s_cell, w + 1)
                act.wait_ge(s_hn, w)
                act.activation(tcell[:, :, :].rearrange("p k n -> p (k n)"), cell[:, :, :].rearrange("p k n -> p (k n)"),
                               ACT.Tanh, scale=0.5).then_inc(s_tcell, 1)

            def mlp1(w):
                act.wait_ge(s_w1, w + 1)
                act.wait_ge(s_w2, w)
                act.activation(x1T[:, :], bank[3][:, 2 * P:3 * P], ACT.Relu, bias=bias[:, 20:21], scale=0.5).then_inc(s_x1, 1)

            def mlp2(w):
                act.wait_ge(s_w2, w + 1)
                act.wait_ge(s_w3, w)
                act.activation(x2T[:, :], bank[3][:, 3 * P:4 * P], ACT.Relu, bias=bias[:, 21:22]).then_inc(s_x2, 1)

            def norm_row1(w):
                act.wait_ge(s_tr1, w)
                act.wait_ge(s_nbias, w + 1)
                act.activation(hrow[:, :], xr[:, bass.ds(w, 1), :].rearrange("p a d -> p (a d)"), ACT.Relu,
                               bias=nbias[:, 1:2], scale=rstd[:, 1:2]).then_inc(s_hrow1, 1)

            def copy_hT1(w):
                act.wait_ge(s_tr1, w + 1)
                act.wait_ge(s_g, w)
                act.copy(hT[:, :, :].rearrange("p k n -> p (k n)"), bank[5][:, 0:D]).then_inc(s_hT1, 1)

            def g_rows(w):
                act.wait_ge(s_gsc, w + 1)
                late = isinstance(w, int) and w > G_EARLY
                act.wait_ge(s_gstored[late], (w - G_EARLY if late else w) * 16)
                act.copy(grow[:, :], bank[5][:, D:2 * D]).then_inc(s_grow, 1)

            def node_tile(w, v):
                if w is not None:
                    gates(w)
                    cell_tanh(w)
                if v is not None:
                    norm_row1(v)
                if w is not None:
                    mlp1(w)
                if v is not None:
                    copy_hT1(v)
                    g_rows(v)
                if w is not None:
                    mlp2(w)

            def copy_m(i, b, bk=2):
                act.wait_ge(s_m, i * 2 + (b + 2))
                act.wait_ge(s_comb, i * 4 + (2 * b + 2))
                for c in range(2):
                    last = act.copy(m_sb[:, b, 4 * c:4 * c + 4, :].rearrange("p j e -> p (j e)"), bank[bk + c][:, :])
                last.then_inc(s_mcopied, 1)

            def copy_half(i, b, h, bk):
                act.wait_ge(s_comb, i * 4 + (2 * b + h + 5))
                act.wait_ge(s_passed, i * (2 * GROUP) + (b * GROUP + h * ACCS))
                for c in range(2):
                    last = act.copy(comb[:, b, 4 * h + 2 * c:4 * h + 2 * c + 2, :].rearrange("p j d -> p (j d)"), bank[bk + c][:, :])
                last.then_inc(s_combsb, 1)

            def copy_comb(i, b):
                copy_half(i, b, 0, 4)
                copy_half(i, b, 1, 6)

            act.sem_inc(s_combsb, 2)
            flag = flag_of(act)
            with act.If(flag < 1):
                node_tile(0, None)
                with act.Fori(1, EARLY) as w:
                    node_tile(w, w - 1)
                copy_m(0, 0, 6)
                w = EARLY
                gates(w)
                cell_tanh(w)
                mlp1(w)
                copy_half(0, 0, 0, 6)
                mlp2(w)
                norm_row1(w - 1)
                copy_hT1(w - 1)
                g_rows(w - 1)
                copy_half(0, 0, 1, 6)
                copy_m(0, 1, 6)
                w = NT - 2
                gates(w)
                cell_tanh(w)
                copy_half(0, 1, 0, 6)
                mlp1(w)
                copy_half(0, 1, 1, 0)
                mlp2(w)
                norm_row1(w - 1)
                copy_hT1(w - 1)
                g_rows(w - 1)
                w = NT - 1
                gates(w)
                cell_tanh(w)
                copy_m(1, 0, 0)
                copy_half(1, 0, 0, 0)
                mlp1(w)
                mlp2(w)
                norm_row1(w - 1)
                copy_hT1(w - 1)
                g_rows(w - 1)
                copy_half(1, 0, 1, 6)
                copy_m(1, 1, 0)
                norm_row1(w)
                copy_hT1(w)
                copy_half(1, 1, 0, 6)
                copy_m(2, 0)
                copy_half(1, 1, 1, 0)
                g_rows(w)
                with act.Fori(2, NPAIR - 1) as i:
                    copy_comb(i, 0)
                    copy_m(i, 1)
                    copy_comb(i, 1)
                    copy_m(i + 1, 0)
                copy_comb(NPAIR - 1, 0)
                copy_m(NPAIR - 1, 1)
                copy_comb(NPAIR - 1, 1)
            with act.Else():
                with act.Fori(0, G_EARLY) as w:
                    node_tile(w, None)
                    node_tile(None, w)
                for w in range(G_EARLY, NT):
                    node_tile(w, None)
                    node_tile(None, w)
                with act.Fori(0, NPAIR) as i:
                    copy_comb(i, 0)
                    copy_comb(i, 1)
            act.nop()

            def relu_turned(p, q, n):
                act.wait_ge(l_turned, p + 1)
                act.wait_ge(l_prod, p + 1)
                act.activation(f_rT[q].rearrange("p u d -> p (u d)")[:, 0:KD * n * P], bank[q][:, 0:KD * n * P],
                               ACT.Relu).then_inc(l_rT, 1)

            def relu_rows(p, q, n):
                act.wait_ge(l_prod, p + 3)
                act.wait_ge(l_q, p)
                act.activation(f_r[q][:, 0:n, :].rearrange("p u d -> p (u d)"), bank[2 + q][:, 0:n * D], ACT.Relu).then_inc(l_r, 1)

            relu_turned(0, 0, 2)
            with act.Fori(0, NPT // 2 - 1) as i:
                for q in range(2):
                    relu_rows(i * 2 + q, q, 2)
                    relu_turned(i * 2 + (q + 1), 1 - q, 2)
            relu_rows(NPT - 3, 0, 2)
            relu_turned(NPT - 2, 1, 2)
            relu_rows(NPT - 2, 1, 2)
            relu_turned(NPT - 1, 0, 1)
            relu_rows(NPT - 1, 0, 1)

        @block.vector
        def _(dve):
            def stats(v, n, which, applied, count, summed=None):
                dve.wait_ge(s_xin[0], 16)
                dve.wait_ge(applied, count)
                if summed is not None:
                    dve.wait_ge(s_xr, summed)
                dve.bn_stats(bst[:, which, :], v).then_inc(s_stats, 1)
                dve.wait_ge(s_stats, n + 1)
                dve.sem_inc(go_aggr, 1)
                dve.bn_aggr(mv[:, which, :], bst[:, which, :]).then_inc(s_aggr, 1)
                dve.wait_ge(s_aggr, n + 1)
                dve.tensor_scalar(veps[:, which:which + 1], mv[:, which, 1:2], 1e-5, None, ALU.add).then_inc(s_veps, 1)

            def x_tile(t):
                return xr[:, bass.ds(t, 1), :].rearrange("p a d -> p (a d)")

            def stats0(t):
                dve.wait_ge(s_aggr0, t)
                dve.sem_inc(go_aggr, 1)
                dve.bn_stats(bst0[:, :], x_tile(t)).then_inc(s_stats0, 1)
                dve.wait_ge(s_stats0, t + 1)
                dve.sem_inc(go_aggr, 1)
                dve.bn_aggr(mv_of[:, :], bst0[:, :]).then_inc(s_mv_of, 1)
                dve.wait_ge(s_mv_of, t + 1)
                dve.tensor_copy(mv0[:, bass.ds(t, 1), :].rearrange("p a s -> p (a s)"), mv_of[:, :]).then_inc(s_aggr0, 1)

            dve.wait_ge(s_xin[0], 16)
            dve.sem_inc(go_aggr, 1)
            for t in range(LEAD):
                stats0(t)
            dve.wait_ge(s_relps, 1)
            dve.tensor_copy(relT[:, 0].rearrange("p k o -> p (k o)"), bank[4][:, :]).then_inc(s_relT, 1)
            dve.wait_ge(s_relps, 2)
            dve.tensor_copy(relT[:, 1].rearrange("p k o -> p (k o)"), bank[5][:, :]).then_inc(s_relT, 1)
            dve.wait_ge(s_relps, 3)
            dve.tensor_copy(bias[:, :], bank[6][:, 0:NB]).then_inc(s_relT, 1)
            dve.wait_ge(s_relT, 3)
            dve.tensor_tensor(gate_bias[:, :], bias[:, 4:12], bias[:, 12:20], ALU.add).then_inc(s_gb, 1)
            dve.wait_ge(s_gb, 1)
            dve.tensor_scalar(gate_half[:, :], gate_bias[:, :], 0.5, None, ALU.mult).then_inc(s_gb, 1)

            def edge_columns():
                for n, to in enumerate((srcT, dstT, typT)):
                    dve.wait_ge(s_eps_ps, n + 1)
                    dve.tensor_copy(to[:, :], bank[(6, 7, 1)[n]][:, 0:ET]).then_inc(s_eT, 1)
                yield
                dve.wait_ge(s_eps_ps, 4)
                dve.tensor_copy(wT[:, :], bank[6][:, 0:ET]).then_inc(s_eT, 1)

                prep = [0]

                def step(ins):
                    prep[0] += 1
                    ins.then_inc(s_prep, 1)
                    dve.wait_ge(s_prep, prep[0])

                dve.wait_ge(s_eT, 4)
                for r in range(2):
                    step(dve.tensor_scalar(isr[:, r, :], typT[:, :], float(r), None, ALU.is_equal))
                    step(dve.scalar_tensor_tensor(out=isr[:, r, :], in0=srcT[:, :], scalar=float(r * NODES - ZROW),
                                                  in1=isr[:, r, :], op0=ALU.add, op1=ALU.mult))
                yield
                step(dve.scalar_tensor_tensor(out=gidx[:, :], in0=isr[:, 0, :], scalar=float(ZROW), in1=isr[:, 1, :],
                                              op0=ALU.add, op1=ALU.add))
                step(dve.tensor_copy(dst_i[:, :], dstT[:, :]))
                step(dve.tensor_scalar(to_spare[:, :], srcT[:, :], -1.0, spare[:, 0:1], ALU.mult, ALU.add))
                dve.tensor_scalar(onep[:, :], eps_b[:, :], 1.0, None, ALU.add).then_inc(s_gidx, 1)
                yield
                dve.wait_ge(s_base_ps, 1)
                dve.tensor_copy(base_f[:, :], bank[7][:, 0:NG]).then_inc(s_base, 1)
                evacuate(0, 2)
                yield
                dve.wait_ge(s_base, 1)
                step(dve.tensor_tensor(loc[:, :, :], dstT[:, :].rearrange("p (g j) -> p g j", j=GROUP),
                                       base_f[:, :].unsqueeze(2).to_broadcast([P, NG, GROUP]), ALU.subtract))
                step(dve.tensor_reduce(chk[:, 0:1], loc[:, :, :].rearrange("p g j -> p (g j)"), AX.X, ALU.max))
                step(dve.tensor_reduce(chk[:, 1:2], loc[:, :, :].rearrange("p g j -> p (g j)"), AX.X, ALU.min))
                step(dve.tensor_scalar(chk[:, 2:3], chk[:, 0:1], float(P - 1), None, ALU.is_gt))
                step(dve.scalar_tensor_tensor(out=chk[:, 3:4], in0=chk[:, 1:2], scalar=0.0, in1=chk[:, 2:3],
                                              op0=ALU.is_lt, op1=ALU.add))
                evacuate(2, 5)
                yield
                step(dve.tensor_tensor(chk_row[:, 0, 0:NG - 1], base_f[0:1, 1:NG], base_f[0:1, 0:NG - 1], ALU.is_lt))
                step(dve.tensor_reduce(chk_row[:, 1, 0:1], chk_row[:, 0, 0:NG - 1], AX.X, ALU.max))
                nw = NPAIR - LAG
                step(dve.scalar_tensor_tensor(out=chk_row[:, 2, 0:nw], in0=wbase[0:1, 0:nw], scalar=float(P),
                                              in1=base_f[0:1, 2 * LAG:NG:2], op0=ALU.add, op1=ALU.is_gt))
                step(dve.tensor_reduce(chk_row[:, 1, 1:2], chk_row[:, 2, 0:nw], AX.X, ALU.max))
                step(dve.scalar_tensor_tensor(out=chk_row[:, 1, 1:2], in0=base_f[0:1, 4:5], scalar=float((G_EARLY - 1) * P),
                                              in1=chk_row[:, 1, 1:2], op0=ALU.is_gt, op1=ALU.add))
                dve.tensor_copy(ctrl[0:1, 0:NG], base_f[0:1, :])
                step(dve.tensor_tensor(chk_row[:, 1, 2:3], chk_row[:, 1, 0:1], chk_row[:, 1, 1:2], ALU.add))
                step(dve.tensor_tensor(chk[0:1, 3:4], chk[0:1, 3:4], chk_row[:, 1, 2:3], ALU.add))
                dve.sem_inc(s_viol, 1)
                evacuate(5, 6)
                yield
                dve.wait_ge(s_viol, 2)
                step(dve.tensor_scalar(ctrl[0:1, FLAG:FLAG + 1], bank[6][0:1, 0:1], 0.0, None, ALU.is_gt))
                dve.sem_inc(s_ctrl, 2)
                yield
                step(dve.tensor_copy(b_part[:, 0], b_raw[:, 0]))
                step(dve.tensor_tensor(b_rest[:, 0], b_raw[:, 0], b_part[:, 0], ALU.subtract))
                step(dve.tensor_copy(b_part[:, 1], b_rest[:, 0]))
                step(dve.tensor_tensor(b_rest[:, 1], b_rest[:, 0], b_part[:, 1], ALU.subtract))
                step(dve.tensor_copy(b_part[:, 2], b_rest[:, 1]))
                yield
                step(dve.tensor_scalar(b_acc[:, 0], b_part[:, 0], ident[0:3, 0:1], None, ALU.mult))
                for n in (1, 2):
                    step(dve.scalar_tensor_tensor(out=b_acc[:, n], in0=b_part[:, n], scalar=ident[0:3, n:n + 1],
                                                  in1=b_acc[:, n - 1], op0=ALU.mult, op1=ALU.add))
                dve.tensor_copy(b_rows[:, :, :], b_acc[:, 2]).then_inc(s_brows, 1)
                yield

            def evacuate(a, b):
                of = [(w3T[:, :], bank[6][:, 0:D]), (w1T[:, :, :].rearrange("p k o -> p (k o)"), bank[1][:, 0:D]),
                      (w2T[:, :], bank[1][:, D:D + P])] + \
                     [(ihT[:, 2 * c:2 * c + 2].rearrange("p c k o -> p (c k o)"), bank[(6, 7, 6)[c]][:, :]) for c in range(3)]
                for n in range(a, b):
                    dve.wait_ge(s_wps, n + 1)
                    dve.tensor_copy(*of[n]).then_inc(s_wT, 1)

            def add_bias(t, r):
                dve.wait_ge(s_b, t * 2 + (r + 1))
                dve.wait_ge(s_yrow, t * 2)
                dve.tensor_tensor(ysum[:, r, :], bank[4 + r][:, 0:D], brel_b[:, r, :], ALU.add).then_inc(s_ysum, 1)

            def table_tile(t, ahead=True):
                if ahead:
                    stats0(t + LEAD)
                add_bias(t, 0)
                add_bias(t, 1)

            dve.wait_ge(s_bias, 16 * 6)
            dve.wait_ge(s_xin[1], 16)
            dve.sem_inc(go_aggr, 1)
            with dve.Fori(0, X_LOADS[1][1] - LEAD) as t:
                table_tile(t)
            dve.wait_ge(s_xin[2], 32)
            dve.sem_inc(go_aggr, 1)
            with dve.Fori(X_LOADS[1][1] - LEAD, MID) as t:
                table_tile(t)
            slots = edge_columns()
            for n in range(NSLOT):
                next(slots)
                table_tile(MID + n)
            with dve.Fori(MID + NSLOT, NT - LEAD) as t:
                table_tile(t)
            with dve.Fori(NT - LEAD, NT) as t:
                table_tile(t, False)
            dve.sem_inc(s_added, 2)
            dve.wait_ge(s_aggz, KD)

            def one_hot(i, b):
                dve.wait_ge(s_summed, i * 2 + (b + 1))
                dve.tensor_tensor(oh[:, b, :, :], iota_row[:, :].unsqueeze(1).to_broadcast([P, GROUP, P]),
                                  loc[:, bass.ds(i * 2 + b, 1), :].rearrange("p a j -> p (a j)").unsqueeze(2).to_broadcast([P, GROUP, P]),
                                  ALU.is_equal).then_inc(s_oh, 1)

            def add_window(i, b):
                base = dve.value_load(ctrl[0:1, bass.ds(i * 2 + b, 1)], min_val=0, max_val=NODES - 1)
                dve.wait_ge(s_summed, i * 2 + (b + 3))
                dve.wait_ge(s_added, i * 2 + (b + 2))
                v = aggT[:, :, bass.ds(base, P)]
                dve.tensor_tensor(v, v, bank[b][:, 0:D].rearrange("p (k n) -> p k n", k=KD), ALU.add).then_inc(s_added, 1)

            def cell_c(w):
                dve.wait_ge(s_tg, w + 1)
                dve.wait_ge(s_tcell, w)
                dve.scalar_tensor_tensor(out=cell[:, :, :], in0=tg[:, 0:2, :], scalar=1.0, in1=tg[:, 2:4, :],
                                         op0=ALU.add, op1=ALU.mult).then_inc(s_cell, 1)

            def cell_h(w):
                dve.wait_ge(s_tcell, w + 1)
                dve.wait_ge(s_w1, w)
                dve.scalar_tensor_tensor(out=hn[:, :, :], in0=tg[:, 4:6, :], scalar=1.0, in1=tcell[:, :, :],
                                         op0=ALU.add, op1=ALU.mult).then_inc(s_hn, 1)

            def residual(w):
                dve.wait_ge(s_w3, w + 1)
                dve.tensor_tensor(x_tile(w), x_tile(w), bank[4][:, 0:D], ALU.add).then_inc(s_xr, 1)
                stats(x_tile(w), w, 1, s_hrow1, w, w + 1)

            def finish_scale(v):
                dve.wait_ge(s_rstd, v + 1)
                dve.scalar_tensor_tensor(out=nbias[:, 1:2], in0=mv[:, 1, 0:1], scalar=-1.0, in1=rstd[:, 1:2],
                                         op0=ALU.mult, op1=ALU.mult).then_inc(s_nbias, 1)

            def own_part(v):
                dve.wait_ge(s_hrow1, v + 1)
                dve.tensor_tensor(x_tile(v), x_tile(v), offset_b[:, :], ALU.add).then_inc(s_off, 1)
                dve.wait_ge(s_g, v + 1)
                dve.scalar_tensor_tensor(out=aggT[:, :, bass.ds(v * P, P)], in0=bank[5][:, D:2 * D].rearrange("p (k n) -> p k n", k=KD),
                                         scalar=onep[:, 0:1], in1=gb1_b[:, :].rearrange("p (k n) -> p k n", k=KD),
                                         op0=ALU.mult, op1=ALU.add).then_inc(s_gsc, 1)

            def sources(i, b, done):
                dve.wait_ge(s_sidx, done)
                dve.tensor_copy(scol[:, b, :], srcT[:, bass.ds(i * (2 * GROUP) + b * GROUP, GROUP)]).then_inc(s_scol, 1)

            def same_source(i, b, used, bk=0):
                dve.wait_ge(s_srow, i * 2 + (b + 1))
                dve.wait_ge(*used(i, b))
                dve.wait_ge(s_prior, i * 2 + b)
                for c in range(2):
                    last = dve.tensor_tensor(same[:, b, 4 * c:4 * c + 4, :], bank[bk + c][:, :].rearrange("p (j e) -> p j e", e=P),
                                             scol[:, b, 4 * c:4 * c + 4].unsqueeze(2).to_broadcast([P, 4, P]), ALU.is_equal)
                last.then_inc(s_same, 1)

            def scatter_rows(i, b):
                dve.wait_ge(s_same, i * 2 + (b + 1))
                dve.wait_ge(s_dup, i * 2 + b)
                dve.tensor_tensor(prior[:, :, :], same[:, b], earlier[:, :].unsqueeze(1).to_broadcast([P, GROUP, P]),
                                  ALU.mult).then_inc(s_prior, 1)
                dve.wait_ge(s_prior, i * 2 + (b + 1))
                dve.wait_ge(s_dupm, i * 2 + b)
                dve.tensor_reduce(dup[:, :], prior[:, :, :], AX.X, ALU.max).then_inc(s_dup, 1)
                dve.wait_ge(s_dup, i * 2 + (b + 1))
                dve.wait_ge(s_sidx, i * 2 + b)
                dve.tensor_tensor(sidx_f[:, :], dup[:, :], to_spare[:, bass.ds(i * (2 * GROUP) + b * GROUP, GROUP)],
                                  ALU.mult).then_inc(s_dupm, 1)
                dve.wait_ge(s_dupm, i * 2 + (b + 1))
                dve.tensor_tensor(sidx[:, bass.ds(i * (2 * GROUP) + b * GROUP, GROUP)], sidx_f[:, :], scol[:, b, :], ALU.add).then_inc(s_sidx, 1)

            def weigh(i, b, what, sem_in, used):
                dve.wait_ge(sem_in, i * 2 + (b + 1))
                dve.wait_ge(*used(i, b))
                wcol = wT[:, bass.ds(i * (2 * GROUP) + b * GROUP, GROUP)].unsqueeze(2).to_broadcast([P, GROUP, P])
                dve.tensor_tensor(weighted(i, b), what, wcol, ALU.mult).then_inc(s_ohw, 1)

            dve.wait_ge(s_wT, 6)
            flag = flag_of(dve)
            with dve.If(flag < 1):
                one_hot(0, 0)
                one_hot(0, 1)
                for i in range(LAG):
                    add_window(i, 0)
                    one_hot(i + 1, 0)
                    add_window(i, 1)
                    one_hot(i + 1, 1)
                def node_round(i, w, v, more):
                    cell_c(w)
                    cell_h(w)
                    add_window(i, 0)
                    if more:
                        one_hot(i + 1, 0)
                    if v is not None:
                        finish_scale(v)
                        own_part(v)
                    add_window(i, 1)
                    if more:
                        one_hot(i + 1, 1)
                    residual(w)

                node_round(LAG, 0, None, True)
                with dve.Fori(LAG + 1, NPAIR - 2) as i:
                    node_round(i, i - LAG, i - (LAG + 1), True)
                used = lambda i, b: (s_m, i * 2 + b)
                dve.sem_inc(s_m, 1)

                def window_one_hot(i, b):
                    dve.wait_ge(*used(i, b))
                    dve.tensor_tensor(weighted(i, b), iota_row[:, :].unsqueeze(1).to_broadcast([P, GROUP, P]),
                                      loc[:, bass.ds(i * 2 + b, 1), :].rearrange("p a j -> p (a j)").unsqueeze(2).to_broadcast([P, GROUP, P]),
                                      ALU.is_equal).then_inc(s_eq, 1)

                def group_round(i, b, more):
                    if more:
                        sources(*((i, 1) if b == 0 else (i + 1, 0)), i * 2 + b)
                    window_one_hot(i, b)
                    same_source(i, b, used)
                    weigh(i, b, weighted(i, b), s_eq, used)
                    scatter_rows(i, b)

                i, w = NPAIR - 2, EARLY - 1
                sources(0, 0, 0)
                sources(0, 1, 0)
                cell_c(w)
                cell_h(w)
                window_one_hot(0, 0)
                same_source(0, 0, used, 6)
                weigh(0, 0, weighted(0, 0), s_eq, used)
                add_window(i, 0)
                one_hot(i + 1, 0)
                finish_scale(w - 1)
                own_part(w - 1)
                scatter_rows(0, 0)
                add_window(i, 1)
                one_hot(i + 1, 1)
                residual(w)
                i, w = NPAIR - 1, EARLY
                window_one_hot(0, 1)
                same_source(0, 1, used, 6)
                cell_c(w)
                cell_h(w)
                weigh(0, 1, weighted(0, 1), s_eq, used)
                add_window(i, 0)
                window_one_hot(1, 0)
                finish_scale(w - 1)
                residual(w)
                own_part(w - 1)
                add_window(i, 1)
                scatter_rows(0, 1)
                sources(1, 0, 1)
                w = NT - 2
                cell_c(w)
                cell_h(w)
                finish_scale(w - 1)
                same_source(1, 0, used, 6)
                weigh(1, 0, weighted(1, 0), s_eq, used)
                residual(w)
                own_part(w - 1)
                scatter_rows(1, 0)
                sources(1, 1, 2)
                w = NT - 1
                cell_c(w)
                cell_h(w)
                window_one_hot(1, 1)
                finish_scale(w - 1)
                same_source(1, 1, used, 6)
                weigh(1, 1, weighted(1, 1), s_eq, used)
                residual(w)
                own_part(w - 1)
                sources(2, 0, 3)
                scatter_rows(1, 1)
                finish_scale(w)
                window_one_hot(2, 0)
                same_source(2, 0, used, 2)
                weigh(2, 0, weighted(2, 0), s_eq, used)
                own_part(w)
                sources(2, 1, 4)
                scatter_rows(2, 0)
                group_round(2, 1, True)
                with dve.Fori(3, NPAIR - 1) as i:
                    group_round(i, 0, True)
                    group_round(i, 1, True)
                group_round(NPAIR - 1, 0, True)
                group_round(NPAIR - 1, 1, False)
            with dve.Else():
                with dve.Fori(0, NG) as g:
                    with dve.Fori(0, NT) as w:
                        k = g * NT + w
                        dve.wait_ge(g_oh, k)
                        dve.tensor_tensor(wloc[:, :], dstT[:, bass.ds(g * GROUP, GROUP)],
                                          wbase[:, bass.ds(w, 1)].to_broadcast([P, GROUP]), ALU.subtract).then_inc(g_loc, 1)
                        dve.wait_ge(g_loc, k + 1)
                        dve.wait_ge(g_summed, k)
                        dve.tensor_tensor(oh[:, 0, :, :], iota_row[:, :].unsqueeze(1).to_broadcast([P, GROUP, P]),
                                          wloc[:, :].unsqueeze(2).to_broadcast([P, GROUP, P]), ALU.is_equal).then_inc(g_oh, 1)
                        dve.wait_ge(g_summed, k + 1)
                        dve.wait_ge(g_added, k)
                        v = aggT[:, :, bass.ds(w * P, P)]
                        dve.tensor_tensor(v, v, bank[0][:, 0:D].rearrange("p (k n) -> p k n", k=KD), ALU.add).then_inc(g_added, 1)
                with dve.Fori(0, NT) as w:
                    cell_c(w)
                    cell_h(w)
                    residual(w)
                    finish_scale(w)
                    own_part(w)
                used = lambda i, b: (s_comb, i * 4 + (2 * b + 2))
                with dve.Fori(0, NPAIR) as i:
                    for b in range(2):
                        sources(i, b, i * 2 + b)
                        same_source(i, b, used)
                        weigh(i, b, same[:, b], s_same, used)
                        scatter_rows(i, b)
            dve.nop()

            dve.sem_inc(l_tot, 2)

            def total(p, q4, n):
                q = q4 % 2
                dve.wait_ge(f_loaded[q4], (p - q4) * 16 + 16 * ACCS)
                dve.wait_ge(l_tot, p + 2)
                dve.tensor_tensor(f_s01[:, 0:n, :], fa[q4][0][:, 0:n, :], fa[q4][1][:, 0:n, :], ALU.add).then_inc(l_s01, 1)
                dve.wait_ge(l_s01, p + 1)
                dve.wait_ge(l_s23, p + 1)
                dve.wait_ge(l_turned, p)
                dve.tensor_tensor(f_tot[q][:, 0:n, :], f_s01[:, 0:n, :], f_s23[q][:, 0:n, :], ALU.add).then_inc(l_tot, 1)

            def row_stats(p, q, n):
                dve.wait_ge(l_r, p + 1)
                dve.wait_ge(l_aggr, p)
                for u in range(n):
                    last = dve.bn_stats(bst[:, u, :], f_r[q][:, u, :])
                last.then_inc(l_stats, 1)
                dve.wait_ge(l_stats, p + 1)
                dve.wait_ge(l_q, p + 1)
                dve.sem_inc(go_aggr, 1)
                for u in range(n):
                    last = dve.bn_aggr(mv[:, u, :], bst[:, u, :])
                last.then_inc(l_aggr, 1)
                dve.wait_ge(l_aggr, p + 1)
                dve.wait_ge(l_rstd, p)
                dve.sem_inc(go_aggr, 1)
                dve.tensor_scalar(veps[:, 0:n], mv[:, 0:n, 1:2].rearrange("p t a -> p (t a)"), 1e-10, None, ALU.add).then_inc(l_veps, 1)

            def centre(p, q, n):
                dve.wait_ge(l_aggr, p + 1)
                dve.wait_ge(l_out, p)
                for u in range(n):
                    last = dve.scalar_tensor_tensor(out=f_q[q][:, u, :], in0=f_r[q][:, u, :], scalar=mv[:, u, 0:1], in1=scale_b[:, :],
                                                    op0=ALU.subtract, op1=ALU.mult)
                last.then_inc(l_q, 1)

            def add_rows(p, q, n):
                dve.wait_ge(l_rstd, p + 1)
                dve.wait_ge(l_q, p + 2)
                dve.wait_ge(l_stored[q], (p - q) * 8)
                for u in range(n):
                    last = dve.scalar_tensor_tensor(out=f_o[q][:, u, :], in0=f_q[q][:, u, :], scalar=rstd[:, u:u + 1],
                                                    in1=x_tile(p * 2 + u), op0=ALU.mult, op1=ALU.add)
                last.then_inc(l_out, 1)

            def pair_round(p, q4, n, before, after):
                q = q4 % 2
                if after:
                    total(p + 1, (q4 + 1) % AHEAD, after)
                if before:
                    add_rows(p - 1, 1 - q, 2)
                row_stats(p, q, n)
                centre(p, q, n)

            dve.wait_ge(s_off, NT)
            dve.sem_inc(l_out, 1)
            dve.sem_inc(l_q, 1)
            total(0, 0, 2)
            pair_round(0, 0, 2, False, 2)
            with dve.Fori(0, NPT // AHEAD - 1) as i:
                for q4 in range(1, AHEAD + 1):
                    pair_round(i * AHEAD + q4, q4 % AHEAD, 2, True, 2)
            for p in range(NPT - AHEAD, NPT):
                pair_round(p, p % AHEAD, 1 if p == NPT - 1 else 2, True, (2 if p < NPT - 2 else 1) if p < NPT - 1 else 0)
            add_rows(NPT - 1, 0, 1)

        @block.tensor
        def _(pe):
            pe.wait_ge(s_const, 1)
            pe.wait_ge(s_wrel, 32)
            for r in range(2):
                for k in range(KD):
                    for c in range(KD):
                        last = pe.transpose(bank[4 + r][:, k * D + c * P:k * D + (c + 1) * P],
                                            rel_raw[:, r, c, k * P:(k + 1) * P], ident[:, :])
                last.then_inc(s_relps, 1)
            pe.wait_ge(s_bias, 16 * 6)
            pe.transpose(bank[6][:, 0:NB], bias_rows[:, :], ident[0:NB, 0:NB]).then_inc(s_relps, 1)

            def turn(t):
                pe.wait_ge(s_hrow, t + 1)
                pe.wait_ge(s_hT, t)
                for k in range(KD):
                    last = pe.transpose(bank[0][:, k * P:(k + 1) * P], hrow[:, k * P:(k + 1) * P], ident[:, :])
                last.then_inc(s_tr, 1)

            def product1(t, r):
                pe.wait_ge(s_hT, t + 1)
                pe.wait_ge(s_mid, t * 2)
                for o in range(KD):
                    for k in range(KD):
                        last = pe.matmul(bank[2 + r][:, o * P:(o + 1) * P], relT[:, r, k, o * P:(o + 1) * P],
                                         hT[:, k, :], start=(k == 0), stop=(k == KD - 1))
                last.then_inc(s_a, 1)

            def product2(t, r):
                pe.wait_ge(s_mid, t * 2 + (r + 1))
                pe.wait_ge(s_ysum, t * 2)
                for k in range(KD):
                    last = pe.matmul(bank[4 + r][:, 0:D], midT[:, r, k, :], relT[:, r, k, :], start=(k == 0), stop=(k == KD - 1))
                last.then_inc(s_b, 1)

            def edge_columns(n):
                a = e_f[:, n] if n < 3 else e_w
                for c in range(EC):
                    rows = P if c < EC - 1 else RT
                    last = pe.transpose(bank[(6, 7, 1, 6)[n]][:, c * P:c * P + rows], a[0:rows, c, :], ident[0:rows, 0:rows])
                last.then_inc(s_eps_ps, 1)

            def gate_weights(n):
                for c in range(2):
                    for k in range(KD):
                        last = pe.transpose(bank[(6, 7, 6)[n]][:, (2 * c + k) * P:(2 * c + k + 1) * P],
                                            ih_raw[:, 2 * n + c, k * P:(k + 1) * P], ident[:, :])
                last.then_inc(s_wps, 1)

            def layout():
                pe.wait_ge(s_ef, 3)
                for n in range(3):
                    edge_columns(n)
                yield
                pe.wait_ge(s_eT, 1)
                edge_columns(3)
                yield
                pe.wait_ge(s_eT, 2)
                pe.matmul(bank[7][:, 0:NG], row0[:, :], dstT[:, 0:ET:GROUP], start=True, stop=True).then_inc(s_base_ps, 1)
                yield
                pe.wait_ge(s_wts, 16 * N_WTS)
                pe.wait_ge(s_eT, 4)
                for c in range(KD):
                    last = pe.transpose(bank[6][:, c * P:(c + 1) * P], w3_raw[:, c, :], ident[:, :])
                last.then_inc(s_wps, 1)
                for k in range(KD):
                    last = pe.transpose(bank[1][:, k * P:(k + 1) * P], w1_raw[:, k * P:(k + 1) * P], ident[:, :])
                last.then_inc(s_wps, 1)
                yield
                pe.wait_ge(s_wT, 2)
                pe.transpose(bank[1][:, D:D + P], w2_raw[:, :], ident[:, :]).then_inc(s_wps, 1)
                gate_weights(0)
                pe.wait_ge(s_base, 1)
                gate_weights(1)
                yield
                pe.wait_ge(s_wT, 4)
                gate_weights(2)
                yield
                pe.wait_ge(s_viol, 1)
                pe.wait_ge(s_wT, 6)
                pe.matmul(bank[6][0:1, 0:1], chk[:, 3:4], ones[:, 0:1], start=True, stop=True).then_inc(s_viol, 1)
                yield
                yield
                yield

            turn(0)
            pe.wait_ge(s_relT, 3)

            def table_tile(t, last):
                product1(t, 0)
                product1(t, 1)
                if not last:
                    turn(t + 1)
                product2(t, 0)
                product2(t, 1)

            with pe.Fori(0, MID) as t:
                table_tile(t, False)
            slots = layout()
            for n in range(NSLOT):
                next(slots)
                table_tile(MID + n, False)
            with pe.Fori(MID + NSLOT, NT - 1) as t:
                table_tile(t, False)
            table_tile(NT - 1, True)
            pe.wait_ge(s_ysum, 2 * NT)
            pe.wait_ge(s_wT, 6)
            pe.wait_ge(s_brows, 1)
            pe.sem_inc(s_summed, 2)

            def sum_tiles(b, parts, signal):
                for k, j0, j1 in parts:
                    for j in range(j0, j1):
                        last = pe.matmul(bank[b][:, k * P:(k + 1) * P], msgs[:, b, j, k * P:(k + 1) * P], oh[:, b, j, :],
                                         start=(j == 0), stop=(j == GROUP - 1))
                if signal is not None:
                    last.then_inc(signal, 1)

            def sum_half(i, b, h):
                if h == 0:
                    pe.wait_ge(s_oh, i * 2 + (b + 1))
                    pe.wait_ge(s_added, i * 2 + (b + 1))
                pe.wait_ge(s_gathered[b][h], i * (8 * GROUP) + 8 * GROUP)
                if h == 0:
                    sum_tiles(b, ((0, 0, GROUP // 2),), None)
                else:
                    sum_tiles(b, ((0, GROUP // 2, GROUP), (1, 0, GROUP)), s_summed)

            def gates(w):
                pe.wait_ge(s_tg, w)
                for c in range(6):
                    for k in range(KD):
                        last = pe.matmul(bank[2 + c // 4][:, (c % 4) * P:(c % 4 + 1) * P], ihT[:, c, k, :],
                                         aggT[:, k, bass.ds(w * P, P)], start=(k == 0), stop=(k == KD - 1))
                last.then_inc(s_gates, 1)

            def mlp1(w):
                pe.wait_ge(s_hn, w + 1)
                pe.wait_ge(s_x1, w)
                for k in range(KD):
                    last = pe.matmul(bank[3][:, 2 * P:3 * P], w1T[:, k, :], hn[:, k, :], start=(k == 0), stop=(k == KD - 1))
                last.then_inc(s_w1, 1)

            def mlp2(w):
                pe.wait_ge(s_x1, w + 1)
                pe.wait_ge(s_x2, w)
                pe.matmul(bank[3][:, 3 * P:4 * P], w2T[:, :], x1T[:, :], start=True, stop=True).then_inc(s_w2, 1)

            def mlp3(w):
                pe.wait_ge(s_x2, w + 1)
                pe.wait_ge(s_xr, w)
                pe.matmul(bank[4][:, 0:D], ones_bf[:, :], b_rows[:, 0, :], start=True, stop=False)
                pe.matmul(bank[4][:, 0:D], x2T[:, :], w3T[:, :], start=False, stop=True).then_inc(s_w3, 1)

            def turn1(v):
                pe.wait_ge(s_hrow1, v + 1)
                pe.wait_ge(s_grow, v)
                for k in range(KD):
                    last = pe.transpose(bank[5][:, k * P:(k + 1) * P], hrow[:, k * P:(k + 1) * P], ident[:, :])
                last.then_inc(s_tr1, 1)

            def g_product(v):
                pe.wait_ge(s_hT1, v + 1)
                for k in range(KD):
                    last = pe.matmul(bank[5][:, D:2 * D], hT[:, k, :], gw1[:, k, :], start=(k == 0), stop=(k == KD - 1))
                last.then_inc(s_g, 1)

            def node_tile(w, v):
                if w is not None:
                    gates(w)
                    mlp1(w)
                if v is not None:
                    turn1(v)
                    g_product(v)
                if w is not None:
                    mlp2(w)
                    mlp3(w)

            def source_rows(i, b, bk=0):
                pe.wait_ge(s_scol, i * 2 + (b + 1))
                pe.wait_ge(s_same, i * 2 + b)
                for j in range(GROUP):
                    last = pe.transpose(bank[bk + j // 4][:, (j % 4) * P:(j % 4 + 1) * P],
                                        scol[:, b, j:j + 1].to_broadcast([P, P]), ident[:, :])
                last.then_inc(s_srow, 1)

            def half_out(i, b, h, lhs, rhs, bk):
                for j in range(h * GROUP // 2, (h + 1) * GROUP // 2):
                    last = pe.matmul(bank[bk + (j % 4) // 2][:, (j % 2) * D:(j % 2 + 1) * D], lhs(j), rhs(j), start=True, stop=True)
                last.then_inc(s_comb, 1)

            def rows_out(i, b, lhs, rhs):
                for h in range(2):
                    pe.wait_ge(s_combsb, i * 4 + (2 * b + h + 1))
                    half_out(i, b, h, lhs, rhs, 4 + 2 * h)

            flag = flag_of(pe)
            with pe.If(flag < 1):
                for i in range(LAG):
                    for b in range(2):
                        sum_half(i, b, 0)
                        sum_half(i, b, 1)

                def node_round(i, w, v):
                    pe.wait_ge(s_added, i * 2 + 2)
                    gates(w)
                    sum_half(i, 0, 0)
                    sum_half(i, 0, 1)
                    mlp1(w)
                    if v is not None:
                        turn1(v)
                    sum_half(i, 1, 0)
                    if v is not None:
                        g_product(v)
                    mlp2(w)
                    sum_half(i, 1, 1)
                    mlp3(w)

                node_round(LAG, 0, None)
                with pe.Fori(LAG + 1, NPAIR - 2) as i:
                    node_round(i, i - LAG, i - (LAG + 1))

                def weights_of(i, b, bk=2):
                    pe.wait_ge(s_same, i * 2 + (b + 1))
                    pe.wait_ge(s_ohw, i * 2 + (b + 1))
                    pe.wait_ge(s_mcopied, i * 2 + b)
                    for j in range(GROUP):
                        last = pe.matmul(bank[bk + j // 4][:, (j % 4) * P:(j % 4 + 1) * P], weighted(i, b)[:, j, :], same[:, b, j, :],
                                         start=True, stop=True)
                    last.then_inc(s_m, 1)

                def window_half(i, b, h, bk):
                    pe.wait_ge(s_mcopied, i * 2 + (b + 1))
                    pe.wait_ge(s_hwin[b], i * 16 + 16)
                    half_out(i, b, h, lambda j: m_sb[:, b, j, :], lambda j: hwin[:, b, :], bk)

                pe.sem_inc(s_comb, 4)
                i, w = NPAIR - 2, EARLY - 1
                pe.wait_ge(s_added, i * 2 + 2)
                gates(w)
                source_rows(0, 0, 6)
                sum_half(i, 0, 0)
                sum_half(i, 0, 1)
                mlp1(w)
                turn1(w - 1)
                sum_half(i, 1, 0)
                g_product(w - 1)
                mlp2(w)
                weights_of(0, 0, 6)
                sum_half(i, 1, 1)
                mlp3(w)
                i, w = NPAIR - 1, EARLY
                pe.wait_ge(s_added, i * 2 + 2)
                gates(w)
                pe.wait_ge(s_mcopied, 1)
                source_rows(0, 1, 6)
                sum_half(i, 0, 0)
                sum_half(i, 0, 1)
                mlp1(w)
                pe.wait_ge(s_same, 2)
                window_half(0, 0, 0, 6)
                mlp2(w)
                sum_half(i, 1, 0)
                mlp3(w)
                turn1(w - 1)
                g_product(w - 1)
                sum_half(i, 1, 1)
                pe.wait_ge(s_combsb, 2 + 1)
                window_half(0, 0, 1, 6)
                pe.wait_ge(s_combsb, 2 + 2)
                weights_of(0, 1, 6)
                w = NT - 2
                pe.wait_ge(s_added, NG + 2)
                gates(w)
                window_half(0, 1, 0, 6)
                mlp1(w)
                window_half(0, 1, 1, 0)
                mlp2(w)
                pe.wait_ge(s_combsb, 2 + 3)
                source_rows(1, 0, 6)
                mlp3(w)
                turn1(w - 1)
                g_product(w - 1)
                w = NT - 1
                gates(w)
                pe.wait_ge(s_combsb, 2 + 4)
                weights_of(1, 0, 0)
                source_rows(1, 1, 6)
                window_half(1, 0, 0, 0)
                mlp1(w)
                mlp2(w)
                mlp3(w)
                turn1(w - 1)
                g_product(w - 1)
                pe.wait_ge(s_same, 4)
                window_half(1, 0, 1, 6)
                pe.wait_ge(s_combsb, 2 + 5)
                weights_of(1, 1, 0)
                turn1(w)
                source_rows(2, 0, 2)
                pe.wait_ge(s_combsb, 2 + 6)
                window_half(1, 1, 0, 6)
                g_product(w)
                weights_of(2, 0)
                window_half(1, 1, 1, 0)
                pe.wait_ge(s_combsb, 2 + 8)
                source_rows(2, 1)
                pe.wait_ge(s_xr, NT)
                pe.wait_ge(s_grow, NT)

                def window_rows(i, b):
                    pe.wait_ge(s_mcopied, i * 2 + (b + 1))
                    pe.wait_ge(s_hwin[b], i * 16 + 16)
                    rows_out(i, b, lambda j: m_sb[:, b, j, :], lambda j: hwin[:, b, :])

                with pe.Fori(2, NPAIR - 1) as i:
                    window_rows(i, 0)
                    weights_of(i, 1)
                    source_rows(i + 1, 0)
                    window_rows(i, 1)
                    weights_of(i + 1, 0)
                    source_rows(i + 1, 1)
                window_rows(NPAIR - 1, 0)
                weights_of(NPAIR - 1, 1)
                window_rows(NPAIR - 1, 1)
            with pe.Else():
                with pe.Fori(0, NG) as g:
                    pe.wait_ge(g_gathered, g * (16 * GROUP) + 16 * GROUP)
                    pe.sem_inc(go_windows, 1)
                    with pe.Fori(0, NT) as w:
                        pe.wait_ge(g_oh, g * NT + w + 1)
                        pe.wait_ge(g_added, g * NT + w)
                        sum_tiles(0, ((0, 0, GROUP), (1, 0, GROUP)), g_summed)
                pe.wait_ge(g_added, NG * NT)
                with pe.Fori(0, NT) as w:
                    node_tile(w, None)
                    node_tile(None, w)
                pe.sem_inc(s_comb, 4)
                pe.wait_ge(s_grow, NT)
                with pe.Fori(0, NPAIR) as i:
                    for b in range(2):
                        source_rows(i, b)
                        pe.wait_ge(s_ohw, i * 2 + (b + 1))
                        pe.wait_ge(g_gathered2, i * (32 * GROUP) + 16 * GROUP * (b + 1))
                        rows_out(i, b, lambda j: ohw[:, b, j, :], lambda j: msgs[:, 1, j, :])
            pe.nop()

            def turn_sums(p, q, n):
                pe.wait_ge(l_tot, p + 3)
                pe.wait_ge(l_rT, p)
                for k in range(KD):
                    for u in range(n):
                        last = pe.transpose(bank[q][:, (k * n + u) * P:(k * n + u + 1) * P], f_tot[q][:, u, k * P:(k + 1) * P], ident[:, :])
                last.then_inc(l_turned, 1)

            def last_product(p, q, n):
                pe.wait_ge(l_rT, p + 1)
                pe.wait_ge(l_r, p)
                rT = f_rT[q].rearrange("p u d -> p (u d)")
                for u in range(n):
                    pe.matmul(bank[2 + q][:, u * D:(u + 1) * D], ones_bf[:, :], b_rows[:, 1, :], start=True, stop=False)
                    for k in range(KD):
                        last = pe.matmul(bank[2 + q][:, u * D:(u + 1) * D], rT[:, (k * n + u) * P:(k * n + u + 1) * P],
                                         gw2[:, k, :], start=False, stop=(k == KD - 1))
                last.then_inc(l_prod, 1)

            pe.wait_ge(s_combsb, 2 * NG + 2)
            pe.sem_inc(l_prod, 2)
            turn_sums(0, 0, 2)
            with pe.Fori(0, NPT // 2 - 1) as i:
                for q in range(2):
                    last_product(i * 2 + q, q, 2)
                    turn_sums(i * 2 + (q + 1), 1 - q, 2)
            last_product(NPT - 3, 0, 2)
            turn_sums(NPT - 2, 1, 2)
            last_product(NPT - 2, 1, 2)
            turn_sums(NPT - 1, 0, 1)
            last_product(NPT - 1, 0, 1)


N_WTS = 13

_INS = ['x', 'src', 'dst', 'edge_type_2', 'edge_weight', 'L0_gnn_W_rel', 'L0_gnn_b_rel', 'L0_gnn_W_ih', 'L0_gnn_b_ih',
        'L0_gnn_b_hh', 'L0_gnn_W1', 'L0_gnn_b1', 'L0_gnn_W2', 'L0_gnn_b2', 'L0_gnn_W3', 'L0_gnn_b3', 'L1_gnn_W1',
        'L1_gnn_b1', 'L1_gnn_W2', 'L1_gnn_b2', 'L1_gnn_eps', 'L1_gnn_offset', 'L1_gnn_scale']


def kernel(**inputs):
    import numpy as _np
    import concourse.bacc as _bacc
    from concourse import mybir as _mybir
    from concourse.bass_utils import run_bass_kernel_spmd as _run

    nc = _bacc.Bacc("TRN2", target_bir_lowering=False, num_devices=1)
    arrays, args = {}, []
    for name in _INS:
        a = _np.ascontiguousarray(inputs[name])
        arrays[f"in_{name}_dram"] = a
        args.append(nc.dram_tensor(f"in_{name}_dram", a.shape, _mybir.dt.from_np(a.dtype), kind="ExternalInput").ap())
    shape = inputs['x'].shape
    args.append(nc.dram_tensor("out_0_dram", shape, _mybir.dt.float32, kind="ExternalOutput").ap())
    gnn_kernel(nc, *args)
    r = _run(nc, [arrays], core_ids=[0])
    return r.results[0]["out_0_dram"]
```
